# Optimizing a Trainium2 kernel written in Bass

```python
import numpy as np
import jax
import jax.numpy as jnp

def _softmax(x, axis=-1):
    return jax.nn.softmax(x, axis=axis)

def _gelu(x):
    return jax.nn.gelu(x, approximate=True)

def _silu(x):
    return jax.nn.silu(x)

def _sigmoid(x):
    return jax.nn.sigmoid(x)

def _layernorm(x, axis=-1, eps=1e-05):
    m = jnp.mean(x, axis=axis, keepdims=True)
    v = jnp.var(x, axis=axis, keepdims=True)
    return (x - m) / jnp.sqrt(v + eps)

def _scatter_add(tgt, idx, src, axis=0):
    return tgt.at[idx].add(src)

def _segment_sum(src, seg, n):
    return jax.ops.segment_sum(src, seg, n)
kernel_name = 'mk_decoder_postln_d2_seqx_r8_97b760'

def setup_inputs(seed: int=0):
    np.random.seed(seed)
    _w = jnp.asarray

    def _rec_inputs():
        import jax
        import jax.numpy as jnp
        _rk = jax.random.key(seed)
        x = -0.0002928 + 1 * jax.random.normal(jax.random.fold_in(_rk, 1), (32, 128, 128), jnp.float32)
        _lenS = 128 - jax.random.randint(jax.random.fold_in(_rk, 7), (32,), 0, max(1, 128 // 4) + 1, jnp.int32)
        _lenS2 = 128 - jax.random.randint(jax.random.fold_in(_rk, 8), (32,), 0, max(1, 128 // 4) + 1, jnp.int32)
        _ctx_512P = jax.random.normal(jax.random.fold_in(_rk, 11), (32, 16, 64), jnp.float32)
        _ctx_512c = jax.random.dirichlet(jax.random.fold_in(_rk, 511), 0.3 * jnp.ones((16,), jnp.float32), (32, 128))
        _ctx_512t = jnp.einsum('bsk,bkd->bsd', _ctx_512c, _ctx_512P)
        _ctx_512t = _ctx_512t * jax.lax.rsqrt(jnp.mean(jnp.square(_ctx_512t)) + 1e-12) * 0.953939
        ctx_512 = 0.00222621 + 0.99962 * (_ctx_512t + 0.3 * jax.random.normal(jax.random.fold_in(_rk, 611), (32, 128, 64), jnp.float32))
        return (x, ctx_512)
    x, ctx_512 = _rec_inputs()

    def _L0_attn_setup():
        import jax, jax.numpy as jnp
        import numpy as np
        H = 64
        HK = 8
        HD = 64
        DM = 128
        WINDOW = 128
        key = jax.random.key(seed)
        ks = jax.random.split(key, 9)
        B, S = (2, 128)
        s = 0.02
        return {'x': jax.random.normal(ks[0], (B, S, DM), jnp.float32), 'Wq': jax.random.normal(ks[1], (H * HD, DM), jnp.float32) * s, 'bq': jax.random.normal(ks[2], (H * HD,), jnp.float32) * s, 'Wk': jax.random.normal(ks[3], (HK * HD, DM), jnp.float32) * s, 'bk': jax.random.normal(ks[4], (HK * HD,), jnp.float32) * s, 'Wv': jax.random.normal(ks[5], (HK * HD, DM), jnp.float32) * s, 'bv': jax.random.normal(ks[6], (HK * HD,), jnp.float32) * s, 'Wo': jax.random.normal(ks[7], (DM, H * HD), jnp.float32) * s, 'bo': jax.random.normal(ks[8], (DM,), jnp.float32) * s, 'sinks': jnp.ones((H,), jnp.float32)}
    _L0_attn_all = _L0_attn_setup()
    _L0_attn_in = {k: v for k, v in _L0_attn_all.items() if k in ('Wq', 'bq', 'Wk', 'bk', 'Wv', 'bv', 'Wo', 'bo', 'sinks')}
    del _L0_attn_all

    def _L0_xattn_setup():
        import jax, jax.numpy as jnp
        import numpy as np
        H, D, C1, C2, S, M, B, W = (16, 32, 128, 64, 256, 64, 2, 4)

        def _ln(x, g, b):
            m = jnp.mean(x, -1, keepdims=True)
            v = jnp.var(x, -1, keepdims=True)
            return (x - m) * jax.lax.rsqrt(v + 1e-05) * g + b

        def _mha(x, y, wq, wk, wv, li1_w, li1_b, lnx_g, lnx_b, lny_g, lny_b, ln3_g, ln3_b, li2_w, li2_b, li3_w, li3_b, causal):
            xn = _ln(x, lnx_g, lnx_b)
            yn = _ln(y, lny_g, lny_b)
            q = jnp.einsum('bsc,hcd->bhsd', xn, wq)
            k = jnp.einsum('btc,hcd->bhtd', yn, wk)
            v = jnp.einsum('btc,hcd->bhtd', yn, wv)
            a = jax.nn.softmax(jnp.einsum('bhsd,bhtd->bhst', q, k) * D ** (-0.5), axis=-1)
            if causal:
                s, t = (a.shape[-2], a.shape[-1])
                mask = (jnp.arange(t)[None, :] > jnp.arange(s)[:, None]).astype(a.dtype)
                a = a * mask
            o = jnp.einsum('bhst,bhtd->bhsd', a, v)
            o = o.transpose(0, 2, 1, 3).reshape(x.shape[0], x.shape[1], H * D)
            x_out = x + o @ li1_w + li1_b
            h = jax.nn.gelu(_ln(x_out, ln3_g, ln3_b) @ li2_w + li2_b, approximate=False)
            return x_out + h @ li3_w + li3_b
        key = jax.random.key(seed)
        ks = iter(jax.random.split(key, 64))

        def w(shape, scale=0.02):
            return jax.random.normal(next(ks), shape, jnp.float32) * scale
        inp = {'xx': jax.random.normal(next(ks), (B, S, C1), jnp.float32), 'ee': jax.random.normal(next(ks), (B, M, C2), jnp.float32), 'ln1_g': jnp.ones(C1, jnp.float32), 'ln1_b': jnp.zeros(C1, jnp.float32), 'ln2_g': jnp.ones(C1, jnp.float32), 'ln2_b': jnp.zeros(C1, jnp.float32)}
        for pfx, cy in (('a1', C1), ('a2', C2)):
            inp[pfx + '_wq'] = w((H, C1, D))
            inp[pfx + '_wk'] = w((H, cy, D))
            inp[pfx + '_wv'] = w((H, cy, D))
            inp[pfx + '_li1_w'] = w((H * D, C1))
            inp[pfx + '_li1_b'] = jnp.zeros(C1, jnp.float32)
            inp[pfx + '_lnx_g'] = jnp.ones(C1, jnp.float32)
            inp[pfx + '_lnx_b'] = jnp.zeros(C1, jnp.float32)
            inp[pfx + '_lny_g'] = jnp.ones(cy, jnp.float32)
            inp[pfx + '_lny_b'] = jnp.zeros(cy, jnp.float32)
            inp[pfx + '_ln3_g'] = jnp.ones(C1, jnp.float32)
            inp[pfx + '_ln3_b'] = jnp.zeros(C1, jnp.float32)
            inp[pfx + '_li2_w'] = w((C1, C1 * W))
            inp[pfx + '_li2_b'] = jnp.zeros(C1 * W, jnp.float32)
            inp[pfx + '_li3_w'] = w((C1 * W, C1))
            inp[pfx + '_li3_b'] = jnp.zeros(C1, jnp.float32)
        inp['training'] = 0
        return inp
    _L0_xattn_all = _L0_xattn_setup()
    _L0_xattn_in = {k: v for k, v in _L0_xattn_all.items() if k in ('ln1_g', 'ln1_b', 'ln2_g', 'ln2_b', 'a1_wq', 'a1_wk', 'a1_wv', 'a1_li1_w', 'a1_li1_b', 'a1_lnx_g', 'a1_lnx_b', 'a1_lny_g', 'a1_lny_b', 'a1_ln3_g', 'a1_ln3_b', 'a1_li2_w', 'a1_li2_b', 'a1_li3_w', 'a1_li3_b', 'a2_wq', 'a2_wk', 'a2_wv', 'a2_li1_w', 'a2_li1_b', 'a2_lnx_g', 'a2_lnx_b', 'a2_lny_g', 'a2_lny_b', 'a2_ln3_g', 'a2_ln3_b', 'a2_li2_w', 'a2_li2_b', 'a2_li3_w', 'a2_li3_b')}
    del _L0_xattn_all

    def _L0_ffn_setup():
        import jax, jax.numpy as jnp
        import numpy as np
        B, S, H = (4, 256, 128)
        F = 512
        E = 8
        JITTER_EPS = 0.01

        def _sparse_mixer_top2(scores, jitter_eps):
            vals, idx = jax.lax.top_k(scores, 2)
            neg_inf = -jnp.inf
            m1 = vals[:, :1]
            factor1 = jnp.maximum(jnp.abs(scores), m1)
            mask1 = (m1 - scores) / factor1 > 2 * jitter_eps
            p1 = jax.nn.softmax(jnp.where(mask1, neg_inf, scores), axis=-1)
            mult1 = jnp.take_along_axis(p1, idx[:, :1], axis=-1)[:, 0]
            m2 = vals[:, 1:2]
            factor2 = jnp.maximum(jnp.abs(scores), m2)
            mask2 = (m2 - scores) / factor2 > 2 * jitter_eps
            top1_onehot = jnp.arange(scores.shape[-1])[None, :] == idx[:, :1]
            s2 = jnp.where(top1_onehot, neg_inf, scores)
            p2 = jax.nn.softmax(jnp.where(mask2, neg_inf, s2), axis=-1)
            mult2 = jnp.take_along_axis(p2, idx[:, 1:2], axis=-1)[:, 0]
            return (mult1, mult2, idx)
        key = jax.random.key(seed)
        k0, k1, k2, k3, k4 = jax.random.split(key, 5)
        hidden_states = jax.random.normal(k0, (B, S, H), dtype=jnp.float32)
        gate_w = jax.random.normal(k1, (E, H), dtype=jnp.float32) * 0.02
        w1 = jax.random.normal(k2, (E, F, H), dtype=jnp.float32) * 0.02
        w2 = jax.random.normal(k3, (E, H, F), dtype=jnp.float32) * 0.02
        w3 = jax.random.normal(k4, (E, F, H), dtype=jnp.float32) * 0.02
        return {'hidden_states': hidden_states, 'gate_w': gate_w, 'w1': w1, 'w2': w2, 'w3': w3}
    _L0_ffn_all = _L0_ffn_setup()
    _L0_ffn_in = {k: v for k, v in _L0_ffn_all.items() if k in ('gate_w', 'w1', 'w2', 'w3')}
    del _L0_ffn_all

    def _L1_attn_setup():
        import jax, jax.numpy as jnp
        import numpy as np
        EMBED_DIM = 128
        NUM_HEADS = 16
        HEAD_DIM = EMBED_DIM // NUM_HEADS
        MAX_REL = 16
        key = jax.random.key(seed)
        ks = jax.random.split(key, 7)
        T, B, E = (128, 4, EMBED_DIM)
        scale = 1.0 / np.sqrt(E)
        return {'query': jax.random.normal(ks[0], (T, B, E), jnp.float32), 'in_proj_weight': jax.random.normal(ks[1], (3 * E, E), jnp.float32) * scale, 'in_proj_bias': jnp.zeros((3 * E,), jnp.float32), 'rel_k_table': jax.random.uniform(ks[2], (2 * MAX_REL + 1, HEAD_DIM), jnp.float32), 'rel_v_table': jax.random.uniform(ks[3], (2 * MAX_REL + 1, HEAD_DIM), jnp.float32), 'out_w': jax.random.normal(ks[4], (E, E), jnp.float32) * scale, 'out_b': jnp.zeros((E,), jnp.float32)}
    _L1_attn_all = _L1_attn_setup()
    _L1_attn_in = {k: v for k, v in _L1_attn_all.items() if k in ('in_proj_weight', 'in_proj_bias', 'rel_k_table', 'rel_v_table', 'out_w', 'out_b')}
    del _L1_attn_all

    def _L1_xattn_setup():
        import jax, jax.numpy as jnp
        import numpy as np
        HEADS = 16
        D_MODEL = 128
        IMG_MODEL = 64
        D_K = D_MODEL // HEADS
        key = jax.random.key(seed)
        ks = jax.random.split(key, 12)
        B, LQ, LKV = (8, 256, 128)
        s_dm = 1.0 / np.sqrt(D_MODEL)
        s_im = 1.0 / np.sqrt(IMG_MODEL)
        return {'q': jax.random.normal(ks[0], (B, LQ, D_MODEL), jnp.float32), 'k': jax.random.normal(ks[1], (B, LKV, IMG_MODEL), jnp.float32), 'v': jax.random.normal(ks[2], (B, LKV, IMG_MODEL), jnp.float32), 'Wq': jax.random.normal(ks[3], (D_MODEL, D_MODEL), jnp.float32) * s_dm, 'bq': jnp.zeros((D_MODEL,), jnp.float32), 'Wk': jax.random.normal(ks[4], (IMG_MODEL, D_MODEL), jnp.float32) * s_im, 'bk': jnp.zeros((D_MODEL,), jnp.float32), 'Wv': jax.random.normal(ks[5], (IMG_MODEL, D_MODEL), jnp.float32) * s_im, 'bv': jnp.zeros((D_MODEL,), jnp.float32), 'Wo': jax.random.normal(ks[6], (D_MODEL, D_MODEL), jnp.float32) * s_dm, 'bo': jnp.zeros((D_MODEL,), jnp.float32)}
    _L1_xattn_all = _L1_xattn_setup()
    _L1_xattn_in = {k: v for k, v in _L1_xattn_all.items() if k in ('Wq', 'bq', 'Wk', 'bk', 'Wv', 'bv', 'Wo', 'bo')}
    del _L1_xattn_all

    def _L1_ffn_setup():
        import jax, jax.numpy as jnp
        import numpy as np
        B, S, D_MODEL, D_FF = (4, 256, 128, 512)

        def _quantum_transform(hidden, theta, w_real, w_imag):
            imag = w_imag * jnp.sin(theta + hidden * 0.1)
            quantum_phase = jnp.cos(theta) * w_real + jnp.sin(theta) * w_imag
            return hidden + quantum_phase * imag * 0.1
        key = jax.random.key(seed)
        ks = jax.random.split(key, 8)
        return {'x': jax.random.normal(ks[0], (B, S, D_MODEL), dtype=jnp.float32), 'W1': jax.random.normal(ks[1], (D_MODEL, D_FF), dtype=jnp.float32) * (1.0 / np.sqrt(D_MODEL)), 'b1': jnp.zeros((D_FF,), dtype=jnp.float32), 'quantum_phases': jax.random.normal(ks[2], (D_FF,), dtype=jnp.float32) * (2.0 * np.pi), 'quantum_weights_real': jax.random.normal(ks[3], (D_FF,), dtype=jnp.float32) * 0.1, 'quantum_weights_imag': jax.random.normal(ks[4], (D_FF,), dtype=jnp.float32) * 0.1, 'W2': jax.random.normal(ks[5], (D_FF, D_MODEL), dtype=jnp.float32) * (1.0 / np.sqrt(D_FF)), 'b2': jnp.zeros((D_MODEL,), dtype=jnp.float32)}
    _L1_ffn_all = _L1_ffn_setup()
    _L1_ffn_in = {k: v for k, v in _L1_ffn_all.items() if k in ('W1', 'b1', 'quantum_phases', 'quantum_weights_real', 'quantum_weights_imag', 'W2', 'b2')}
    del _L1_ffn_all
    return {'x': x, 'ctx_512': ctx_512, 'L0_attn_Wq': _L0_attn_in['Wq'], 'L0_attn_bq': _L0_attn_in['bq'], 'L0_attn_Wk': _L0_attn_in['Wk'], 'L0_attn_bk': _L0_attn_in['bk'], 'L0_attn_Wv': _L0_attn_in['Wv'], 'L0_attn_bv': _L0_attn_in['bv'], 'L0_attn_Wo': _L0_attn_in['Wo'], 'L0_attn_bo': _L0_attn_in['bo'], 'L0_attn_sinks': _L0_attn_in['sinks'], 'L0_xattn_ln1_g': _L0_xattn_in['ln1_g'], 'L0_xattn_ln1_b': _L0_xattn_in['ln1_b'], 'L0_xattn_ln2_g': _L0_xattn_in['ln2_g'], 'L0_xattn_ln2_b': _L0_xattn_in['ln2_b'], 'L0_xattn_a1_wq': _L0_xattn_in['a1_wq'], 'L0_xattn_a1_wk': _L0_xattn_in['a1_wk'], 'L0_xattn_a1_wv': _L0_xattn_in['a1_wv'], 'L0_xattn_a1_li1_w': _L0_xattn_in['a1_li1_w'], 'L0_xattn_a1_li1_b': _L0_xattn_in['a1_li1_b'], 'L0_xattn_a1_lnx_g': _L0_xattn_in['a1_lnx_g'], 'L0_xattn_a1_lnx_b': _L0_xattn_in['a1_lnx_b'], 'L0_xattn_a1_lny_g': _L0_xattn_in['a1_lny_g'], 'L0_xattn_a1_lny_b': _L0_xattn_in['a1_lny_b'], 'L0_xattn_a1_ln3_g': _L0_xattn_in['a1_ln3_g'], 'L0_xattn_a1_ln3_b': _L0_xattn_in['a1_ln3_b'], 'L0_xattn_a1_li2_w': _L0_xattn_in['a1_li2_w'], 'L0_xattn_a1_li2_b': _L0_xattn_in['a1_li2_b'], 'L0_xattn_a1_li3_w': _L0_xattn_in['a1_li3_w'], 'L0_xattn_a1_li3_b': _L0_xattn_in['a1_li3_b'], 'L0_xattn_a2_wq': _L0_xattn_in['a2_wq'], 'L0_xattn_a2_wk': _L0_xattn_in['a2_wk'], 'L0_xattn_a2_wv': _L0_xattn_in['a2_wv'], 'L0_xattn_a2_li1_w': _L0_xattn_in['a2_li1_w'], 'L0_xattn_a2_li1_b': _L0_xattn_in['a2_li1_b'], 'L0_xattn_a2_lnx_g': _L0_xattn_in['a2_lnx_g'], 'L0_xattn_a2_lnx_b': _L0_xattn_in['a2_lnx_b'], 'L0_xattn_a2_lny_g': _L0_xattn_in['a2_lny_g'], 'L0_xattn_a2_lny_b': _L0_xattn_in['a2_lny_b'], 'L0_xattn_a2_ln3_g': _L0_xattn_in['a2_ln3_g'], 'L0_xattn_a2_ln3_b': _L0_xattn_in['a2_ln3_b'], 'L0_xattn_a2_li2_w': _L0_xattn_in['a2_li2_w'], 'L0_xattn_a2_li2_b': _L0_xattn_in['a2_li2_b'], 'L0_xattn_a2_li3_w': _L0_xattn_in['a2_li3_w'], 'L0_xattn_a2_li3_b': _L0_xattn_in['a2_li3_b'], 'L0_ffn_gate_w': _L0_ffn_in['gate_w'], 'L0_ffn_w1': _L0_ffn_in['w1'], 'L0_ffn_w2': _L0_ffn_in['w2'], 'L0_ffn_w3': _L0_ffn_in['w3'], 'L1_attn_in_proj_weight': _L1_attn_in['in_proj_weight'], 'L1_attn_in_proj_bias': _L1_attn_in['in_proj_bias'], 'L1_attn_rel_k_table': _L1_attn_in['rel_k_table'], 'L1_attn_rel_v_table': _L1_attn_in['rel_v_table'], 'L1_attn_out_w': _L1_attn_in['out_w'], 'L1_attn_out_b': _L1_attn_in['out_b'], 'L1_xattn_Wq': _L1_xattn_in['Wq'], 'L1_xattn_bq': _L1_xattn_in['bq'], 'L1_xattn_Wk': _L1_xattn_in['Wk'], 'L1_xattn_bk': _L1_xattn_in['bk'], 'L1_xattn_Wv': _L1_xattn_in['Wv'], 'L1_xattn_bv': _L1_xattn_in['bv'], 'L1_xattn_Wo': _L1_xattn_in['Wo'], 'L1_xattn_bo': _L1_xattn_in['bo'], 'L1_ffn_W1': _L1_ffn_in['W1'], 'L1_ffn_b1': _L1_ffn_in['b1'], 'L1_ffn_quantum_phases': _L1_ffn_in['quantum_phases'], 'L1_ffn_quantum_weights_real': _L1_ffn_in['quantum_weights_real'], 'L1_ffn_quantum_weights_imag': _L1_ffn_in['quantum_weights_imag'], 'L1_ffn_W2': _L1_ffn_in['W2'], 'L1_ffn_b2': _L1_ffn_in['b2']}

def reference(x, ctx_512, L0_attn_Wq, L0_attn_bq, L0_attn_Wk, L0_attn_bk, L0_attn_Wv, L0_attn_bv, L0_attn_Wo, L0_attn_bo, L0_attn_sinks, L0_xattn_ln1_g, L0_xattn_ln1_b, L0_xattn_ln2_g, L0_xattn_ln2_b, L0_xattn_a1_wq, L0_xattn_a1_wk, L0_xattn_a1_wv, L0_xattn_a1_li1_w, L0_xattn_a1_li1_b, L0_xattn_a1_lnx_g, L0_xattn_a1_lnx_b, L0_xattn_a1_lny_g, L0_xattn_a1_lny_b, L0_xattn_a1_ln3_g, L0_xattn_a1_ln3_b, L0_xattn_a1_li2_w, L0_xattn_a1_li2_b, L0_xattn_a1_li3_w, L0_xattn_a1_li3_b, L0_xattn_a2_wq, L0_xattn_a2_wk, L0_xattn_a2_wv, L0_xattn_a2_li1_w, L0_xattn_a2_li1_b, L0_xattn_a2_lnx_g, L0_xattn_a2_lnx_b, L0_xattn_a2_lny_g, L0_xattn_a2_lny_b, L0_xattn_a2_ln3_g, L0_xattn_a2_ln3_b, L0_xattn_a2_li2_w, L0_xattn_a2_li2_b, L0_xattn_a2_li3_w, L0_xattn_a2_li3_b, L0_ffn_gate_w, L0_ffn_w1, L0_ffn_w2, L0_ffn_w3, L1_attn_in_proj_weight, L1_attn_in_proj_bias, L1_attn_rel_k_table, L1_attn_rel_v_table, L1_attn_out_w, L1_attn_out_b, L1_xattn_Wq, L1_xattn_bq, L1_xattn_Wk, L1_xattn_bk, L1_xattn_Wv, L1_xattn_bv, L1_xattn_Wo, L1_xattn_bo, L1_ffn_W1, L1_ffn_b1, L1_ffn_quantum_phases, L1_ffn_quantum_weights_real, L1_ffn_quantum_weights_imag, L1_ffn_W2, L1_ffn_b2):
    import jax
    import jax.numpy as jnp

    def _L0_attn_ref(x, Wq, bq, Wk, bk, Wv, bv, Wo, bo, sinks):
        import jax, jax.numpy as jnp
        import numpy as np
        H = 64
        HK = 8
        HD = 64
        DM = 128
        WINDOW = 128
        B, S, _ = x.shape
        G = H // HK
        q = (x @ Wq.T + bq).reshape(B, S, H, HD).transpose(0, 2, 1, 3)
        k = (x @ Wk.T + bk).reshape(B, S, HK, HD).transpose(0, 2, 1, 3)
        v = (x @ Wv.T + bv).reshape(B, S, HK, HD).transpose(0, 2, 1, 3)
        k = jnp.repeat(k, G, axis=1)
        v = jnp.repeat(v, G, axis=1)
        scale = 1.0 / np.sqrt(HD).astype(np.float32)
        scores = jnp.einsum('bhqd,bhkd->bhqk', q, k) * scale
        qi = jnp.arange(S)[:, None]
        kj = jnp.arange(S)[None, :]
        allowed = (qi >= kj) & (qi - kj < WINDOW)
        neg = jnp.asarray(-1e+30, scores.dtype)
        scores = jnp.where(allowed[None, None], scores, neg)
        sink = jnp.broadcast_to(sinks[None, :, None, None], (B, H, S, 1))
        logits = jnp.concatenate([scores, sink], axis=-1)
        probs = jax.nn.softmax(logits, axis=-1)[..., :-1]
        o = jnp.einsum('bhqk,bhkd->bhqd', probs, v)
        o = o.transpose(0, 2, 1, 3).reshape(B, S, H * HD)
        return o @ Wo.T + bo

    def _L0_xattn_ref(xx, ee, ln1_g, ln1_b, ln2_g, ln2_b, a1_wq, a1_wk, a1_wv, a1_li1_w, a1_li1_b, a1_lnx_g, a1_lnx_b, a1_lny_g, a1_lny_b, a1_ln3_g, a1_ln3_b, a1_li2_w, a1_li2_b, a1_li3_w, a1_li3_b, a2_wq, a2_wk, a2_wv, a2_li1_w, a2_li1_b, a2_lnx_g, a2_lnx_b, a2_lny_g, a2_lny_b, a2_ln3_g, a2_ln3_b, a2_li2_w, a2_li2_b, a2_li3_w, a2_li3_b, training):
        import jax, jax.numpy as jnp
        import numpy as np
        H, D, C1, C2, S, M, B, W = (16, 32, 128, 64, 256, 64, 2, 4)

        def _ln(x, g, b):
            m = jnp.mean(x, -1, keepdims=True)
            v = jnp.var(x, -1, keepdims=True)
            return (x - m) * jax.lax.rsqrt(v + 1e-05) * g + b

        def _mha(x, y, wq, wk, wv, li1_w, li1_b, lnx_g, lnx_b, lny_g, lny_b, ln3_g, ln3_b, li2_w, li2_b, li3_w, li3_b, causal):
            xn = _ln(x, lnx_g, lnx_b)
            yn = _ln(y, lny_g, lny_b)
            q = jnp.einsum('bsc,hcd->bhsd', xn, wq)
            k = jnp.einsum('btc,hcd->bhtd', yn, wk)
            v = jnp.einsum('btc,hcd->bhtd', yn, wv)
            a = jax.nn.softmax(jnp.einsum('bhsd,bhtd->bhst', q, k) * D ** (-0.5), axis=-1)
            if causal:
                s, t = (a.shape[-2], a.shape[-1])
                mask = (jnp.arange(t)[None, :] > jnp.arange(s)[:, None]).astype(a.dtype)
                a = a * mask
            o = jnp.einsum('bhst,bhtd->bhsd', a, v)
            o = o.transpose(0, 2, 1, 3).reshape(x.shape[0], x.shape[1], H * D)
            x_out = x + o @ li1_w + li1_b
            h = jax.nn.gelu(_ln(x_out, ln3_g, ln3_b) @ li2_w + li2_b, approximate=False)
            return x_out + h @ li3_w + li3_b
        x = _ln(xx, ln1_g, ln1_b)
        x = x + _mha(x, x, a1_wq, a1_wk, a1_wv, a1_li1_w, a1_li1_b, a1_lnx_g, a1_lnx_b, a1_lny_g, a1_lny_b, a1_ln3_g, a1_ln3_b, a1_li2_w, a1_li2_b, a1_li3_w, a1_li3_b, causal=True)
        x = _ln(x, ln2_g, ln2_b)
        return x + _mha(x, ee, a2_wq, a2_wk, a2_wv, a2_li1_w, a2_li1_b, a2_lnx_g, a2_lnx_b, a2_lny_g, a2_lny_b, a2_ln3_g, a2_ln3_b, a2_li2_w, a2_li2_b, a2_li3_w, a2_li3_b, causal=False)

    def _L0_ffn_ref(hidden_states, gate_w, w1, w2, w3):
        import jax, jax.numpy as jnp
        import numpy as np
        B, S, H = (4, 256, 128)
        F = 512
        E = 8
        JITTER_EPS = 0.01

        def _sparse_mixer_top2(scores, jitter_eps):
            vals, idx = jax.lax.top_k(scores, 2)
            neg_inf = -jnp.inf
            m1 = vals[:, :1]
            factor1 = jnp.maximum(jnp.abs(scores), m1)
            mask1 = (m1 - scores) / factor1 > 2 * jitter_eps
            p1 = jax.nn.softmax(jnp.where(mask1, neg_inf, scores), axis=-1)
            mult1 = jnp.take_along_axis(p1, idx[:, :1], axis=-1)[:, 0]
            m2 = vals[:, 1:2]
            factor2 = jnp.maximum(jnp.abs(scores), m2)
            mask2 = (m2 - scores) / factor2 > 2 * jitter_eps
            top1_onehot = jnp.arange(scores.shape[-1])[None, :] == idx[:, :1]
            s2 = jnp.where(top1_onehot, neg_inf, scores)
            p2 = jax.nn.softmax(jnp.where(mask2, neg_inf, s2), axis=-1)
            mult2 = jnp.take_along_axis(p2, idx[:, 1:2], axis=-1)[:, 0]
            return (mult1, mult2, idx)
        Bv, Sv, Hv = hidden_states.shape
        x = hidden_states.reshape(-1, Hv)
        scores = x @ gate_w.T
        mult1, mult2, idx = _sparse_mixer_top2(scores, JITTER_EPS)
        out = jnp.zeros_like(x)
        for e in range(E):
            w_tok = mult1 * (idx[:, 0] == e) + mult2 * (idx[:, 1] == e)
            h = jax.nn.silu(x @ w1[e].T) * (x @ w3[e].T)
            out = out + w_tok[:, None] * (h @ w2[e].T)
        return out.reshape(Bv, Sv, Hv)

    def _L1_attn_ref(query, in_proj_weight, in_proj_bias, rel_k_table, rel_v_table, out_w, out_b):
        import jax, jax.numpy as jnp
        import numpy as np
        EMBED_DIM = 128
        NUM_HEADS = 16
        HEAD_DIM = EMBED_DIM // NUM_HEADS
        MAX_REL = 16
        T, B, E = query.shape
        H, d = (NUM_HEADS, HEAD_DIM)
        scaling = d ** (-0.5)
        qkv = jnp.einsum('tbe,fe->tbf', query, in_proj_weight) + in_proj_bias
        q, k, v = jnp.split(qkv, 3, axis=-1)
        q = q * scaling

        def to_heads(x):
            return x.reshape(T, B * H, d).transpose(1, 0, 2)
        q, k, v = (to_heads(q), to_heads(k), to_heads(v))
        pos = jnp.arange(T)
        dist = pos[None, :] - pos[:, None]
        idx = jnp.clip(dist, -MAX_REL, MAX_REL) + MAX_REL
        rel_k = rel_k_table[idx]
        rel_v = rel_v_table[idx]
        scores = jnp.einsum('nqd,nkd->nqk', q, k) + jnp.einsum('nqd,qkd->nqk', q, rel_k)
        probs = jax.nn.softmax(scores, axis=-1)
        attn = jnp.einsum('nqk,nkd->nqd', probs, v) + jnp.einsum('nqk,qkd->nqd', probs, rel_v)
        attn = attn.transpose(1, 0, 2).reshape(T, B, E)
        out = jnp.einsum('tbe,fe->tbf', attn, out_w) + out_b
        return out

    def _L1_xattn_ref(q, k, v, Wq, bq, Wk, bk, Wv, bv, Wo, bo):
        import jax, jax.numpy as jnp
        import numpy as np
        HEADS = 16
        D_MODEL = 128
        IMG_MODEL = 64
        D_K = D_MODEL // HEADS
        B, LQ, _ = q.shape
        LKV = k.shape[1]
        qh = (q @ Wq + bq).reshape(B, LQ, HEADS, D_K).transpose(0, 2, 1, 3)
        kh = (k @ Wk + bk).reshape(B, LKV, HEADS, D_K).transpose(0, 2, 1, 3)
        vh = (v @ Wv + bv).reshape(B, LKV, HEADS, D_K).transpose(0, 2, 1, 3)
        scale = 1.0 / np.sqrt(D_K)
        scores = jnp.einsum('bhqd,bhkd->bhqk', qh, kh) * scale
        attn = jax.nn.softmax(scores, axis=-1)
        out = jnp.einsum('bhqk,bhkd->bhqd', attn, vh)
        concat = out.transpose(0, 2, 1, 3).reshape(B, LQ, D_MODEL)
        return concat @ Wo + bo

    def _L1_ffn_ref(x, W1, b1, quantum_phases, quantum_weights_real, quantum_weights_imag, W2, b2):
        import jax, jax.numpy as jnp
        import numpy as np
        B, S, D_MODEL, D_FF = (4, 256, 128, 512)

        def _quantum_transform(hidden, theta, w_real, w_imag):
            imag = w_imag * jnp.sin(theta + hidden * 0.1)
            quantum_phase = jnp.cos(theta) * w_real + jnp.sin(theta) * w_imag
            return hidden + quantum_phase * imag * 0.1
        hidden = jnp.einsum('bsd,df->bsf', x, W1) + b1
        q = _quantum_transform(hidden, quantum_phases, quantum_weights_real, quantum_weights_imag)
        act = jax.nn.relu(q)
        return jnp.einsum('bsf,fd->bsd', act, W2) + b2
    x = _layernorm(x + _L0_attn_ref(x, L0_attn_Wq, L0_attn_bq, L0_attn_Wk, L0_attn_bk, L0_attn_Wv, L0_attn_bv, L0_attn_Wo, L0_attn_bo, L0_attn_sinks), axis=-1)
    x = _layernorm(x + _L0_xattn_ref(x, ctx_512, L0_xattn_ln1_g, L0_xattn_ln1_b, L0_xattn_ln2_g, L0_xattn_ln2_b, L0_xattn_a1_wq, L0_xattn_a1_wk, L0_xattn_a1_wv, L0_xattn_a1_li1_w, L0_xattn_a1_li1_b, L0_xattn_a1_lnx_g, L0_xattn_a1_lnx_b, L0_xattn_a1_lny_g, L0_xattn_a1_lny_b, L0_xattn_a1_ln3_g, L0_xattn_a1_ln3_b, L0_xattn_a1_li2_w, L0_xattn_a1_li2_b, L0_xattn_a1_li3_w, L0_xattn_a1_li3_b, L0_xattn_a2_wq, L0_xattn_a2_wk, L0_xattn_a2_wv, L0_xattn_a2_li1_w, L0_xattn_a2_li1_b, L0_xattn_a2_lnx_g, L0_xattn_a2_lnx_b, L0_xattn_a2_lny_g, L0_xattn_a2_lny_b, L0_xattn_a2_ln3_g, L0_xattn_a2_ln3_b, L0_xattn_a2_li2_w, L0_xattn_a2_li2_b, L0_xattn_a2_li3_w, L0_xattn_a2_li3_b, 0), axis=-1)
    x = _layernorm(x + _L0_ffn_ref(x, L0_ffn_gate_w, L0_ffn_w1, L0_ffn_w2, L0_ffn_w3), axis=-1)
    x = _layernorm(x + _L1_attn_ref(x, L1_attn_in_proj_weight, L1_attn_in_proj_bias, L1_attn_rel_k_table, L1_attn_rel_v_table, L1_attn_out_w, L1_attn_out_b), axis=-1)
    x = _layernorm(x + _L1_xattn_ref(x, ctx_512, ctx_512, L1_xattn_Wq, L1_xattn_bq, L1_xattn_Wk, L1_xattn_bk, L1_xattn_Wv, L1_xattn_bv, L1_xattn_Wo, L1_xattn_bo), axis=-1)
    x = _layernorm(x + _L1_ffn_ref(x, L1_ffn_W1, L1_ffn_b1, L1_ffn_quantum_phases, L1_ffn_quantum_weights_real, L1_ffn_quantum_weights_imag, L1_ffn_W2, L1_ffn_b2), axis=-1)
    return x

_drawn_inputs = setup_inputs


def setup_inputs(seed=0):
    import zlib

    import numpy as np

    out = dict(_drawn_inputs(seed))
    spreads = {'L0_attn_sinks': (1.0, 0.6),
     'L0_xattn_ln1_g': (1.0, 0.2),
     'L0_xattn_ln1_b': (0.0, 0.1),
     'L0_xattn_ln2_g': (1.0, 0.2),
     'L0_xattn_ln2_b': (0.0, 0.1),
     'L0_xattn_a1_li1_b': (0.0, 0.1),
     'L0_xattn_a1_lnx_g': (1.0, 0.6),
     'L0_xattn_a1_lnx_b': (0.0, 0.8),
     'L0_xattn_a1_lny_g': (1.0, 0.6),
     'L0_xattn_a1_lny_b': (0.0, 0.8),
     'L0_xattn_a1_ln3_g': (1.0, 0.6),
     'L0_xattn_a1_ln3_b': (0.0, 0.8),
     'L0_xattn_a1_li2_b': (0.0, 0.8),
     'L0_xattn_a1_li3_b': (0.0, 0.1),
     'L0_xattn_a2_li1_b': (0.0, 0.1),
     'L0_xattn_a2_lnx_g': (1.0, 0.6),
     'L0_xattn_a2_lnx_b': (0.0, 0.8),
     'L0_xattn_a2_lny_g': (1.0, 0.6),
     'L0_xattn_a2_lny_b': (0.0, 0.8),
     'L0_xattn_a2_ln3_g': (1.0, 0.6),
     'L0_xattn_a2_ln3_b': (0.0, 0.8),
     'L0_xattn_a2_li2_b': (0.0, 0.78),
     'L0_xattn_a2_li3_b': (0.0, 0.1),
     'L1_attn_in_proj_bias': (0.0, 0.1),
     'L1_attn_out_b': (0.0, 0.1),
     'L1_xattn_bq': (0.0, 0.376),
     'L1_xattn_bk': (0.0, 2.0),
     'L1_xattn_bv': (0.0, 0.1),
     'L1_xattn_bo': (0.0, 0.1),
     'L1_ffn_b1': (0.0, 0.1),
     'L1_ffn_b2': (0.0, 0.1)}
    factors = {'L0_attn_Wq': 8.0,
     'L0_attn_bq': 8.0,
     'L0_attn_Wk': 8.0,
     'L0_attn_bk': 8.0,
     'L0_xattn_a1_wq': 8.0,
     'L0_xattn_a1_wk': 8.0,
     'L0_xattn_a1_wv': 8.0,
     'L0_xattn_a1_li1_w': 8.0,
     'L0_xattn_a1_li2_w': 3.707,
     'L0_xattn_a1_li3_w': 3.142,
     'L0_xattn_a2_wq': 8.0,
     'L0_xattn_a2_wk': 8.0,
     'L0_xattn_a2_wv': 4.698,
     'L0_xattn_a2_li1_w': 4.603,
     'L0_xattn_a2_li2_w': 3.472,
     'L0_xattn_a2_li3_w': 2.906,
     'L0_ffn_gate_w': 4.57,
     'L0_ffn_w1': 3.985,
     'L0_ffn_w2': 3.973,
     'L0_ffn_w3': 3.984,
     'L1_ffn_quantum_phases': 8.0,
     'L1_ffn_quantum_weights_real': 33.45,
     'L1_ffn_quantum_weights_imag': 8.0}
    for name, (base, spread) in spreads.items():
        noise = np.random.default_rng([zlib.crc32(name.encode()), seed]).standard_normal(out[name].shape)
        drawn = base * np.exp(spread * noise) if base else spread * noise
        out[name] = jnp.asarray(drawn.astype(out[name].dtype))
    for name, factor in factors.items():
        out[name] = (out[name] * factor).astype(out[name].dtype)
    return out
```

```python
from contextlib import ExitStack

import concourse.bass as bass
from concourse import mybir
from concourse.alu_op_type import AluOpType as ALU

ACT = mybir.ActivationFunctionType
X_AXIS = mybir.AxisListType.X
F32 = mybir.dt.float32
BF16 = mybir.dt.bfloat16

NB = 32
S = 128
DM = 128
DC = 64
EPS = 1e-5
BANK = 512
WEIGHTS = 7720
NEG = -1e30


def need(eng, sem, value):
    if isinstance(value, int) and value <= 0:
        return
    eng.wait_ge(sem, value)


def count(b, per, add):
    return b * per + add


def back(b, n, per):
    return (b, n) if n >= 0 else (b - 1, n + per)


def early(b):
    return isinstance(b, int) and b < 2


def late(b):
    return isinstance(b, int) and b + 2 >= NB


def over_pairs(eng, body, drain=None):
    for b in (0, 1):
        body(b, b, b == 0, False)
    with eng.Fori(1, NB // 2 - 1) as i:
        for par in (0, 1):
            body(i * 2 + par, par, False, False)
    for b in (NB - 2, NB - 1):
        body(b, b % 2, False, b == NB - 1)


def cols(tile, b, width):
    if isinstance(b, int):
        return tile[:, b * width:(b + 1) * width]
    return tile[:, bass.ds(b * width, width)]


def spread(row, parts=128):
    n = row.shape[0]
    return row.rearrange("(a n) -> a n", a=1).broadcast_to([parts, n])


class Norm:

    def __init__(self, g, name, per, ctx):
        nc = g.nc
        self.g, self.per = g, per
        self.stats = ctx.enter_context(nc.sbuf_tensor(name + "_stats", [128, per, 6], F32))
        self.mv = ctx.enter_context(nc.sbuf_tensor(name + "_mean_var", [128, per, 2], F32))
        self.var_eps = ctx.enter_context(nc.sbuf_tensor(name + "_var_eps", [128, per, 1], F32))
        self.rstd = ctx.enter_context(nc.sbuf_tensor(name + "_rstd", [128, per, 1], F32))
        self.stats_done = g.sem(name + "_stats_done")
        self.moments = g.sem(name + "_moments_ready")
        self.eps_added = g.sem(name + "_eps_added")
        self.rstd_ready = g.sem(name + "_rstd_ready")

    def dve_moments(self, dve, b, n, src):
        done = count(b, self.per, n + 1)
        dve.bn_stats(self.stats[:, n, :], src).then_inc(self.stats_done, 1)
        self.g.wait_apart(dve, self.stats_done, done)
        dve.bn_aggr(self.mv[:, n, :], self.stats[:, n, :]).then_inc(self.moments, 1)

    def pool_rstd(self, pool, b, n):
        done = count(b, self.per, n + 1)
        pool.wait_ge(self.moments, done)
        pool.tensor_tensor(self.var_eps[:, n, :], self.mv[:, n, 1:2], self.g.eps[:, :], ALU.add).then_inc(self.eps_added, 1)
        pool.wait_ge(self.eps_added, done)
        pool.tensor_tensor(self.rstd[:, n, :], self.var_eps[:, n, :], self.g.minus_half[:, :], ALU.pow).then_inc(self.rstd_ready, 1)

    def dve_scale(self, dve, b, n, out, src):
        dve.wait_ge(self.rstd_ready, count(b, self.per, n + 1))
        return dve.tensor_scalar(out, src, self.mv[:, n, 0:1], self.rstd[:, n, 0:1], ALU.subtract, ALU.mult)


class Globals:

    def __init__(self, nc, t, ctx):
        self.nc, self.t, self.ctx, self.phase = nc, t, ctx, None
        sb = self.sb
        self.ident = sb("ident", [128, 128], F32)
        self.ident_bf = sb("ident_bf", [128, 128], BF16)
        self.eps = sb("eps", [128, 1], F32)
        self.minus_half = sb("minus_half", [128, 1], F32)
        self.x1 = sb("x1", [128, NB * DM], F32)
        self.xc = sb("xc", [128, NB * DM], F32)
        self.xo = sb("xo", [128, NB * DM], F32)
        self.nx = sb("nx", [128, NB * DM], F32)
        self.context = sb("context", [128, NB * DC], F32)
        self.context_n = sb("context_n", [128, NB * DC], F32)
        self.weights_area = sb("weights", [128, WEIGHTS], F32)
        self.setup_done = self.sem("setup_done")
        self.waits_passed = {nc.vector.engine: self.sem("dve_waits_passed"), nc.gpsimd.engine: self.sem("pool_waits_passed")}

    def wait_apart(self, eng, sem, value):
        need(eng, sem, value)
        eng.sem_inc(self.waits_passed[eng.engine], 1)

    def sb(self, name, shape, dt=F32, ctx=None):
        return (ctx or self.ctx).enter_context(self.nc.sbuf_tensor(name, shape, dt))

    def sem(self, name):
        sem = (self.phase or self.ctx).enter_context(self.nc.semaphore(name))
        if self.phase:
            self.phase_sems.append(sem)
        return sem

    def run_phase(self, phase):
        with ExitStack() as self.phase:
            self.phase_sems = []
            phase(self)
            numbers = sorted(sem.num for sem in self.phase_sems)
            with self.nc.Block() as block:
                @block.gpsimd
                def _(pool):
                    first = 0
                    for i, number in enumerate(numbers):
                        if i + 1 == len(numbers) or numbers[i + 1] != number + 1:
                            pool.sem_clear(range(numbers[first], number + 1))
                            first = i + 1
        self.phase = None

    def banks(self, names, ctx):
        return [ctx.enter_context(self.nc.psum_tensor(n, [128, BANK], F32)) for n in names]


class Area:

    def __init__(self, tile):
        self.whole, self.used = tile, 0

    def take(self, width):
        first, self.used = self.used, self.used + width
        assert self.used <= self.whole.shape[1]
        return self.whole[:, first:self.used]


class Weights:

    def __init__(self, g, name, area):
        self.g, self.name, self.loads, self.tiles, self.area = g, name, [], {}, area
        self.loaded = g.sem(name + "weights_loaded")

    def tile(self, key, shape, src, where=None):
        tile = self.area.take(shape[1])
        self.tiles[key] = tile
        self.loads.append((tile if where is None else where(tile), src))
        return tile

    def __getitem__(self, key):
        return self.tiles[key]

    @property
    def total(self):
        return 16 * len(self.loads)

    def issue(self, eng):
        for dst, src in self.loads:
            eng.dma_start(dst, src).then_inc(self.loaded, 16)


def declare_weights(g):
    t = g.t
    g.weights = {}
    area = Area(g.weights_area)
    col = lambda v: v.rearrange("(p a) -> p a", a=1)
    chunks = lambda tile: tile[:, :].rearrange("p (c n) -> p c n", n=DM)
    rows = lambda m: m.rearrange("(c p) n -> p c n", p=128)
    for name, src, dy in (("b_", "L0_xattn_a1_", DM), ("d_", "L0_xattn_a2_", DC)):
        w = g.weights[name] = Weights(g, name, area)
        w.tile("wq", [128, 512], t[src + "wq"], lambda x: x[:, :])
        w.tile("wk", [128, 512], t[src + "wk"], lambda x: x[0:dy, :])
        w.tile("wv", [128, 512], t[src + "wv"], lambda x: x[0:dy, :])
        w.tile("wo", [128, 4 * DM], rows(t[src + "li1_w"]), chunks)
        w.tile("bo", [128, DM], spread(t[src + "li1_b"]), lambda x: x[:, :])
        w.tile("gx", [128, 1], col(t[src + "lnx_g"]), lambda x: x[:, :])
        w.tile("bx", [128, 1], col(t[src + "lnx_b"]), lambda x: x[:, :])
        w.tile("gy", [128, 1], col(t[src + "lny_g"]), lambda x: x[0:dy, :])
        w.tile("by", [128, 1], col(t[src + "lny_b"]), lambda x: x[0:dy, :])
    for name, src in (("c_", "L0_xattn_a1_"), ("e_", "L0_xattn_a2_")):
        w = g.weights[name] = Weights(g, name, area)
        w.tile("w1", [128, 512], t[src + "li2_w"], lambda x: x[:, :])
        w.tile("w2", [128, 4 * DM], rows(t[src + "li3_w"]), chunks)
        w.tile("b1", [128, 4], t[src + "li2_bT"], lambda x: x[:, :])
        w.tile("b2", [128, DM], spread(t[src + "li3_b"]), lambda x: x[:, :])
        w.tile("gx", [128, 1], col(t[src + "ln3_g"]), lambda x: x[:, :])
        w.tile("bx", [128, 1], col(t[src + "ln3_b"]), lambda x: x[:, :])
        if name == "c_":
            w.tile("ln_g", [128, DM], spread(t["L0_xattn_ln2_g"]), lambda x: x[:, :])
            w.tile("ln_b", [128, DM], spread(t["L0_xattn_ln2_b"]), lambda x: x[:, :])


def declare_later_weights(g):
    t = g.t
    area = Area(g.weights_area)
    chunks = lambda tile: tile[:, :].rearrange("p (c n) -> p c n", n=DM)
    rows = lambda m: m.rearrange("(c p) n -> p c n", p=128)
    w = g.weights["i_"] = Weights(g, "i_", area)
    w.tile("w1", [128, 512], t["L1_ffn_W1"], lambda x: x[:, :])
    w.tile("w2", [128, 4 * DM], rows(t["L1_ffn_W2"]), chunks)
    w.tile("b1", [128, 4], t["L1_ffn_b1T"], lambda x: x[:, :])
    w.tile("b2", [128, DM], spread(t["L1_ffn_b2"]), lambda x: x[:, :])
    w.tile("theta", [128, 4], t["L1_ffn_quantum_phasesT"], lambda x: x[:, :])
    w.tile("wr", [128, 4], t["L1_ffn_quantum_weights_realT"], lambda x: x[:, :])
    w.tile("wi", [128, 4], t["L1_ffn_quantum_weights_imagT"], lambda x: x[:, :])
    w = g.weights["g_"] = Weights(g, "g_", area)
    for name, shape in (("wq", [128, 128]), ("wq_rep", [128, 512]), ("wk_rep", [128, 512]), ("wv", [128, 128]), ("wo", [128, 128]), ("keys", [128, 16 * 63]),
                        ("values", [128, 32 * 32]), ("bq", [128, 1]), ("bv", [128, 1]), ("bq_rep", [128, 4]), ("bk_rep", [128, 4]),
                        ("own_scaled", [128, 128]), ("own", [128, 128]), ("row_head", [128, 4]), ("row_position", [128, 4])):
        w.tile(name, shape, t["L1_attn_" + name], lambda x: x[:, :])
    w.tile("bo", [128, DM], spread(t["L1_attn_out_b"]), lambda x: x[:, :])
    w = g.weights["h_"] = Weights(g, "h_", area)
    w.tile("wq", [128, 512], t["L1_xattn_WqP"], lambda x: x[:, :])
    w.tile("wk", [128, 512], t["L1_xattn_WkP"], lambda x: x[0:DC, :])
    w.tile("wv", [128, 512], t["L1_xattn_WvP"], lambda x: x[0:DC, :])
    w.tile("wo", [128, 4 * DM], rows(t["L1_xattn_WoP"]), chunks)
    w.tile("bo", [128, DM], spread(t["L1_xattn_bo"]), lambda x: x[:, :])
    w.tile("bv", [128, 512], spread(t["L1_xattn_bvP"]), lambda x: x[:, :])
    w.tile("bq", [128, 4], t["L1_xattn_bqP"], lambda x: x[:, :])
    w.tile("bk", [128, 4], t["L1_xattn_bkP"], lambda x: x[:, :])


def setup(g):
    nc = g.nc
    steps = g.sem("setup_steps")
    ctx_loaded = g.sem("context_loaded")
    with nc.Block() as block:
        @block.sync
        def _(sp):
            sp.dma_start(g.context[:, :].rearrange("s (b c) -> s b c", b=NB), g.t["ctx_512"].rearrange("b s c -> s b c")).then_inc(ctx_loaded, 16)
            sp.wait_ge(ctx_loaded, 16)

        @block.gpsimd
        def _(pool):
            pool.memset(g.eps[:, :], EPS).then_inc(steps, 1)
            pool.memset(g.minus_half[:, :], -0.5).then_inc(steps, 1)
            pool.memset(g.ident[:, :], 0.0).then_inc(steps, 1)
            pool.memset(g.ident_bf[:, :], 0.0).then_inc(steps, 1)
            pool.wait_ge(steps, 4)
            for m in (g.ident, g.ident_bf):
                pool.affine_select(out=m[:, :], in_=m[:, :], compare_op=ALU.not_equal, fill=1.0, base=0,
                                   pattern=[[-1, 128]], channel_multiplier=1).then_inc(steps, 1)
            pool.wait_ge(steps, 6)
            pool.sem_inc(g.setup_done, 1)


def self_attention(g):
    nc, t = g.nc, g.t
    H, HK, HD, G4 = 64, 8, 64, 4
    NG = H // G4
    NP = NG // 2
    XL, XW = 2, NB // 2
    NCH = H * HD // 128
    SCALE = HD ** -0.5
    with ExitStack() as ctx:
        sb = lambda name, shape, dt=F32: g.sb("a_" + name, shape, dt, ctx)
        wq = sb("wq", [128, H * HD])
        wk2 = sb("wk2", [128, HK * 128])
        wv = sb("wv", [128, HK * HD])
        wo = sb("wo", [128, NCH * DM])
        bq = sb("bq", [128, NCH])
        bk2 = sb("bk2", [128, HK])
        bv = sb("bv", [128, HK * HD])
        bo = sb("bo", [128, DM])
        ln_g, ln_b = sb("ln_g", [128, DM]), sb("ln_b", [128, DM])
        sinks, neg_sinks = sb("sinks", [128, H]), sb("neg_sinks", [128, H])
        mask = sb("mask", [128, G4 * S], BF16)
        x_in = sb("x_in", [128, 2, DM])
        xT = sb("xT", [128, 2, S])
        kT = sb("kT", [128, 2, HK * S])
        v = sb("v", [128, 2, HK * HD])
        qT = sb("qT", [128, 2, 4 * S])
        ex, probs = sb("ex", [128, 2, G4 * S]), sb("probs", [128, 2, G4 * S])
        probsT = sb("probsT", [128, 4, G4 * S])
        oT = sb("oT", [128, 2, 4 * S])
        max_neg, shift = sb("max_neg", [128, 2, G4]), sb("shift", [128, 2, G4])
        sums, sink_arg, sink_exp = sb("sums", [128, 2, G4]), sb("sink_arg", [128, 2, G4]), sb("sink_exp", [128, 2, G4])
        denom, rden = sb("denom", [128, 2, G4]), sb("rden", [128, 2, G4])
        res, res2 = sb("res", [128, DM]), sb("res2", [128, DM])
        n1, n1g = sb("n1", [128, DM]), sb("n1g", [128, DM])
        s_even, s_odd, pt0, pt1, po0, po1, p_y, p_q = g.banks(
            ["a_s_even", "a_s_odd", "a_pt0", "a_pt1", "a_po0", "a_po1", "a_py", "a_pq"], ctx)
        p_s, p_t, p_o = [s_even, s_odd], [pt0, pt1], [po0, po1]
        norm = Norm(g, "a_ln", 4, ctx)

        sem = lambda n: g.sem("a_" + n)
        weights, w_wo = sem("weights_loaded"), sem("wo_loaded")
        x_loaded = [sem(f"x_loaded{k}") for k in range(XL)]
        x_ready, mask_zero, mask_ready, neg_sinks_ready = sem("x_ready"), sem("mask_zero"), sem("mask_ready"), sem("neg_sinks_ready")
        xT_done, xT_ready = sem("xT_done"), sem("xT_ready")
        kv_done, kv_ready = sem("kv_done"), sem("kv_ready")
        q_done, q_ready = sem("q_done"), sem("q_ready")
        scores_done, max_ready, shift_ready, ex_ready = sem("scores_done"), sem("max_ready"), sem("shift_ready"), sem("ex_ready")
        arg_ready, sinkexp_ready, denom_ready, rden_ready = sem("arg_ready"), sem("sinkexp_ready"), sem("denom_ready"), sem("rden_ready")
        probsT_done, probsT_ready = sem("probsT_done"), sem("probsT_ready")
        probs_ready = sem("probs_ready")
        oT_done, oT_ready = sem("oT_done"), sem("oT_ready")
        y_done, res_ready, res2_ready = sem("y_done"), sem("res_ready"), sem("res2_ready")
        x1_ready, n1_ready, n1g_ready, xc_ready, nx_ready, context_ready = sem("x1_ready"), sem("n1_ready"), sem("n1g_ready"), sem("xc_ready"), sem("nx_ready"), sem("context_ready")
        E0 = 4

        def head(gr, j):
            return gr // 2 * 8 + 2 * j + gr % 2

        def heads(gr):
            return slice(head(gr, 0), head(gr, 3) + 1, 2)

        with nc.Block() as block:
            @block.sync
            def _(sp):
                for k in range(XL):
                    sp.dma_start(g.x1[:, k * XW * DM:(k + 1) * XW * DM].rearrange("s (b n) -> s b n", b=XW),
                                 t["x"][k * XW:(k + 1) * XW].rearrange("b s n -> s b n")).then_inc(x_loaded[k], 16)
                sp.dma_start(wk2[:, :], t["L0_attn_Wk2T"]).then_inc(weights, 16)
                sp.dma_start(bk2[:, :], t["L0_attn_bk2"]).then_inc(weights, 16)
                sp.dma_start(wv[:, :], t["L0_attn_WvT"]).then_inc(weights, 16)
                sp.dma_start(bv[:, :], spread(t["L0_attn_bv"])).then_inc(weights, 16)
                sp.dma_start(bq[:, :], t["L0_attn_bqT"]).then_inc(weights, 16)
                sp.dma_start(sinks[:, :], spread(t["L0_attn_sinks"])).then_inc(weights, 16)
                sp.dma_start(wq[:, :], t["L0_attn_WqT"]).then_inc(weights, 16)
                sp.dma_start(wo[:, :].rearrange("p (c n) -> p c n", n=DM), t["L0_attn_WoT"].rearrange("(c p) n -> p c n", p=128)).then_inc(w_wo, 16)
                sp.dma_start(bo[:, :], spread(t["L0_attn_bo"])).then_inc(w_wo, 16)
                sp.dma_start(ln_g[:, :], spread(t["L0_xattn_ln1_g"])).then_inc(w_wo, 16)
                sp.dma_start(ln_b[:, :], spread(t["L0_xattn_ln1_b"])).then_inc(w_wo, 16)
                for w in g.weights.values():
                    w.issue(sp)

            @block.gpsimd
            def _(pool):
                pool.memset(mask[:, :], 0.0).then_inc(mask_zero, 1)
                pool.wait_ge(mask_zero, 1)
                m = mask[:, :].rearrange("p (a k) -> p a k", a=G4)
                pool.affine_select(out=m, in_=m, compare_op=ALU.is_ge, fill=NEG, base=0,
                                   pattern=[[0, G4], [-1, S]], channel_multiplier=1).then_inc(mask_ready, 1)

                def copy_x(b, par):
                    pool.tensor_copy(x_in[:, par, :], cols(g.x1, b, DM)).then_inc(x_ready, 1)

                for k in range(XL):
                    pool.wait_ge(x_loaded[k], 16)
                copy_x(0, 0)
                pool.wait_ge(weights, 7 * 16)
                pool.wait_ge(w_wo, 4 * 16)

                def finish(b, gr):
                    if gr == E0:
                        pool.wait_ge(res_ready, b + 1)
                        need(pool, x1_ready, b)
                        pool.tensor_tensor(res2[:, :], res[:, :], bo[:, :], ALU.add).then_inc(res2_ready, 1)
                    if gr == E0 + 1:
                        norm.pool_rstd(pool, b, 0)
                    if gr == E0 + 2:
                        norm.pool_rstd(pool, b, 1)
                    if gr == E0 + 4:
                        norm.pool_rstd(pool, b, 2)
                    if gr == E0 + 6:
                        pool.wait_ge(n1_ready, b + 1)
                        need(pool, xc_ready, b)
                        pool.tensor_tensor(n1g[:, :], n1[:, :], ln_g[:, :], ALU.mult).then_inc(n1g_ready, 1)
                        g.wait_apart(pool, n1g_ready, b + 1)
                        pool.tensor_tensor(cols(g.xc, b, DM), n1g[:, :], ln_b[:, :], ALU.add).then_inc(xc_ready, 1)
                    if gr == E0 + 8:
                        norm.pool_rstd(pool, b, 3)

                def argue(b, gr):
                    n = count(b, NG, gr)
                    par = gr % 2
                    pool.wait_ge(shift_ready, n + 1)
                    need(pool, sinkexp_ready, n - 1)
                    pool.tensor_tensor(sink_arg[:, par, :], sinks[:, heads(gr)], shift[:, par, :], ALU.add).then_inc(arg_ready, 1)

                def total(b, gr):
                    n = count(b, NG, gr)
                    par = gr % 2
                    pool.wait_ge(sinkexp_ready, n + 1)
                    pool.wait_ge(ex_ready, n + 1)
                    need(pool, rden_ready, n - 1)
                    pool.tensor_tensor(denom[:, par, :], sums[:, par, :], sink_exp[:, par, :], ALU.add).then_inc(denom_ready, 1)

                def divide(b, gr):
                    n = count(b, NG, gr)
                    par = gr % 2
                    pool.wait_ge(rden_ready, n + 1)
                    need(pool, probsT_done, n - 1)
                    pool.tensor_tensor(probs[:, par, :].rearrange("p (h k) -> p h k", k=S), ex[:, par, :].rearrange("p (h k) -> p h k", k=S),
                                       rden[:, par, :].rearrange("p (h a) -> p h a", a=1).broadcast_to([128, G4, S]), ALU.mult).then_inc(probs_ready, 1)

                def body(b, par, first, last):
                    for gr in range(NG):
                        argue(b, gr)
                        total(b, gr)
                        divide(b, gr)
                        if not first:
                            finish(b - 1, gr)
                        if gr == E0 and not last:
                            copy_x(b + 1, 1 - par)
                over_pairs(pool, body)
                for gr in range(E0, E0 + 9):
                    finish(NB - 1, gr)

            @block.scalar
            def _(act):
                act.wait_ge(weights, 7 * 16)

                def q_copy(b, k):
                    n = count(b, NP, k)
                    act.wait_ge(q_done, n + 1)
                    need(act, scores_done, count(b, NG, 2 * k - 2))
                    for c in range(4):
                        ch = 4 * k + c
                        ins = act.activation(qT[:, k % 2, c * S:(c + 1) * S], p_q[:, c * S:(c + 1) * S], ACT.Identity, bias=bq[:, ch:ch + 1])
                    ins.then_inc(q_ready, 1)

                def xT_copy(b, par):
                    act.wait_ge(xT_done, b + 1)
                    act.activation(xT[:, par, :], p_q[:, 0:S], ACT.Copy).then_inc(xT_ready, 1)

                def exps(b, gr):
                    n = count(b, NG, gr)
                    par = gr % 2
                    act.wait_ge(shift_ready, n + 1)
                    need(act, probs_ready, n - 1)
                    need(act, denom_ready, n - 1)
                    for j in range(G4):
                        ins = act.activation(ex[:, par, j * S:(j + 1) * S], p_s[par][:, j * S:(j + 1) * S], ACT.Exp,
                                             bias=shift[:, par, j:j + 1], scale=SCALE, accum_out=sums[:, par, j:j + 1])
                    ins.then_inc(ex_ready, 1)
                    act.wait_ge(arg_ready, n + 1)
                    act.activation(sink_exp[:, par, :], sink_arg[:, par, :], ACT.Exp).then_inc(sinkexp_ready, 1)

                xT_copy(0, 0)
                q_copy(0, 0)

                def body(b, par, first, last):
                    for gr in range(NG):
                        exps(b, gr)
                        if gr % 2 == 0:
                            if gr < NG - 2:
                                q_copy(b, gr // 2 + 1)
                            elif not last:
                                q_copy(b + 1, 0)
                        if gr == 7 and not last:
                            xT_copy(b + 1, 1 - par)
                over_pairs(act, body)

            @block.vector
            def _(dve):
                dve.wait_ge(weights, 7 * 16)
                dve.tensor_scalar(neg_sinks[:, :], sinks[:, :], -1.0, None, ALU.mult).then_inc(neg_sinks_ready, 1)
                dve.wait_ge(neg_sinks_ready, 1)

                def kv_copy(b, k, par):
                    dve.wait_ge(kv_done, count(b, 3, k + 1))
                    if k < 2:
                        dve.tensor_tensor(kT[:, par, k * 4 * S:(k + 1) * 4 * S].rearrange("p (h s) -> p h s", s=S), p_q[:, :].rearrange("p (h s) -> p h s", s=S),
                                          bk2[:, 4 * k:4 * k + 4].rearrange("p (h a) -> p h a", a=1).broadcast_to([128, 4, S]), ALU.add).then_inc(kv_ready, 1)
                    else:
                        dve.tensor_tensor(v[:, par, :], p_q[:, :], bv[:, :], ALU.add).then_inc(kv_ready, 1)

                def shifts(b, gr):
                    n = count(b, NG, gr)
                    par = gr % 2
                    dve.wait_ge(scores_done, n + 1)
                    dve.tensor_reduce(max_neg[:, par, :], p_s[par][:, :].rearrange("p (h k) -> p h k", k=S), X_AXIS, ALU.max, negate=True).then_inc(max_ready, 1)
                    dve.wait_ge(max_ready, n + 1)
                    need(dve, ex_ready, n - 1)
                    need(dve, arg_ready, n - 1)
                    dve.scalar_tensor_tensor(out=shift[:, par, :], in0=max_neg[:, par, :], scalar=SCALE,
                                             in1=neg_sinks[:, heads(gr)], op0=ALU.mult, op1=ALU.min).then_inc(shift_ready, 1)

                def invert(b, gr):
                    n = count(b, NG, gr)
                    par = gr % 2
                    dve.wait_ge(denom_ready, n + 1)
                    need(dve, probs_ready, n - 1)
                    dve.reciprocal(rden[:, par, :], denom[:, par, :]).then_inc(rden_ready, 1)

                def probsT_copy(b, gr):
                    n = count(b, NG, gr)
                    dve.wait_ge(probsT_done, n + 1)
                    need(dve, oT_done, count(b, NP, gr // 2 - 1))
                    dve.tensor_copy(probsT[:, gr % 4, :], p_t[gr % 2][:, :]).then_inc(probsT_ready, 1)

                def oT_copy(b, k):
                    n = count(b, NP, k)
                    dve.wait_ge(oT_done, n + 1)
                    need(dve, y_done, n - 1)
                    dve.tensor_copy(oT[:, k % 2, :], p_o[k % 2][:, :]).then_inc(oT_ready, 1)

                def finish(b, gr, par):
                    if gr == E0:
                        dve.wait_ge(y_done, count(b, NP, NP))
                        need(dve, res2_ready, b)
                        dve.tensor_tensor(res[:, :], p_y[:, 0:DM], x_in[:, par, :], ALU.add).then_inc(res_ready, 1)
                    if gr == E0 + 1:
                        dve.wait_ge(res2_ready, b + 1)
                        norm.dve_moments(dve, b, 0, res2[:, :])
                    if gr == E0 + 2:
                        norm.dve_moments(dve, b, 1, cols(g.context, b, DC))
                    if gr == E0 + 3:
                        norm.dve_scale(dve, b, 0, cols(g.x1, b, DM), res2[:, :]).then_inc(x1_ready, 1)
                    if gr == E0 + 4:
                        g.wait_apart(dve, x1_ready, b + 1)
                        norm.dve_moments(dve, b, 2, cols(g.x1, b, DM))
                    if gr == E0 + 5:
                        norm.dve_scale(dve, b, 1, cols(g.context_n, b, DC), cols(g.context, b, DC)).then_inc(context_ready, 1)
                    if gr == E0 + 6:
                        need(dve, n1g_ready, b)
                        norm.dve_scale(dve, b, 2, n1[:, :], cols(g.x1, b, DM)).then_inc(n1_ready, 1)
                    if gr == E0 + 8:
                        g.wait_apart(dve, xc_ready, b + 1)
                        norm.dve_moments(dve, b, 3, cols(g.xc, b, DM))
                    if gr == E0 + 10:
                        norm.dve_scale(dve, b, 3, cols(g.nx, b, DM), cols(g.xc, b, DM)).then_inc(nx_ready, 1)

                for k in range(3):
                    kv_copy(0, k, 0)

                def body(b, par, first, last):
                    for gr in range(NG):
                        if gr % 2 == 1 and (not first or gr >= 5):
                            oT_copy(*back(b, gr // 2 - 2, NP))
                        if not first or gr >= 1:
                            invert(*back(b, gr - 1, NG))
                        shifts(b, gr)
                        if not first or gr >= 2:
                            probsT_copy(*back(b, gr - 2, NG))
                        if not first:
                            finish(b - 1, gr, 1 - par)
                        if gr in (9, 11, 13) and not last:
                            kv_copy(b + 1, (gr - 9) // 2, 1 - par)
                over_pairs(dve, body)
                invert(NB - 1, NG - 1)
                for gr in (NG - 2, NG - 1):
                    probsT_copy(NB - 1, gr)
                for k in (NP - 2, NP - 1):
                    oT_copy(NB - 1, k)
                for gr in range(E0, E0 + 11):
                    finish(NB - 1, gr, 1)
                dve.wait_ge(nx_ready, NB)
                dve.wait_ge(context_ready, NB)

            @block.tensor
            def _(pe):
                pe.wait_ge(weights, 7 * 16)
                pe.wait_ge(mask_ready, 1)
                pe.wait_ge(g.setup_done, 1)

                def transpose_x(b, par):
                    pe.wait_ge(x_ready, b + 1)
                    need(pe, q_ready, count(b - 1, NP, 5) if not (isinstance(b, int) and b == 0) else 0)
                    pe.transpose(p_q[:, 0:S], x_in[:, par, :], g.ident[:, :]).then_inc(xT_done, 1)

                def project_kv(b, k, par):
                    if k == 0:
                        pe.wait_ge(xT_ready, b + 1)
                    need(pe, kv_ready, count(b, 3, k))
                    if not (isinstance(b, int) and b == 0):
                        pe.wait_ge(q_ready, count(b - 1, NP, 6 + k))
                    if k < 2:
                        for c in range(4):
                            h = 4 * k + c
                            ins = pe.matmul(p_q[:, c * S:(c + 1) * S], wk2[:, h * 128:(h + 1) * 128], xT[:, par, :], start=True, stop=True)
                    else:
                        ins = pe.matmul(p_q[:, :], xT[:, par, :], wv[:, :], start=True, stop=True)
                    ins.then_inc(kv_done, 1)

                def project_q(b, k, par):
                    n = count(b, NP, k)
                    need(pe, q_ready, n)
                    if k == 5:
                        if not (isinstance(b, int) and b == NB - 1):
                            pe.wait_ge(xT_ready, b + 2)
                    if k in (6, 7):
                        if not (isinstance(b, int) and b == NB - 1):
                            pe.wait_ge(kv_ready, count(b + 1, 3, k - 5))
                    if k == 0:
                        pe.wait_ge(kv_ready, count(b, 3, 3))
                    for c in range(4):
                        ch = 4 * k + c
                        ins = pe.matmul(p_q[:, c * S:(c + 1) * S], wq[:, ch * 128:(ch + 1) * 128], xT[:, par, :], start=True, stop=True)
                    ins.then_inc(q_done, 1)

                def score(b, gr, par):
                    n = count(b, NG, gr)
                    kv = gr // 2
                    r = gr % 2
                    if r == 0:
                        pe.wait_ge(q_ready, count(b, NP, gr // 2 + 1))
                    if gr == 0:
                        pe.wait_ge(kv_ready, count(b, 3, 3))
                    need(pe, ex_ready, n - 1)
                    pe.matmul(p_s[r][:, :], g.ident_bf[:, :], mask[:, :], start=True, stop=False, skip_group_check=True)
                    for j in range(G4):
                        ins = pe.matmul(p_s[r][:, j * S:(j + 1) * S], qT[64 * r:64 * r + 64, kv % 2, j * S:(j + 1) * S],
                                        kT[64 * r:64 * r + 64, par, kv * S:(kv + 1) * S], start=False, stop=True, skip_group_check=True)
                    ins.then_inc(scores_done, 1)

                def transpose_probs(b, gr):
                    n = count(b, NG, gr)
                    r = gr % 2
                    pe.wait_ge(probs_ready, n + 1)
                    need(pe, probsT_ready, n - 1)
                    for j in range(G4):
                        ins = pe.transpose(p_t[r][:, j * S:(j + 1) * S], probs[:, r, j * S:(j + 1) * S], g.ident[:, :])
                    ins.then_inc(probsT_done, 1)

                def weigh(b, k, par):
                    n = count(b, NP, k)
                    pe.wait_ge(probsT_ready, count(b, NG, 2 * k + 2))
                    need(pe, oT_ready, n - 1)
                    for r in (0, 1):
                        ins = pe.matmul(p_o[k % 2][r * HD:(r + 1) * HD, :], v[:, par, k * HD:(k + 1) * HD], probsT[:, (2 * k + r) % 4, :], start=True, stop=True)
                    ins.then_inc(oT_done, 1)

                def project_o(b, k):
                    n = count(b, NP, k)
                    if k == 0:
                        need(pe, res_ready, b)
                    pe.wait_ge(oT_ready, n + 1)
                    for c in range(4):
                        ch = 4 * k + c
                        ins = pe.matmul(p_y[:, 0:DM], oT[:, k % 2, c * S:(c + 1) * S], wo[:, ch * DM:(ch + 1) * DM], start=(ch == 0), stop=(ch == NCH - 1))
                    ins.then_inc(y_done, 1)

                transpose_x(0, 0)
                for k in range(3):
                    project_kv(0, k, 0)
                project_q(0, 0, 0)
                pe.wait_ge(w_wo, 4 * 16)

                def body(b, par, first, last):
                    for gr in range(NG):
                        score(b, gr, par)
                        if not first or gr >= 2:
                            transpose_probs(*back(b, gr - 2, NG))
                        if gr % 2 == 0 and (not first or gr >= 4):
                            weigh(*back(b, gr // 2 - 2, NP), par if gr >= 4 else 1 - par)
                        if gr % 2 == 1 and (not first or gr >= 5):
                            project_o(*back(b, gr // 2 - 2, NP))
                        if gr % 2 == 0:
                            if gr < NG - 2:
                                project_q(b, gr // 2 + 1, par)
                            elif not last:
                                project_q(b + 1, 0, 1 - par)
                        if gr == 7 and not last:
                            transpose_x(b + 1, 1 - par)
                        if gr in (9, 11, 13) and not last:
                            project_kv(b + 1, (gr - 9) // 2, 1 - par)
                over_pairs(pe, body)
                for gr in (NG - 2, NG - 1):
                    transpose_probs(NB - 1, gr)
                for k in (NP - 2, NP - 1):
                    weigh(NB - 1, k, 1)
                    project_o(NB - 1, k)


class Heads16:

    def __init__(self, name, scale, width, own_keys, affine, bias, later_mask):
        self.name, self.scale, self.width = name, scale, width
        self.own_keys, self.affine, self.bias, self.later_mask = own_keys, affine, bias, later_mask


def attention16(g, cfg):
    nc, t = g.nc, g.t
    NG, G4, HD, DY = 4, 4, 32, cfg.width
    OC = 16 * HD // 128
    with ExitStack() as ctx:
        sb = lambda name, shape, dt=F32: g.sb(cfg.name + name, shape, dt, ctx)
        W = g.weights[cfg.name]
        kvw = DY if not cfg.own_keys else DM
        x_in, y_in = sb("x_in", [128, DM]), sb("y_in", [128, DY])
        xT, yT = sb("xT", [128, S]), sb("yT", [128, S])
        qT, kT = sb("qT", [128, 2, 4 * S]), sb("kT", [128, 2, 4 * S])
        v = sb("v", [128, 2, 16 * HD])
        ex, probs = sb("ex", [128, 2, G4 * S]), sb("probs", [128, 2, G4 * S])
        probsT, oT = sb("probsT", [128, 2 * NG, G4 * S]), sb("oT", [128, OC * S])
        max_neg, shift = sb("max_neg", [128, 2, G4]), sb("shift", [128, 2, G4])
        sums, rden = sb("sums", [128, 2, G4]), sb("rden", [128, 2, G4])
        res, res2 = sb("res", [128, DM]), sb("res2", [128, DM])
        banks = g.banks([cfg.name + n for n in ("s0", "s1", "s2", "s3", "pt", "po", "pa", "pb")], ctx)
        p_s, (p_t, p_o, p_a, p_b) = banks[:4], banks[4:]
        norm = Norm(g, cfg.name + "ln", 1, ctx)
        if cfg.later_mask:
            keep = sb("keep", [128, S])

        sem = lambda n: g.sem(cfg.name + n)
        keep_one, keep_ready = sem("keep_one"), sem("keep_ready")
        x_ready, T_done, T_ready = sem("x_ready"), sem("T_done"), sem("T_ready")
        q_done, q_ready, k_done, k_ready, v_done, v_ready = (sem(n) for n in ("q_done", "q_ready", "k_done", "k_ready", "v_done", "v_ready"))
        scores_done, max_ready, shift_ready, ex_ready = sem("scores_done"), sem("max_ready"), sem("shift_ready"), sem("ex_ready")
        rden_ready, probs_ready, probsT_done, probsT_ready = sem("rden_ready"), sem("probs_ready"), sem("probsT_done"), sem("probsT_ready")
        oT_done, oT_ready, y_done, res_ready, res2_ready, out_ready = (sem(n) for n in ("oT_done", "oT_ready", "y_done", "res_ready", "res2_ready", "out_ready"))

        residual = g.x1 if cfg.name == "h_" else g.xc
        q_src = g.x1 if cfg.name == "h_" else g.nx
        k_src = g.context if cfg.name == "h_" else g.context_n

        with nc.Block() as block:
            @block.gpsimd
            def _(pool):
                if cfg.later_mask:
                    pool.memset(keep[:, :], 1.0).then_inc(keep_one, 1)
                    pool.wait_ge(keep_one, 1)
                    pool.affine_select(out=keep[:, :], in_=keep[:, :], compare_op=ALU.is_gt, fill=0.0, base=0,
                                       pattern=[[-1, S]], channel_multiplier=1).then_inc(keep_ready, 1)
                pool.wait_ge(W.loaded, W.total)

                def copy_in(b):
                    g.wait_apart(pool, T_done, b)
                    ins = pool.tensor_copy(x_in[:, :], cols(q_src, b, DM))
                    if not cfg.own_keys:
                        ins.then_inc(x_ready, 1)
                        ins = pool.tensor_copy(y_in[:, :], cols(k_src, b, DC))
                    ins.then_inc(x_ready, 1)

                def divide(b, gr):
                    n = count(b, NG, gr)
                    pool.wait_ge(rden_ready, n + 1)
                    need(pool, probsT_done, n - 1)
                    pool.tensor_tensor(probs[:, gr % 2, :].rearrange("p (h k) -> p h k", k=S), ex[:, gr % 2, :].rearrange("p (h k) -> p h k", k=S),
                                       rden[:, gr % 2, :].rearrange("p (h a) -> p h a", a=1).broadcast_to([128, G4, S]), ALU.mult).then_inc(probs_ready, 1)

                def finish(b, gr):
                    if gr == 0:
                        g.wait_apart(pool, res_ready, b + 1)
                        if cfg.name == "h_":
                            need(pool, out_ready, b)
                            pool.tensor_tensor(res2[:, :], res[:, :], W["bo"][:, :], ALU.add).then_inc(res2_ready, 1)
                        else:
                            pool.tensor_tensor(cols(g.xo, b, DM), res[:, :], W["bo"][:, :], ALU.add).then_inc(res2_ready, 1)
                    if gr == 1:
                        norm.pool_rstd(pool, b, 0)

                copy_in(0)
                copy_in(1)

                def body(b, par, first, last):
                    for gr in range(NG):
                        divide(b, gr)
                        if gr in (0, 1) and not early(b):
                            finish(b - 2, gr)
                        if gr == 0 and not late(b):
                            copy_in(b + 2)
                over_pairs(pool, body)
                for b in (NB - 2, NB - 1):
                    for gr in (0, 1):
                        finish(b, gr)

            @block.scalar
            def _(act):
                act.wait_ge(W.loaded, W.total)

                def T_copy(b):
                    act.wait_ge(T_done, b + 1)
                    if cfg.affine:
                        act.activation(xT[:, :], p_a[:, 0:S], ACT.Identity, scale=W["gx"][:, 0:1], bias=W["bx"][:, 0:1])
                        src = p_a[0:kvw, 0:S] if cfg.own_keys else p_a[0:kvw, S:2 * S]
                        act.activation(yT[0:kvw, :], src, ACT.Identity, scale=W["gy"][0:kvw, 0:1], bias=W["by"][0:kvw, 0:1]).then_inc(T_ready, 1)
                    else:
                        act.activation(xT[:, :], p_a[:, 0:S], ACT.Copy)
                        act.activation(yT[0:kvw, :], p_a[0:kvw, S:2 * S], ACT.Copy).then_inc(T_ready, 1)

                def q_copy(b, par):
                    act.wait_ge(q_done, b + 1)
                    if cfg.bias:
                        for c in range(4):
                            ins = act.activation(qT[:, par, c * S:(c + 1) * S], p_b[:, c * S:(c + 1) * S], ACT.Identity, bias=W["bq"][:, c:c + 1])
                    else:
                        ins = act.activation(qT[:, par, :], p_b[:, :], ACT.Copy)
                    ins.then_inc(q_ready, 1)

                def exps(b, gr):
                    n = count(b, NG, gr)
                    act.wait_ge(shift_ready, n + 1)
                    need(act, probs_ready, n - 1)
                    for j in range(G4):
                        ins = act.activation(ex[:, gr % 2, j * S:(j + 1) * S], p_s[gr][:, j * S:(j + 1) * S], ACT.Exp,
                                             bias=shift[:, gr % 2, j:j + 1], scale=cfg.scale, accum_out=sums[:, gr % 2, j:j + 1])
                    ins.then_inc(ex_ready, 1)

                def k_copy(b, par):
                    act.wait_ge(k_done, b + 1)
                    if cfg.bias:
                        for c in range(4):
                            ins = act.activation(kT[:, par, c * S:(c + 1) * S], p_a[:, c * S:(c + 1) * S], ACT.Identity, bias=W["bk"][:, c:c + 1])
                    else:
                        ins = act.activation(kT[:, par, :], p_a[:, :], ACT.Copy)
                    ins.then_inc(k_ready, 1)

                def oT_copy(b):
                    act.wait_ge(oT_done, b + 1)
                    need(act, y_done, b)
                    act.activation(oT[:, :], p_o[:, :], ACT.Copy).then_inc(oT_ready, 1)

                T_copy(0)
                q_copy(0, 0)
                k_copy(0, 0)

                def body(b, par, first, last):
                    for gr in range(NG):
                        if gr == 0 and not early(b):
                            oT_copy(b - 2)
                        if gr == 0 and not last:
                            T_copy(b + 1)
                        exps(b, gr)
                        if gr == 1 and not last:
                            q_copy(b + 1, 1 - par)
                        if gr == 2 and not last:
                            k_copy(b + 1, 1 - par)
                over_pairs(act, body)
                oT_copy(NB - 2)
                oT_copy(NB - 1)

            @block.vector
            def _(dve):
                dve.wait_ge(W.loaded, W.total)
                if cfg.later_mask:
                    dve.wait_ge(keep_ready, 1)

                def v_copy(b, par):
                    dve.wait_ge(v_done, b + 1)
                    need(dve, oT_done, b - 1)
                    if cfg.bias:
                        dve.tensor_tensor(v[:, par, :], p_b[:, 0:16 * HD], W["bv"][:, :], ALU.add).then_inc(v_ready, 1)
                    else:
                        dve.tensor_copy(v[:, par, :], p_b[:, 0:16 * HD]).then_inc(v_ready, 1)

                def shifts(b, gr):
                    n = count(b, NG, gr)
                    par = gr % 2
                    dve.wait_ge(scores_done, n + 1)
                    dve.tensor_reduce(max_neg[:, par, :], p_s[gr][:, :].rearrange("p (h k) -> p h k", k=S), X_AXIS, ALU.max, negate=True).then_inc(max_ready, 1)
                    dve.wait_ge(max_ready, n + 1)
                    need(dve, ex_ready, n - 1)
                    dve.tensor_scalar(shift[:, par, :], max_neg[:, par, :], cfg.scale, None, ALU.mult).then_inc(shift_ready, 1)

                def invert(b, gr):
                    n = count(b, NG, gr)
                    dve.wait_ge(ex_ready, n + 1)
                    need(dve, probs_ready, n - 1)
                    dve.reciprocal(rden[:, gr % 2, :], sums[:, gr % 2, :]).then_inc(rden_ready, 1)

                def probsT_copy(b, gr, par):
                    dve.wait_ge(probsT_done, count(b, NG, gr + 1))
                    need(dve, oT_done, b - 1)
                    to = probsT[:, par * NG + gr, :]
                    if cfg.later_mask:
                        dve.tensor_tensor(to.rearrange("p (h q) -> p h q", q=S), p_t[:, :].rearrange("p (h q) -> p h q", q=S),
                                          keep[:, :].rearrange("p (a q) -> p a q", a=1).broadcast_to([128, G4, S]), ALU.mult).then_inc(probsT_ready, 1)
                    else:
                        dve.tensor_copy(to, p_t[:, :]).then_inc(probsT_ready, 1)

                def finish(b, gr):
                    if gr == 0:
                        dve.wait_ge(y_done, b + 1)
                        need(dve, res2_ready, b)
                        dve.tensor_tensor(res[:, :], p_b[:, 0:DM], cols(residual, b, DM), ALU.add).then_inc(res_ready, 1)
                    if gr == 1:
                        src = res2[:, :] if cfg.name == "h_" else cols(g.xo, b, DM)
                        g.wait_apart(dve, res2_ready, b + 1)
                        norm.dve_moments(dve, b, 0, src)
                    if gr == 3:
                        src, dst = (res2[:, :], g.x1) if cfg.name == "h_" else (cols(g.xo, b, DM), g.nx)
                        norm.dve_scale(dve, b, 0, cols(dst, b, DM), src).then_inc(out_ready, 1)

                v_copy(0, 0)

                def body(b, par, first, last):
                    for gr in range(NG):
                        if not first or gr >= 1:
                            invert(*back(b, gr - 1, NG))
                        shifts(b, gr)
                        if not first or gr >= 2:
                            probsT_copy(*back(b, gr - 2, NG), par if gr >= 2 else 1 - par)
                        if not early(b):
                            finish(b - 2, gr)
                        if gr == 3 and not last:
                            v_copy(b + 1, 1 - par)
                over_pairs(dve, body)
                invert(NB - 1, NG - 1)
                for gr in (NG - 2, NG - 1):
                    probsT_copy(NB - 1, gr, 1)
                for b in (NB - 2, NB - 1):
                    for gr in range(NG):
                        finish(b, gr)
                dve.wait_ge(out_ready, NB)

            @block.tensor
            def _(pe):
                pe.wait_ge(W.loaded, W.total)
                pe.wait_ge(g.setup_done, 1)

                def transpose_in(b):
                    need(pe, k_ready, b)
                    if cfg.own_keys:
                        pe.wait_ge(x_ready, b + 1)
                        pe.transpose(p_a[:, 0:S], x_in[:, :], g.ident[:, :]).then_inc(T_done, 1)
                    else:
                        pe.wait_ge(x_ready, count(b, 2, 2))
                        pe.transpose(p_a[:, 0:S], x_in[:, :], g.ident[:, :])
                        pe.transpose(p_a[0:DC, S:2 * S], y_in[:, :], g.ident[:, :]).then_inc(T_done, 1)

                def project_q(b):
                    pe.wait_ge(T_ready, b + 1)
                    if isinstance(b, int) and b < 3:
                        need(pe, v_ready, b)
                    need(pe, res_ready, b - 2)
                    for c in range(4):
                        ins = pe.matmul(p_b[:, c * S:(c + 1) * S], W["wq"][:, c * 128:(c + 1) * 128], xT[:, :], start=True, stop=True)
                    ins.then_inc(q_done, 1)

                def project_k(b):
                    pe.wait_ge(T_ready, b + 1)
                    for c in range(4):
                        ins = pe.matmul(p_a[:, c * S:(c + 1) * S], W["wk"][0:kvw, c * 128:(c + 1) * 128], yT[0:kvw, :], start=True, stop=True)
                    ins.then_inc(k_done, 1)

                def project_v(b):
                    pe.wait_ge(q_ready, b + 1)
                    pe.matmul(p_b[:, 0:16 * HD], yT[0:kvw, :], W["wv"][0:kvw, :], start=True, stop=True).then_inc(v_done, 1)

                def score(b, gr, par):
                    n = count(b, NG, gr)
                    if gr == 0:
                        pe.wait_ge(q_ready, b + 1)
                        pe.wait_ge(k_ready, b + 1)
                    need(pe, ex_ready, n - 3)
                    for c in range(4):
                        r = 32 * gr
                        ins = pe.matmul(p_s[gr][:, c * S:(c + 1) * S], qT[r:r + 32, par, c * S:(c + 1) * S], kT[r:r + 32, par, c * S:(c + 1) * S],
                                        start=True, stop=True, tile_position=(r, 0))
                    ins.then_inc(scores_done, 1)

                def transpose_probs(b, gr):
                    n = count(b, NG, gr)
                    pe.wait_ge(probs_ready, n + 1)
                    need(pe, probsT_ready, n)
                    for j in range(G4):
                        ins = pe.transpose(p_t[:, j * S:(j + 1) * S], probs[:, gr % 2, j * S:(j + 1) * S], g.ident[:, :])
                    ins.then_inc(probsT_done, 1)

                def weigh(b, half, par):
                    if half == 0:
                        pe.wait_ge(v_ready, b + 1)
                        pe.wait_ge(probsT_ready, count(b, NG, NG))
                        need(pe, oT_ready, b)
                    for c in (2 * half, 2 * half + 1):
                        for j in range(G4):
                            h = 4 * c + j
                            ins = pe.matmul(p_o[j * HD:(j + 1) * HD, c * S:(c + 1) * S], v[:, par, h * HD:(h + 1) * HD],
                                            probsT[:, par * NG + j, c * S:(c + 1) * S], start=True, stop=True)
                    if half == 1:
                        ins.then_inc(oT_done, 1)

                def project_o(b):
                    pe.wait_ge(oT_ready, b + 1)
                    if b_known_last(b):
                        pe.wait_ge(v_ready, NB)
                        need(pe, res_ready, b)
                    else:
                        pe.wait_ge(v_ready, b + 3)
                    for c in range(OC):
                        ins = pe.matmul(p_b[:, 0:DM], oT[:, c * S:(c + 1) * S], W["wo"][:, c * DM:(c + 1) * DM], start=(c == 0), stop=(c == OC - 1))
                    ins.then_inc(y_done, 1)

                def b_known_last(b):
                    return isinstance(b, int) and b + 3 > NB

                transpose_in(0)
                project_q(0)
                project_k(0)
                project_v(0)

                def body(b, par, first, last):
                    for gr in range(NG):
                        score(b, gr, par)
                        if gr == 0 and not last:
                            transpose_in(b + 1)
                        if not first or gr >= 2:
                            transpose_probs(*back(b, gr - 2, NG))
                        if gr == 0 and not early(b):
                            project_o(b - 2)
                        if gr == 1 and not last:
                            project_q(b + 1)
                        if gr == 2 and not last:
                            project_k(b + 1)
                        if gr >= 2 and not first:
                            weigh(b - 1, gr - 2, 1 - par)
                        if gr == 3 and not last:
                            project_v(b + 1)
                over_pairs(pe, body)
                project_o(NB - 2)
                for gr in (NG - 2, NG - 1):
                    transpose_probs(NB - 1, gr)
                for half in (0, 1):
                    weigh(NB - 1, half, 1)
                project_o(NB - 1)


BB = 4
NBK = NB // BB


class NormBlock:

    def __init__(self, g, name, per, ctx):
        nc = g.nc
        self.g, self.per = g, per
        sb = lambda n, w: ctx.enter_context(nc.sbuf_tensor(name + n, [128, per, BB, w], F32))
        self.stats, self.mv, self.var_eps, self.rstd = sb("_stats", 6), sb("_mean_var", 2), sb("_var_eps", 1), sb("_rstd", 1)
        self.stats_done, self.moments = g.sem(name + "_stats_done"), g.sem(name + "_moments_ready")
        self.eps_added, self.rstd_ready = g.sem(name + "_eps_added"), g.sem(name + "_rstd_ready")

    def dve_moments(self, dve, i, n, src):
        done = count(i, self.per, n + 1)
        for k in range(BB):
            ins = dve.bn_stats(self.stats[:, n, k, :], src[:, k * DM:(k + 1) * DM])
        ins.then_inc(self.stats_done, 1)
        self.g.wait_apart(dve, self.stats_done, done)
        for k in range(BB):
            ins = dve.bn_aggr(self.mv[:, n, k, :], self.stats[:, n, k, :])
        ins.then_inc(self.moments, 1)

    def pool_rstd(self, pool, i, n):
        done = count(i, self.per, n + 1)
        four = lambda tile: tile[:, :].rearrange("p (a k) -> p a k", a=1).broadcast_to([128, BB, 1])
        pool.wait_ge(self.moments, done)
        pool.tensor_tensor(self.var_eps[:, n], self.mv[:, n, :, 1:2], four(self.g.eps), ALU.add).then_inc(self.eps_added, 1)
        pool.wait_ge(self.eps_added, done)
        pool.tensor_tensor(self.rstd[:, n], self.var_eps[:, n], four(self.g.minus_half), ALU.pow).then_inc(self.rstd_ready, 1)

    def dve_scale(self, dve, i, n, out, src):
        dve.wait_ge(self.rstd_ready, count(i, self.per, n + 1))
        for k in range(BB):
            ins = dve.tensor_scalar(out[:, k * DM:(k + 1) * DM], src[:, k * DM:(k + 1) * DM], self.mv[:, n, k, 0:1], self.rstd[:, n, k, 0:1],
                                    ALU.subtract, ALU.mult)
        return ins


def over_blocks(eng, body, ahead=1):
    for i in range(ahead):
        body(i, i == 0, False)
    with eng.Fori(ahead, NBK - 1) as i:
        body(i, False, False)
    body(NBK - 1, False, True)


def block_cols(tile, i):
    return cols(tile, i, BB * DM)


def mlp(g, name):
    nc = g.nc
    FC, FF = 4, 512
    quantum, two_norms = name == "i_", name == "c_"
    W = g.weights[name]
    PI = 3.14159274101257324
    TURN_HI, TURN_LO = 6.28125, 0.0019353071795864769
    ROUND = 1.5 * 2.0 ** 23
    with ExitStack() as ctx:
        sb = lambda n, shape, dt=F32: g.sb(name + n, shape, dt, ctx)
        x_in, xT = sb("x_in", [128, BB * DM]), sb("xT", [128, BB * S])
        hidden = sb("hidden", [128, FC, BB * S])
        res, sum1, sum2, sum3 = (sb(n, [128, BB * DM]) for n in ("res", "sum1", "sum2", "sum3"))
        n1, n1g = sb("n1", [128, BB * DM]), sb("n1g", [128, BB * DM])
        p_t, h0, h1, p_y = g.banks([name + n for n in ("pt", "h0", "h1", "py")], ctx)
        p_h = [h0, h1]
        norm = NormBlock(g, name + "ln", 2 if two_norms else 1, ctx)
        sem = lambda n: g.sem(name + n)
        x_ready, T_done, T_ready, h_done, h_ready, y_done = (sem(n) for n in ("x_ready", "T_done", "T_ready", "h_done", "h_ready", "y_done"))
        res_ready, sum1_ready, sum2_ready, sum3_ready = (sem(n) for n in ("res_ready", "sum1_ready", "sum2_ready", "sum3_ready"))
        n1_ready, n1g_ready, xc_ready, out_ready = (sem(n) for n in ("n1_ready", "n1g_ready", "xc_ready", "out_ready"))
        total = sum1 if quantum else sum2 if two_norms else sum3
        total_ready = sum1_ready if quantum else sum2_ready if two_norms else sum3_ready
        if quantum:
            pre, arg, turns, turns_i, arg1, arg2, arg3, sine, mixed = (
                sb(n, [128, 2, BB * S]) for n in ("pre", "arg", "turns", "turns_i", "arg1", "arg2", "arg3", "sine", "mixed"))
            small = {n: sb("k_" + n, [128, FC]) for n in ("turns", "turns_i", "r1", "r2", "r3", "neg", "abs", "cos_arg", "sin", "cos", "sw", "cw", "phase", "phase_w", "coef", "b_tenth", "offset", "half_pi")}
            k_step, coef_ready, hidden_read, arg_done, turns_done, turns_i_done, arg1_done, arg2_done, arg3_done, sine_done, mixed_done = (
                sem(n) for n in ("k_step", "coef_ready", "hidden_read", "arg_done", "turns_done", "turns_i_done", "arg1_done", "arg2_done", "arg3_done", "sine_done", "mixed_done"))

        with nc.Block() as block:
            @block.gpsimd
            def _(pool):
                pool.wait_ge(W.loaded, W.total)
                wide = lambda tile: tile[:, :].rearrange("p (a n) -> p a n", a=1).broadcast_to([128, BB, DM])
                four = lambda tile: tile.rearrange("p (k n) -> p k n", n=DM)

                def copy_in(i):
                    g.wait_apart(pool, T_done, i)
                    pool.tensor_copy(x_in[:, :], block_cols(g.x1 if quantum else g.nx, i)).then_inc(x_ready, 1)

                def finish(i):
                    pool.wait_ge(res_ready, i + 1)
                    need(pool, out_ready if quantum else sum2_ready, i)
                    pool.tensor_tensor(four(sum1[:, :]), four(res[:, :]), wide(W["b2"]), ALU.add).then_inc(sum1_ready, 1)
                    if not quantum:
                        g.wait_apart(pool, sum1_ready, i + 1)
                        need(pool, n1_ready if two_norms else sum3_ready, i)
                        pool.tensor_tensor(sum2[:, :], sum1[:, :], block_cols(g.xc, i), ALU.add).then_inc(sum2_ready, 1)
                    if name == "e_":
                        g.wait_apart(pool, sum2_ready, i + 1)
                        need(pool, out_ready, i)
                        pool.tensor_tensor(sum3[:, :], sum2[:, :], block_cols(g.x1, i), ALU.add).then_inc(sum3_ready, 1)
                    norm.pool_rstd(pool, i, 0)
                    if two_norms:
                        pool.wait_ge(n1_ready, i + 1)
                        need(pool, xc_ready, i)
                        pool.tensor_tensor(four(n1g[:, :]), four(n1[:, :]), wide(W["ln_g"]), ALU.mult).then_inc(n1g_ready, 1)
                        g.wait_apart(pool, n1g_ready, i + 1)
                        pool.tensor_tensor(four(block_cols(g.xc, i)), four(n1g[:, :]), wide(W["ln_b"]), ALU.add).then_inc(xc_ready, 1)
                        norm.pool_rstd(pool, i, 1)

                copy_in(0)
                copy_in(1)

                def body(i, first, last):
                    if not first:
                        finish(i - 1)
                    if not last and not (isinstance(i, int) and i + 2 >= NBK):
                        copy_in(i + 2)
                body(0, True, False)
                with pool.Fori(1, NBK - 2) as i:
                    body(i, False, False)
                body(NBK - 2, False, False)
                body(NBK - 1, False, True)
                finish(NBK - 1)

            @block.scalar
            def _(act):
                act.wait_ge(W.loaded, W.total)

                def T_copy(i):
                    act.wait_ge(T_done, i + 1)
                    need(act, h_done, count(i, FC, 0))
                    if quantum:
                        act.activation(xT[:, :], p_t[:, :], ACT.Copy).then_inc(T_ready, 1)
                    else:
                        act.activation(xT[:, :], p_t[:, :], ACT.Identity, scale=W["gx"][:, 0:1], bias=W["bx"][:, 0:1]).then_inc(T_ready, 1)

                def gelu(i, f):
                    n = count(i, FC, f)
                    act.wait_ge(h_done, n + 1)
                    need(act, y_done, n - 3)
                    act.activation(hidden[:, f, :], p_h[f % 2][:, :], ACT.Gelu, bias=W["b1"][:, f:f + 1]).then_inc(h_ready, 1)

                def pre_sine(i, f):
                    n = count(i, FC, f)
                    act.wait_ge(h_done, n + 1)
                    need(act, mixed_done, n - 1)
                    act.activation(pre[:, f % 2, :], p_h[f % 2][:, :], ACT.Identity, bias=W["b1"][:, f:f + 1])
                    need(act, arg1_done, n - 1)
                    act.activation(arg[:, f % 2, :], p_h[f % 2][:, :], ACT.Identity, scale=0.1, bias=small["offset"][:, f:f + 1]).then_inc(arg_done, 1)

                def post_sine(i, f):
                    n = count(i, FC, f)
                    act.wait_ge(arg3_done, n + 1)
                    need(act, mixed_done, n - 1)
                    act.activation(sine[:, f % 2, :], arg3[:, f % 2, :], ACT.Sin).then_inc(sine_done, 1)

                def relu(i, f):
                    n = count(i, FC, f)
                    act.wait_ge(mixed_done, n + 1)
                    need(act, y_done, n - 3)
                    act.activation(hidden[:, f, :], mixed[:, f % 2, :], ACT.Relu).then_inc(h_ready, 1)

                if quantum:
                    act.wait_ge(k_step, 6)
                    act.activation(small["sin"][:, :], small["r3"][:, :], ACT.Sin).then_inc(k_step, 1)
                    act.wait_ge(k_step, 10)
                    act.activation(small["cos"][:, :], small["cos_arg"][:, :], ACT.Sin).then_inc(k_step, 1)
                    act.wait_ge(coef_ready, 1)
                T_copy(0)

                def body(i, first, last):
                    for f in range(FC):
                        if quantum:
                            pre_sine(i, f)
                            if not first or f >= 1:
                                post_sine(*back(i, f - 1, FC))
                            if not first or f >= 2:
                                relu(*back(i, f - 2, FC))
                        else:
                            gelu(i, f)
                        if f == 3 and not last:
                            T_copy(i + 1)
                over_blocks(act, body, ahead=2)
                if quantum:
                    post_sine(NBK - 1, FC - 1)
                    relu(NBK - 1, FC - 2)
                    relu(NBK - 1, FC - 1)

            @block.vector
            def _(dve):
                dve.wait_ge(W.loaded, W.total)

                def reduce_arg(a, n, turns, turns_i, r1, r2, r3, sems):
                    dve.tensor_scalar(turns, a, 1.0 / (2.0 * PI), ROUND, ALU.mult, ALU.add).then_inc(sems[0], 1)
                    dve.wait_ge(sems[0], n[0])
                    dve.tensor_scalar(turns_i, turns, ROUND, None, ALU.subtract).then_inc(sems[1], 1)
                    dve.wait_ge(sems[1], n[1])
                    dve.scalar_tensor_tensor(out=r1, in0=turns_i, scalar=-TURN_HI, in1=a, op0=ALU.mult, op1=ALU.add).then_inc(sems[2], 1)
                    dve.wait_ge(sems[2], n[2])
                    dve.scalar_tensor_tensor(out=r2, in0=turns_i, scalar=-TURN_LO, in1=r1, op0=ALU.mult, op1=ALU.add).then_inc(sems[3], 1)
                    dve.wait_ge(sems[3], n[3])

                if quantum:
                    theta, wr, wi = W["theta"], W["wr"], W["wi"]
                    k = small
                    reduce_arg(theta[:, :], (1, 2, 3, 4), k["turns"][:, :], k["turns_i"][:, :], k["r1"][:, :], k["r2"][:, :], k["r3"][:, :], (k_step,) * 4)
                    dve.memset(k["half_pi"][:, :], PI / 2).then_inc(k_step, 1)
                    dve.tensor_scalar(k["r3"][:, :], k["r2"][:, :], -PI, PI, ALU.max, ALU.min).then_inc(k_step, 1)
                    dve.wait_ge(k_step, 7)
                    dve.tensor_scalar(k["neg"][:, :], k["r3"][:, :], -1.0, None, ALU.mult).then_inc(k_step, 1)
                    dve.wait_ge(k_step, 8)
                    dve.tensor_tensor(k["abs"][:, :], k["r3"][:, :], k["neg"][:, :], ALU.max).then_inc(k_step, 1)
                    dve.wait_ge(k_step, 9)
                    dve.tensor_tensor(k["cos_arg"][:, :], k["half_pi"][:, :], k["abs"][:, :], ALU.subtract).then_inc(k_step, 1)
                    dve.wait_ge(k_step, 11)
                    dve.tensor_tensor(k["cw"][:, :], k["cos"][:, :], wr[:, :], ALU.mult).then_inc(k_step, 1)
                    dve.tensor_tensor(k["sw"][:, :], k["sin"][:, :], wi[:, :], ALU.mult).then_inc(k_step, 1)
                    dve.tensor_scalar(k["b_tenth"][:, :], W["b1"][:, :], 0.1, None, ALU.mult).then_inc(k_step, 1)
                    dve.wait_ge(k_step, 14)
                    dve.tensor_tensor(k["phase"][:, :], k["cw"][:, :], k["sw"][:, :], ALU.add).then_inc(k_step, 1)
                    dve.tensor_tensor(k["offset"][:, :], k["b_tenth"][:, :], theta[:, :], ALU.add).then_inc(k_step, 1)
                    dve.wait_ge(k_step, 16)
                    dve.tensor_tensor(k["phase_w"][:, :], k["phase"][:, :], wi[:, :], ALU.mult).then_inc(k_step, 1)
                    dve.wait_ge(k_step, 17)
                    dve.tensor_scalar(k["coef"][:, :], k["phase_w"][:, :], 0.1, None, ALU.mult).then_inc(coef_ready, 1)
                    dve.wait_ge(coef_ready, 1)

                def reduce_range(i, f):
                    n = count(i, FC, f) + 1
                    r = f % 2
                    dve.wait_ge(arg_done, n)
                    reduce_arg(arg[:, r, :], (n, n, n, n), turns[:, r, :], turns_i[:, r, :], arg1[:, r, :], arg2[:, r, :], None,
                               (turns_done, turns_i_done, arg1_done, arg2_done))
                    need(dve, sine_done, n - 2)
                    dve.tensor_scalar(arg3[:, r, :], arg2[:, r, :], -PI, PI, ALU.max, ALU.min).then_inc(arg3_done, 1)

                def mix(i, f):
                    n = count(i, FC, f) + 1
                    r = f % 2
                    dve.wait_ge(sine_done, n)
                    need(dve, h_ready, n - 2)
                    dve.scalar_tensor_tensor(out=mixed[:, r, :], in0=sine[:, r, :], scalar=small["coef"][:, f:f + 1], in1=pre[:, r, :],
                                             op0=ALU.mult, op1=ALU.add).then_inc(mixed_done, 1)

                def project_read(i):
                    dve.wait_ge(y_done, count(i, FC, FC))
                    need(dve, sum1_ready, i)
                    dve.tensor_tensor(res[:, :], p_y[:, :], block_cols(g.x1 if quantum else g.xo, i), ALU.add).then_inc(res_ready, 1)

                def norm1(i):
                    g.wait_apart(dve, total_ready, i + 1)
                    norm.dve_moments(dve, i, 0, total[:, :])

                def norm2(i):
                    if two_norms:
                        need(dve, n1g_ready, i)
                        norm.dve_scale(dve, i, 0, n1[:, :], total[:, :]).then_inc(n1_ready, 1)
                    else:
                        norm.dve_scale(dve, i, 0, block_cols(g.x1, i), total[:, :]).then_inc(out_ready, 1)

                def norm3(i):
                    if two_norms:
                        g.wait_apart(dve, xc_ready, i + 1)
                        norm.dve_moments(dve, i, 1, block_cols(g.xc, i))
                        norm.dve_scale(dve, i, 1, block_cols(g.nx, i), block_cols(g.xc, i)).then_inc(out_ready, 1)

                def body(i, first, last):
                    for f in range(FC):
                        if quantum:
                            reduce_range(i, f)
                            if not first or f >= 1:
                                mix(*back(i, f - 1, FC))
                        if not first:
                            if f == 1:
                                project_read(i - 1)
                            if f == 2:
                                norm1(i - 1)
                            if f == 3:
                                norm2(i - 1)
                                norm3(i - 1)
                over_blocks(dve, body)
                if quantum:
                    mix(NBK - 1, FC - 1)
                project_read(NBK - 1)
                norm1(NBK - 1)
                norm2(NBK - 1)
                norm3(NBK - 1)
                dve.wait_ge(out_ready, NBK)

            @block.tensor
            def _(pe):
                pe.wait_ge(W.loaded, W.total)
                pe.wait_ge(g.setup_done, 1)

                def transpose_in(i):
                    pe.wait_ge(x_ready, i + 1)
                    need(pe, T_ready, i)
                    for k in range(BB):
                        ins = pe.transpose(p_t[:, k * S:(k + 1) * S], x_in[:, k * DM:(k + 1) * DM], g.ident[:, :])
                    ins.then_inc(T_done, 1)

                def expand(i, f):
                    n = count(i, FC, f)
                    if f == 0:
                        pe.wait_ge(T_ready, i + 1)
                    if quantum:
                        need(pe, arg_done, n - 1)
                    else:
                        need(pe, h_ready, n - 1)
                    pe.matmul(p_h[f % 2][:, :], W["w1"][:, f * 128:(f + 1) * 128], xT[:, :], start=True, stop=True).then_inc(h_done, 1)

                def project(i, f):
                    n = count(i, FC, f)
                    if f == 0:
                        need(pe, res_ready, i)
                    pe.wait_ge(h_ready, n + 1)
                    for k in range(BB):
                        ins = pe.matmul(p_y[:, k * DM:(k + 1) * DM], hidden[:, f, k * S:(k + 1) * S], W["w2"][:, f * DM:(f + 1) * DM],
                                        start=(f == 0 and k == 0), stop=(f == FC - 1), skip_group_check=True)
                    ins.then_inc(y_done, 1)

                transpose_in(0)

                def body(i, first, last):
                    for f in range(FC):
                        expand(i, f)
                        if f == 2 and not last:
                            transpose_in(i + 1)
                        if not first or f >= 2:
                            project(*back(i, f - 2, FC))
                over_blocks(pe, body)
                project(NBK - 1, FC - 2)
                project(NBK - 1, FC - 1)


def cross_mlp1(g):
    mlp(g, "c_")


def cross_mlp2(g):
    mlp(g, "e_")


def quantum_mlp(g):
    mlp(g, "i_")


NE = 8


def declare_experts(g, ctx):
    t = g.t
    w = g.weights["f_"] = Weights(g, "f_", Area(g.sb("f_weights", [128, NE * 3 * 512 + NE], F32, ctx)))
    w.tile("gate", [128, NE], t["L0_ffn_gate_wT"], lambda x: x[:, :])
    w.tile("w1", [128, NE * 512], t["L0_ffn_w1T"], lambda x: x[:, :])
    w.tile("w3", [128, NE * 512], t["L0_ffn_w3T"], lambda x: x[:, :])
    w.tile("w2", [128, NE * 512], t["L0_ffn_w2T"].rearrange("(c p) n -> p c n", p=128), lambda x: x[:, :].rearrange("p (c n) -> p c n", n=DM))


def load_experts(g, ctx):
    declare_experts(g, ctx)
    with g.nc.Block() as block:
        @block.sync
        def _(sp):
            g.weights["f_"].issue(sp)


def load_layer1(g):
    declare_later_weights(g)
    with g.nc.Block() as block:
        @block.sync
        def _(sp):
            for name in ("g_", "h_", "i_"):
                g.weights[name].issue(sp)


def gate(g, xT_all, weight):
    nc = g.nc
    JITTER = 0.01
    W = g.weights["f_"]
    with ExitStack() as ctx:
        sb = lambda n, shape, dt=F32: g.sb("fg_" + n, shape, dt, ctx)
        x_in, xT = sb("x_in", [128, BB * DM]), sb("xT", [128, BB * S])
        three = [128, NB, NE]
        scores, top = sb("scores", three), sb("top", three)
        place = sb("place", three, mybir.dt.uint32)
        place_f, neg, size, expert = sb("place_f", three), sb("neg", three), sb("size", three), sb("expert", three)
        dist, far, keep, chosen, others, up, ex, masked = (sb(n, [128, 2, NB, NE]) for n in ("dist", "far", "keep", "chosen", "others", "up", "ex", "masked"))
        total, mult = sb("total", [128, 2, NB]), sb("mult", [128, 2, NB])
        parts = sb("parts", [128, 2, NB, NE])
        p_t, p_g = g.banks(["fg_pt", "fg_pg"], ctx)
        sem = lambda n: g.sem("fg_" + n)
        x_ready, T_done, T_ready, gate_done, scores_ready, expert_ready, top_done, place_done, step, ex_ready, weight_ready = (
            sem(n) for n in ("x_ready", "T_done", "T_ready", "gate_done", "scores_ready", "expert_ready", "top_done", "place_done", "step", "ex_ready", "weight_ready"))
        all_copied = sem("all_copied")
        with nc.Block() as block:
            @block.gpsimd
            def _(pool):
                pool.iota(expert[:, :, :], [[0, NB], [1, NE]], base=0, channel_multiplier=0, allow_small_or_imprecise_dtypes=True).then_inc(expert_ready, 1)
                with pool.Fori(0, NBK) as i:
                    g.wait_apart(pool, T_done, i)
                    pool.tensor_copy(x_in[:, :], block_cols(g.x1, i)).then_inc(x_ready, 1)

            @block.scalar
            def _(act):
                with act.Fori(0, NBK) as i:
                    act.wait_ge(T_done, i + 1)
                    act.wait_ge(gate_done, i)
                    act.wait_ge(all_copied, i)
                    act.activation(xT[:, :], p_t[:, :], ACT.Copy).then_inc(T_ready, 1)
                act.wait_ge(step, EXP_STEP)
                act.activation(ex[:, :, :, :], up[:, :, :, :], ACT.Exp, scale=-1.0).then_inc(ex_ready, 1)

            @block.tensor
            def _(pe):
                pe.wait_ge(W.loaded, W.total)
                pe.wait_ge(g.setup_done, 1)
                with pe.Fori(0, NBK) as i:
                    pe.wait_ge(x_ready, i + 1)
                    pe.wait_ge(T_ready, i)
                    for k in range(BB):
                        ins = pe.transpose(p_t[:, k * S:(k + 1) * S], x_in[:, k * DM:(k + 1) * DM], g.ident[:, :])
                    ins.then_inc(T_done, 1)
                    pe.wait_ge(T_ready, i + 1)
                    pe.wait_ge(scores_ready, i)
                    for k in range(BB):
                        ins = pe.matmul(p_g[:, k * NE:(k + 1) * NE], xT[:, k * S:(k + 1) * S], W["gate"][:, :], start=True, stop=True)
                    ins.then_inc(gate_done, 1)

            @block.vector
            def _(dve):
                with dve.Fori(0, NBK) as i:
                    g.wait_apart(dve, T_ready, i + 1)
                    dve.tensor_copy(block_cols(xT_all, i), xT[:, :]).then_inc(all_copied, 1)
                    g.wait_apart(dve, gate_done, i + 1)
                    dve.tensor_copy(cols(scores[:, :, :].rearrange("p b e -> p (b e)"), i, BB * NE), p_g[:, 0:BB * NE]).then_inc(scores_ready, 1)
                dve.wait_ge(all_copied, NBK)
                dve.wait_ge(scores_ready, NBK)
                for b in range(NB):
                    dve.max(top[:, b, :], scores[:, b, :]).then_inc(top_done, 1)
                dve.wait_ge(top_done, NB)
                for b in range(NB):
                    dve.max_index(place[:, b, :], top[:, b, :], scores[:, b, :]).then_inc(place_done, 1)
                dve.wait_ge(place_done, NB)
                dve.wait_ge(expert_ready, 1)
                bc = lambda tile, n: tile[:, :, n:n + 1].broadcast_to(three)
                steps = [0]

                def then(ins):
                    steps[0] += 1
                    ins.then_inc(step, 1)
                    dve.wait_ge(step, steps[0])

                then(dve.tensor_copy(place_f[:, :, :], place[:, :, :]))
                then(dve.tensor_scalar(neg[:, :, :], scores[:, :, :], -1.0, None, ALU.mult))
                then(dve.tensor_tensor(size[:, :, :], scores[:, :, :], neg[:, :, :], ALU.max))
                for n in (0, 1):
                    then(dve.tensor_tensor(chosen[:, n], expert[:, :, :], bc(place_f, n), ALU.is_equal))
                    then(dve.tensor_tensor(dist[:, n], bc(top, n), scores[:, :, :], ALU.subtract))
                    then(dve.tensor_tensor(far[:, n], size[:, :, :], bc(top, n), ALU.max))
                then(dve.scalar_tensor_tensor(out=keep[:, :, :, :].rearrange("p n b e -> p (n b e)"), in0=far[:, :, :, :].rearrange("p n b e -> p (n b e)"),
                                              scalar=2 * JITTER, in1=dist[:, :, :, :].rearrange("p n b e -> p (n b e)"), op0=ALU.mult, op1=ALU.is_ge))
                then(dve.tensor_scalar(others[:, 1], chosen[:, 0], -1.0, 1.0, ALU.mult, ALU.add))
                then(dve.tensor_copy(others[:, 0], keep[:, 0]))
                then(dve.tensor_tensor(masked[:, 1], keep[:, 1], others[:, 1], ALU.mult))
                then(dve.tensor_copy(masked[:, 0], others[:, 0]))
                then(dve.tensor_scalar(up[:, :, :, :], dist[:, :, :, :], 0.0, None, ALU.max))
                assert steps[0] == EXP_STEP
                dve.wait_ge(ex_ready, 1)
                then(dve.tensor_tensor(parts[:, :, :, :], masked[:, :, :, :], ex[:, :, :, :], ALU.mult))
                then(dve.tensor_reduce(total[:, :, :], parts[:, :, :, :], X_AXIS, ALU.add))
                then(dve.reciprocal(mult[:, :, :], total[:, :, :]))
                for n in (0, 1):
                    then(dve.tensor_tensor(dist[:, n], chosen[:, n], mult[:, n, :].rearrange("p (b a) -> p b a", a=1).broadcast_to(three), ALU.mult))
                dve.tensor_tensor(weight[:, :, :], dist[:, 0], dist[:, 1], ALU.add).then_inc(weight_ready, 1)
                dve.wait_ge(weight_ready, 1)


EXP_STEP = 15


def experts(g):
    nc = g.nc
    FC = 4
    NM = NE * FC
    W = g.weights["f_"]
    with ExitStack() as ctx:
        sb = lambda n, shape, dt=F32: g.sb("f_" + n, shape, dt, ctx)
        xT_all = g.xo
        weight = sb("weight", [128, NB, NE])
        gate(g, xT_all, weight)
        act_a, hidden = sb("act_a", [128, 2, BB * S]), sb("hidden", [128, FC, BB * S])
        w_now = sb("w_now", [128, 2, BB * NE])
        weighed, acc = sb("weighed", [128, 2, BB * DM]), sb("acc", [128, 2, BB * DM])
        total = sb("total", [128, BB * DM])
        a0, a1, b0, b1, y0, y1 = g.banks(["f_" + n for n in ("a0", "a1", "b0", "b1", "y0", "y1")], ctx)
        p_a, p_b, p_y = [a0, a1], [b0, b1], [y0, y1]
        norm = NormBlock(g, "f_ln", 1, ctx)
        sem = lambda n: g.sem("f_" + n)
        a_done, b_done, silu_ready, h_ready, y_done, weighed_ready, acc_ready, total_ready, out_ready, acc_zero = (
            sem(n) for n in ("a_done", "b_done", "silu_ready", "h_ready", "y_done", "weighed_ready", "acc_ready", "total_ready", "out_ready", "acc_zero"))
        w_ready = sem("w_ready")

        with nc.Block() as block:
            @block.gpsimd
            def _(pool):
                def weights_of(i):
                    g.wait_apart(pool, weighed_ready, count(i, NE, 0) if not isinstance(i, int) else i * NE)
                    pool.tensor_copy(w_now[:, 0, :], cols(weight[:, :, :].rearrange("p b e -> p (b e)"), i, BB * NE)).then_inc(w_ready, 1)

                def body(i, first, last):
                    weights_of(i)
                    for e in range(NE):
                        n = count(i, NE, e)
                        if e == 0:
                            if not first:
                                pool.wait_ge(total_ready, i)
                            g.wait_apart(pool, weighed_ready, n + 1)
                            pool.tensor_tensor(acc[:, 0, :], weighed[:, 0, :], block_cols(g.x1, i), ALU.add).then_inc(acc_ready, 1)
                            if not first:
                                norm.pool_rstd(pool, i - 1, 0)
                        else:
                            pool.wait_ge(weighed_ready, n + 1)
                            pool.wait_ge(acc_ready, n)
                            pool.tensor_tensor(acc[:, e % 2, :], weighed[:, e % 2, :], acc[:, 1 - e % 2, :], ALU.add).then_inc(acc_ready, 1)
                over_blocks(pool, body)
                norm.pool_rstd(pool, NBK - 1, 0)

            @block.scalar
            def _(act):
                def body(i, first, last):
                    for m in range(NM):
                        n = count(i, NM, m)
                        act.wait_ge(a_done, n + 1)
                        need(act, h_ready, n - 1)
                        act.activation(act_a[:, m % 2, :], p_a[m % 2][:, :], ACT.Silu).then_inc(silu_ready, 1)
                over_blocks(act, body)

            @block.vector
            def _(dve):
                def weigh(i, e):
                    n = count(i, NE, e)
                    if e == 0:
                        dve.wait_ge(w_ready, i + 1)
                    dve.wait_ge(y_done, count(i, NM, FC * (e + 1)))
                    need(dve, acc_ready, n - 1)
                    dve.tensor_tensor(weighed[:, e % 2, :].rearrange("p (k n) -> p k n", n=DM), p_y[e % 2][:, :].rearrange("p (k n) -> p k n", n=DM),
                                      w_now[:, 0, e:BB * NE:NE].rearrange("p (k a) -> p k a", a=1).broadcast_to([128, BB, DM]), ALU.mult).then_inc(weighed_ready, 1)

                def finish(i, part):
                    if part == 0:
                        dve.wait_ge(acc_ready, count(i, NE, NE))
                        need(dve, out_ready, i)
                        dve.tensor_copy(total[:, :], acc[:, (NE - 1) % 2, :]).then_inc(total_ready, 1)
                        g.wait_apart(dve, total_ready, i + 1)
                        norm.dve_moments(dve, i, 0, total[:, :])
                    else:
                        norm.dve_scale(dve, i, 0, block_cols(g.x1, i), total[:, :]).then_inc(out_ready, 1)

                def body(i, first, last):
                    for m in range(NM):
                        n = count(i, NM, m)
                        dve.wait_ge(silu_ready, n + 1)
                        dve.wait_ge(b_done, n + 1)
                        need(dve, y_done, n - 3)
                        dve.tensor_tensor(hidden[:, m % FC, :], act_a[:, m % 2, :], p_b[m % 2][:, :], ALU.mult).then_inc(h_ready, 1)
                        if m % FC == 2 and (m >= FC or not first):
                            weigh(*back(i, m // FC - 1, NE))
                        if m == 6 and not first:
                            finish(i - 1, 0)
                        if m == 10 and not first:
                            finish(i - 1, 1)
                over_blocks(dve, body)
                weigh(NBK - 1, NE - 1)
                finish(NBK - 1, 0)
                finish(NBK - 1, 1)
                dve.wait_ge(out_ready, NBK)

            @block.tensor
            def _(pe):
                def expand(i, m):
                    n = count(i, NM, m)
                    xT = block_cols(xT_all, i)
                    for w, bank, free, done in (("w1", p_a, silu_ready, a_done), ("w3", p_b, h_ready, b_done)):
                        need(pe, free, n - 1)
                        pe.matmul(bank[m % 2][:, :], W[w][:, m * 128:(m + 1) * 128], xT, start=True, stop=True).then_inc(done, 1)

                def project(i, m):
                    n = count(i, NM, m)
                    e, f = m // FC, m % FC
                    if f == 0:
                        need(pe, weighed_ready, count(i, NE, e - 1))
                    pe.wait_ge(h_ready, n + 1)
                    for k in range(BB):
                        ins = pe.matmul(p_y[e % 2][:, k * DM:(k + 1) * DM], hidden[:, f, k * S:(k + 1) * S], W["w2"][:, m * DM:(m + 1) * DM],
                                        start=(f == 0 and k == 0), stop=(f == FC - 1), skip_group_check=True)
                    ins.then_inc(y_done, 1)

                def body(i, first, last):
                    for m in range(NM):
                        expand(i, m)
                        if not first or m >= 2:
                            project(*back(i, m - 2, NM))
                over_blocks(pe, body)
                project(NBK - 1, NM - 2)
                project(NBK - 1, NM - 1)


RH, RD, RT = 16, 8, NB
SG = 4
RMAX = 16


def relative_attention(g):
    nc = g.nc
    by_place = nc.dram_tensor("distance_scores", [S, RT, RH * RT], F32, kind="Internal").ap()
    probs_dram = nc.dram_tensor("distance_probs", [S, RT, RH * RT], F32, kind="Internal").ap()
    distance_scores(g, g.xo, by_place)
    group_attention(g, g.xo, g.xc, by_place, probs_dram)
    distance_values(g, g.xc, probs_dram)


def distance_scores(g, xT_all, scores_dram):
    nc = g.nc
    W = g.weights["g_"]
    SCALE = RD ** -0.5
    with ExitStack() as ctx:
        sb = lambda n, shape, dt=F32: g.sb("g1_" + n, shape, dt, ctx)
        x_in, xT, qT = sb("x_in", [128, BB * DM]), sb("xT", [128, BB * S]), sb("qT", [128, BB * S])
        out = sb("out", [128, BB, RH * RT])
        p_t, p_q, *p_d = g.banks(["g1_pt", "g1_pq", "g1_d0", "g1_d1", "g1_d2", "g1_d3"], ctx)
        sem = lambda n: g.sem("g1_" + n)
        x_ready, T_done, T_ready, copied, q_done, q_ready, d_done, d_ready = (
            sem(n) for n in ("x_ready", "T_done", "T_ready", "copied", "q_done", "q_ready", "d_done", "d_ready"))
        stored = [sem(f"stored{k}") for k in range(BB)]
        with nc.Block() as block:
            @block.sync
            def _(sp):
                with sp.Fori(0, NBK) as i:
                    for k in range(BB):
                        sp.wait_ge(d_ready, i * BB + k + 1)
                        sp.dma_start(scores_dram[:, bass.ds(i * BB + k, 1), :].rearrange("s a n -> s (a n)"), out[:, k, :]).then_inc(stored[k], 16)
                for k in range(BB):
                    sp.wait_ge(stored[k], 16 * NBK)

            @block.gpsimd
            def _(pool):
                with pool.Fori(0, NBK) as i:
                    g.wait_apart(pool, T_done, i)
                    pool.tensor_copy(x_in[:, :], block_cols(g.x1, i)).then_inc(x_ready, 1)

            @block.scalar
            def _(act):
                with act.Fori(0, NBK) as i:
                    act.wait_ge(T_done, i + 1)
                    act.wait_ge(q_done, i)
                    act.wait_ge(copied, i)
                    act.activation(xT[:, :], p_t[:, :], ACT.Copy).then_inc(T_ready, 1)
                    for k in range(BB):
                        act.wait_ge(d_done, i * BB + k + 1)
                        act.wait_ge(stored[k], i * 16)
                        act.activation(out[:, k, :], p_d[k][:, :], ACT.Copy).then_inc(d_ready, 1)

            @block.vector
            def _(dve):
                dve.wait_ge(W.loaded, W.total)
                with dve.Fori(0, NBK) as i:
                    dve.wait_ge(q_done, i + 1)
                    dve.wait_ge(d_done, i * BB)
                    dve.tensor_scalar(qT[:, :], p_q[:, :], W["bq"][:, 0:1], SCALE, ALU.add, ALU.mult).then_inc(q_ready, 1)
                    g.wait_apart(dve, T_ready, i + 1)
                    dve.tensor_copy(block_cols(xT_all, i), xT[:, :]).then_inc(copied, 1)
                dve.wait_ge(copied, NBK)

            @block.tensor
            def _(pe):
                pe.wait_ge(W.loaded, W.total)
                pe.wait_ge(g.setup_done, 1)
                keys = W["keys"][:, :].rearrange("p (h u) -> p h u", u=2 * RT - 1)
                with pe.Fori(0, NBK) as i:
                    pe.wait_ge(x_ready, i + 1)
                    pe.wait_ge(T_ready, i)
                    for k in range(BB):
                        ins = pe.transpose(p_t[:, k * S:(k + 1) * S], x_in[:, k * DM:(k + 1) * DM], g.ident[:, :])
                    ins.then_inc(T_done, 1)
                    pe.wait_ge(T_ready, i + 1)
                    pe.wait_ge(q_ready, i)
                    pe.matmul(p_q[:, :], W["wq"][:, :], xT[:, :], start=True, stop=True).then_inc(q_done, 1)
                    pe.wait_ge(q_ready, i + 1)
                    for k in range(BB):
                        pe.wait_ge(d_ready, i * BB)
                        pe.matmul(p_d[k][:, :].rearrange("p (h u) -> p h u", u=RT), qT[:, k * S:(k + 1) * S],
                                  keys[:, :, bass.ds(i * (-BB) + (RT - 1 - k), RT)], start=True, stop=True).then_inc(d_done, 1)


def group_attention(g, xT_all, oT_all, scores_dram, probs_dram):
    nc = g.nc
    W = g.weights["g_"]
    with ExitStack() as ctx:
        sb = lambda n, shape, dt=F32: g.sb("g2_" + n, shape, dt, ctx)
        xT, xT_rep = sb("xT", [128, 2, S]), sb("xT_rep", [128, 2, 4 * S])
        q_own, k_all = sb("q_own", [128, 2, 4 * S]), sb("k_all", [128, 4 * S])
        k_sum, k_own = sb("k_sum", [128, 4 * RT]), sb("k_own", [128, 2, 4 * S])
        v_own = sb("v_own", [128, 2, 4 * S])
        near = sb("near", [128, 2, BANK])
        scores, moved, ex, probs = (sb(n, [128, 2, BANK]) for n in ("scores", "moved", "ex", "probs"))
        top, total, inv = (sb(n, [128, 2, RH]) for n in ("top", "total", "inv"))
        probsT, o_all, o = sb("probsT", [128, 4 * S]), sb("o_all", [128, 4 * S]), sb("o", [128, 2, S])
        p_q, p_k, p_v, p_s, p_t, p_o, p_oT = g.banks(["g2_" + n for n in ("pq", "pk", "pv", "ps", "pt", "po", "poT")], ctx)
        sem = lambda n: g.sem("g2_" + n)
        xT_ready, xT_repeated, q_done, q_ready, k_done, k_masked, k_summed, k_ready, v_done, v_ready = (
            sem(n) for n in ("xT_ready", "xT_repeated", "q_done", "q_ready", "k_done", "k_masked", "k_summed", "k_ready", "v_done", "v_ready"))
        s_done, s_ready, top_ready, moved_ready, ex_ready, total_ready, inv_ready, probs_ready = (
            sem(n) for n in ("s_done", "s_ready", "top_ready", "moved_ready", "ex_ready", "total_ready", "inv_ready", "probs_ready"))
        t_done, t_ready, o_done, o_masked, o_ready, oT_done, oT_ready = (
            sem(n) for n in ("t_done", "t_ready", "o_done", "o_masked", "o_ready", "oT_done", "oT_ready"))
        near_loaded = [sem(f"near_loaded{k}") for k in (0, 1)]
        stored = [sem(f"stored{k}") for k in (0, 1)]
        tokens = lambda tile: tile[:, :].rearrange("p (t s) -> p s t", s=S)

        def of_group(tile, j):
            return tokens(tile)[:, j * SG:(j + 1) * SG, :] if isinstance(j, int) else tokens(tile)[:, bass.ds(j * SG, SG), :]

        def rows(dram, j):
            part = dram[j * SG:(j + 1) * SG] if isinstance(j, int) else dram[bass.ds(j * SG, SG)]
            return part.rearrange("s t n -> (s t) n")

        with nc.Block() as block:
            @block.sync
            def _(sp):
                def store(j, par):
                    sp.wait_ge(probs_ready, j + 1)
                    sp.dma_start(rows(probs_dram, j), probs[:, par, :]).then_inc(stored[par], 16)

                for j in (0, 1):
                    sp.dma_start(near[:, j, :], rows(scores_dram, j)).then_inc(near_loaded[j], 16)
                with sp.Fori(0, NB // 2 - 1) as i:
                    for par in (0, 1):
                        store(i * 2 + par, par)
                        sp.wait_ge(s_ready, i * 2 + par + 1)
                        sp.dma_start(near[:, par, :], rows(scores_dram, i * 2 + par + 2)).then_inc(near_loaded[par], 16)
                for j in (NB - 2, NB - 1):
                    store(j, j % 2)
                for par in (0, 1):
                    sp.wait_ge(stored[par], 16 * NB // 2)

            @block.gpsimd
            def _(pool):
                def copy_in(j, par):
                    need(pool, v_done, j - 1)
                    pool.sem_inc(g.waits_passed[pool.engine], 1)
                    pool.tensor_copy(xT[:, par, :].rearrange("p (s t) -> p s t", s=SG), of_group(xT_all, j)).then_inc(xT_ready, 1)

                def repeat(j, par):
                    g.wait_apart(pool, xT_ready, j + 1)
                    pool.tensor_copy(xT_rep[:, par, :].rearrange("p (s i t) -> p s i t", s=SG, i=4),
                                     xT[:, par, :].rearrange("p (s i t) -> p s i t", s=SG, i=1).broadcast_to([128, SG, 4, RT])).then_inc(xT_repeated, 1)

                def move(j, par):
                    pool.wait_ge(top_ready, j + 1)
                    need(pool, ex_ready, j - 1)
                    pool.tensor_tensor(heads(moved[:, par, :]), heads(scores[:, par, :]), per_head(top[:, par, :]), ALU.subtract).then_inc(moved_ready, 1)

                def divide(j, par, k):
                    pool.wait_ge(inv_ready, j + 1)
                    need(pool, t_done, j - 1)
                    need(pool, stored[par], k)
                    pool.tensor_tensor(heads(probs[:, par, :]), heads(ex[:, par, :]), per_head(inv[:, par, :]), ALU.mult).then_inc(probs_ready, 1)

                copy_in(0, 0)
                repeat(0, 0)
                copy_in(1, 1)
                repeat(1, 1)

                def body(j, par, first, last):
                    move(j, par)
                    if not late(j):
                        copy_in(j + 2, par)
                        repeat(j + 2, par)
                    divide(j, par, stored_before(j, par))
                over_pairs(pool, body)

            @block.scalar
            def _(act):
                act.wait_ge(W.loaded, W.total)

                def exp(j, par):
                    act.wait_ge(moved_ready, j + 1)
                    need(act, probs_ready, j - 1)
                    act.activation(ex[:, par, :], moved[:, par, :], ACT.Exp).then_inc(ex_ready, 1)

                def probsT_copy(j):
                    act.wait_ge(t_done, j + 1)
                    need(act, o_done, j)
                    act.activation(probsT[:, :], p_t[:, :], ACT.Copy).then_inc(t_ready, 1)

                def oT_copy(j):
                    act.wait_ge(oT_done, j + 1)
                    act.activation(of_group(oT_all, j), p_oT[:, 0:S].rearrange("p (s t) -> p s t", s=SG), ACT.Identity, bias=W["bv"][:, 0:1]).then_inc(oT_ready, 1)

                def body(j, par, first, last):
                    if not first:
                        probsT_copy(j - 1)
                    if not early(j):
                        oT_copy(j - 2)
                    exp(j, par)
                over_pairs(act, body)
                probsT_copy(NB - 1)
                oT_copy(NB - 2)
                oT_copy(NB - 1)
                act.wait_ge(oT_ready, NB)

            @block.vector
            def _(dve):
                dve.wait_ge(W.loaded, W.total)

                def q_copy(j, par):
                    dve.wait_ge(q_done, j + 1)
                    need(dve, s_done, j - 1)
                    for c in range(4):
                        ins = dve.scalar_tensor_tensor(out=q_own[:, par, c * S:(c + 1) * S], in0=p_q[:, c * S:(c + 1) * S], scalar=W["bq_rep"][:, c:c + 1],
                                                       in1=W["own_scaled"][:, :], op0=ALU.add, op1=ALU.mult)
                    ins.then_inc(q_ready, 1)

                def k_copy(j, par):
                    dve.wait_ge(k_done, j + 1)
                    need(dve, k_summed, j)
                    for c in range(4):
                        ins = dve.scalar_tensor_tensor(out=k_all[:, c * S:(c + 1) * S], in0=p_k[:, c * S:(c + 1) * S], scalar=W["bk_rep"][:, c:c + 1],
                                                       in1=W["own"][:, :], op0=ALU.add, op1=ALU.mult)
                    ins.then_inc(k_masked, 1)
                    dve.wait_ge(k_masked, j + 1)
                    dve.tensor_reduce(k_sum[:, :].rearrange("p (c t) -> p c t", t=RT), k_all[:, :].rearrange("p (c s t) -> p c t s", c=4, s=SG), X_AXIS, ALU.add).then_inc(k_summed, 1)
                    dve.wait_ge(k_summed, j + 1)
                    need(dve, s_done, j - 1)
                    for i in range(4):
                        ins = dve.tensor_scalar(k_own[:, par, :].rearrange("p (c i t) -> p i c t", c=4, i=4)[:, i], k_sum[:, :].rearrange("p (c t) -> p c t", t=RT),
                                                W["row_head"][:, i:i + 1], None, ALU.mult)
                    ins.then_inc(k_ready, 1)

                def v_copy(j, par):
                    dve.wait_ge(v_done, j + 1)
                    need(dve, o_done, j - 1)
                    dve.tensor_tensor(v_own[:, par, :].rearrange("p (a i d) -> p a i d", i=4, d=RD), p_v[:, :].rearrange("p (a i d) -> p a i d", i=4, d=RD),
                                      W["row_head"][:, :].rearrange("p (a i b) -> p a i b", a=1, b=1).broadcast_to([128, 4 * 4, 4, RD]), ALU.mult).then_inc(v_ready, 1)

                def add_near(j, par, k):
                    dve.wait_ge(s_done, j + 1)
                    need(dve, moved_ready, j - 1)
                    dve.wait_ge(near_loaded[par], k + 16)
                    dve.tensor_tensor(scores[:, par, :], p_s[:, :], near[:, par, :], ALU.add).then_inc(s_ready, 1)
                    dve.wait_ge(s_ready, j + 1)
                    dve.tensor_reduce(top[:, par, :], heads(scores[:, par, :]), X_AXIS, ALU.max).then_inc(top_ready, 1)

                def sum_up(j, par):
                    dve.wait_ge(ex_ready, j + 1)
                    dve.tensor_reduce(total[:, par, :], heads(ex[:, par, :]), X_AXIS, ALU.add).then_inc(total_ready, 1)
                    dve.wait_ge(total_ready, j + 1)
                    need(dve, probs_ready, j - 1)
                    dve.reciprocal(inv[:, par, :], total[:, par, :]).then_inc(inv_ready, 1)

                def o_copy(j, par):
                    dve.wait_ge(o_done, j + 1)
                    for c in range(4):
                        ins = dve.tensor_tensor(o_all[:, c * S:(c + 1) * S].rearrange("p (s n) -> p s n", s=SG), p_o[:, c * S:(c + 1) * S].rearrange("p (s n) -> p s n", s=SG),
                                                W["row_position"][:, :].rearrange("p (s a) -> p s a", a=1).broadcast_to([128, SG, 4 * RD]), ALU.mult)
                    ins.then_inc(o_masked, 1)
                    dve.wait_ge(o_masked, j + 1)
                    need(dve, oT_done, j - 1)
                    dve.tensor_reduce(o[:, par, :].rearrange("p (c n) -> p c n", c=4), o_all[:, :].rearrange("p (c s n) -> p c n s", c=4, s=SG), X_AXIS, ALU.add).then_inc(o_ready, 1)

                q_copy(0, 0)
                k_copy(0, 0)
                v_copy(0, 0)

                def body(j, par, first, last):
                    add_near(j, par, stored_before(j, par))
                    if not last:
                        q_copy(j + 1, 1 - par)
                        k_copy(j + 1, 1 - par)
                    sum_up(j, par)
                    if not last:
                        v_copy(j + 1, 1 - par)
                    if not first:
                        o_copy(j - 1, 1 - par)
                over_pairs(dve, body)
                o_copy(NB - 1, 1)

            @block.tensor
            def _(pe):
                pe.wait_ge(W.loaded, W.total)

                def project(j, par):
                    pe.wait_ge(xT_ready, j + 1)
                    for bank, w, free, done in ((p_q, "wq_rep", q_ready, q_done), (p_k, "wk_rep", k_masked, k_done)):
                        need(pe, free, j)
                        for c in range(4):
                            ins = pe.matmul(bank[:, c * S:(c + 1) * S], W[w][:, c * 128:(c + 1) * 128], xT[:, par, :], start=True, stop=True)
                        ins.then_inc(done, 1)

                def project_v(j, par):
                    pe.wait_ge(xT_repeated, j + 1)
                    need(pe, v_ready, j)
                    for s in range(SG):
                        ins = pe.matmul(p_v[:, s * S:(s + 1) * S], xT_rep[:, par, s * S:(s + 1) * S], W["wv"][:, :], start=True, stop=True)
                    ins.then_inc(v_done, 1)

                def score(j, par):
                    pe.wait_ge(q_ready, j + 1)
                    pe.wait_ge(k_ready, j + 1)
                    need(pe, s_ready, j)
                    for c in range(4):
                        ins = pe.matmul(p_s[:, c * S:(c + 1) * S], q_own[:, par, c * S:(c + 1) * S], k_own[:, par, c * S:(c + 1) * S], start=True, stop=True)
                    ins.then_inc(s_done, 1)

                def transpose_probs(j, par):
                    pe.wait_ge(probs_ready, j + 1)
                    need(pe, t_ready, j)
                    for c in range(4):
                        ins = pe.transpose(p_t[:, c * S:(c + 1) * S], probs[:, par, c * S:(c + 1) * S], g.ident[:, :])
                    ins.then_inc(t_done, 1)

                def weigh(j, par):
                    pe.wait_ge(t_ready, j + 1)
                    pe.wait_ge(v_ready, j + 1)
                    need(pe, o_masked, j)
                    for c in range(4):
                        v = v_own[:, par, :].rearrange("p (s c n) -> p c s n", s=SG, c=4)[:, c]
                        ins = pe.matmul(p_o[:, c * S:(c + 1) * S].rearrange("p (s n) -> p s n", s=SG), probsT[:, c * S:(c + 1) * S], v, start=True, stop=True)
                    ins.then_inc(o_done, 1)

                def transpose_o(j, par):
                    pe.wait_ge(o_ready, j + 1)
                    need(pe, oT_ready, j)
                    pe.transpose(p_oT[:, 0:S], o[:, par, :], g.ident[:, :]).then_inc(oT_done, 1)

                project(0, 0)
                project_v(0, 0)

                def body(j, par, first, last):
                    score(j, par)
                    if not last:
                        project(j + 1, 1 - par)
                    if not first:
                        transpose_probs(j - 1, 1 - par)
                    if not last:
                        project_v(j + 1, 1 - par)
                    if not early(j):
                        transpose_o(j - 2, par)
                    if not first:
                        weigh(j - 1, 1 - par)
                over_pairs(pe, body)
                transpose_probs(NB - 1, 1)
                transpose_o(NB - 2, 0)
                weigh(NB - 1, 1)
                transpose_o(NB - 1, 1)


def heads(tile):
    return tile.rearrange("p (h t) -> p h t", t=RT)


def per_head(tile):
    return tile.rearrange("p (h a) -> p h a", a=1).broadcast_to([128, RH, RT])


def stored_before(j, par):
    return (j - par) // 2 * 16 if isinstance(j, int) else j * 8 - 8 * par


def distance_values(g, oT_all, probs_dram):
    nc = g.nc
    W = g.weights["g_"]
    with ExitStack() as ctx:
        sb = lambda n, shape, dt=F32: g.sb("g3_" + n, shape, dt, ctx)
        probs, probsT = sb("probs", [128, 2, BANK]), sb("probsT", [128, 2, BANK])
        values, oT = sb("values", [128, 2, 4 * RD]), sb("oT", [128, 2, S])
        res, res2 = sb("res", [128, DM]), sb("res2", [128, DM])
        t0, t1, p_o, p_y = g.banks(["g3_" + n for n in ("t0", "t1", "po", "py")], ctx)
        p_t = [t0, t1]
        norm = Norm(g, "g3_ln", 1, ctx)
        sem = lambda n: g.sem("g3_" + n)
        loaded = [sem(f"loaded{k}") for k in (0, 1)]
        values_ready, t_done, t_ready, o_done, oT_ready, y_done, res_ready, res2_ready, out_ready = (
            sem(n) for n in ("values_ready", "t_done", "t_ready", "o_done", "oT_ready", "y_done", "res_ready", "res2_ready", "out_ready"))

        def place(dram, t):
            return dram[:, t, :] if isinstance(t, int) else dram[:, bass.ds(t, 1), :].rearrange("s a n -> s (a n)")

        with nc.Block() as block:
            @block.sync
            def _(sp):
                for t in (0, 1):
                    sp.dma_start(probs[:, t, :], place(probs_dram, t)).then_inc(loaded[t], 16)
                with sp.Fori(1, NB // 2) as i:
                    for par in (0, 1):
                        sp.wait_ge(t_done, i * 2 + par - 1)
                        sp.dma_start(probs[:, par, :], place(probs_dram, i * 2 + par)).then_inc(loaded[par], 16)

            @block.gpsimd
            def _(pool):
                def copy_values(t, par):
                    g.wait_apart(pool, o_done, t - 1)
                    pool.tensor_copy(values[:, par, :], cols(W["values"], t, 4 * RD)).then_inc(values_ready, 1)

                def finish(t):
                    pool.wait_ge(res_ready, t + 1)
                    need(pool, out_ready, t)
                    pool.tensor_tensor(res2[:, :], res[:, :], W["bo"][:, :], ALU.add).then_inc(res2_ready, 1)
                    norm.pool_rstd(pool, t, 0)

                copy_values(0, 0)
                copy_values(1, 1)

                def body(t, par, first, last):
                    if not late(t):
                        copy_values(t + 2, par)
                    if not early(t):
                        finish(t - 2)
                over_pairs(pool, body)
                finish(NB - 2)
                finish(NB - 1)

            @block.scalar
            def _(act):
                def body(t, par, first, last):
                    act.wait_ge(t_done, t + 1)
                    need(act, o_done, t - 1)
                    act.activation(probsT[:, par, :], p_t[par][:, :], ACT.Copy).then_inc(t_ready, 1)
                over_pairs(act, body)

            @block.vector
            def _(dve):
                def add_o(t, par):
                    dve.wait_ge(o_done, t + 1)
                    need(dve, y_done, t - 1)
                    dve.tensor_tensor(oT[:, par, :], p_o[:, 0:S], cols(oT_all, t, S), ALU.add).then_inc(oT_ready, 1)

                def add_x(t):
                    dve.wait_ge(y_done, t + 1)
                    need(dve, res2_ready, t)
                    dve.tensor_tensor(res[:, :], p_y[:, 0:DM], cols(g.x1, t, DM), ALU.add).then_inc(res_ready, 1)

                def finish(t):
                    g.wait_apart(dve, res2_ready, t + 1)
                    norm.dve_moments(dve, t, 0, res2[:, :])
                    norm.dve_scale(dve, t, 0, cols(g.x1, t, DM), res2[:, :]).then_inc(out_ready, 1)

                def body(t, par, first, last):
                    if not first:
                        add_o(t - 1, 1 - par)
                    if not early(t):
                        add_x(t - 2)
                        finish(t - 2)
                over_pairs(dve, body)
                add_o(NB - 1, 1)
                for t in (NB - 2, NB - 1):
                    add_x(t)
                    finish(t)
                dve.wait_ge(out_ready, NB)

            @block.tensor
            def _(pe):
                def transpose(t, par, k):
                    pe.wait_ge(loaded[par], k + 16)
                    need(pe, t_ready, t - 1)
                    for c in range(4):
                        ins = pe.transpose(p_t[par][:, c * S:(c + 1) * S], probs[:, par, c * S:(c + 1) * S], g.ident[:, :])
                    ins.then_inc(t_done, 1)

                def weigh(t, par):
                    pe.wait_ge(t_ready, t + 1)
                    pe.wait_ge(values_ready, t + 1)
                    need(pe, oT_ready, t)
                    for c in range(4):
                        ins = pe.matmul(p_o[32 * c:32 * c + 32, 0:S], values[:, par, :], probsT[:, par, c * S:(c + 1) * S], start=True, stop=True)
                    ins.then_inc(o_done, 1)

                def project(t, par):
                    pe.wait_ge(oT_ready, t + 1)
                    need(pe, res_ready, t)
                    pe.matmul(p_y[:, 0:DM], oT[:, par, :], W["wo"][:, :], start=True, stop=True).then_inc(y_done, 1)

                def body(t, par, first, last):
                    transpose(t, par, stored_before(t, par))
                    if not first:
                        weigh(t - 1, 1 - par)
                    if not early(t):
                        project(t - 2, par)
                over_pairs(pe, body)
                weigh(NB - 1, 1)
                project(NB - 2, 0)
                project(NB - 1, 1)


def cross_self(g):
    attention16(g, Heads16("b_", 32 ** -0.5, DM, own_keys=True, affine=True, bias=False, later_mask=True))


def cross_context(g):
    attention16(g, Heads16("d_", 32 ** -0.5, DC, own_keys=False, affine=True, bias=False, later_mask=False))


def context_attention(g):
    attention16(g, Heads16("h_", 8 ** -0.5, DC, own_keys=False, affine=False, bias=True, later_mask=False))


def program(nc, t, out):
    with ExitStack() as ctx:
        g = Globals(nc, t, ctx)
        declare_weights(g)
        setup(g)
        g.run_phase(self_attention)
        with ExitStack() as experts_ctx:
            load_experts(g, experts_ctx)
            for phase in (cross_self, cross_mlp1, cross_context, cross_mlp2):
                g.run_phase(phase)
            load_layer1(g)
            g.run_phase(experts)
        for phase in (relative_attention, context_attention, quantum_mlp):
            g.run_phase(phase)
        stored = g.sem("out_stored")
        with nc.Block() as block:
            @block.sync
            def _(sp):
                sp.dma_start(out.rearrange("b s n -> s b n"), g.x1[:, :].rearrange("s (b n) -> s b n", b=NB)).then_inc(stored, 16)
                sp.wait_ge(stored, 16)


def lay_out(a):
    import numpy as np
    c = np.ascontiguousarray
    t = {}
    for name in ("x", "ctx_512"):
        t[name] = c(a[name])
    wk = a["L0_attn_Wk"].T.reshape(128, 8, 1, 64)
    t["L0_attn_Wk2T"] = c(np.concatenate([wk, wk], axis=2).reshape(128, 1024))
    bk = a["L0_attn_bk"].reshape(8, 64).T
    t["L0_attn_bk2"] = c(np.concatenate([bk, bk], axis=0))
    t["L0_attn_WqT"] = c(a["L0_attn_Wq"].T)
    t["L0_attn_bqT"] = c(a["L0_attn_bq"].reshape(32, 128).T)
    t["L0_attn_WvT"] = c(a["L0_attn_Wv"].T)
    t["L0_attn_WoT"] = c(a["L0_attn_Wo"].T)
    for name in ("L0_attn_bv", "L0_attn_bo", "L0_attn_sinks", "L0_xattn_ln1_g", "L0_xattn_ln1_b"):
        t[name] = c(a[name])
    for a1 in ("L0_xattn_a1_", "L0_xattn_a2_"):
        for name in ("wq", "wk", "wv"):
            w = a[a1 + name]
            t[a1 + name] = c(w.transpose(1, 0, 2).reshape(w.shape[1], -1))
        for name in ("li1_w", "li1_b", "lnx_g", "lnx_b", "lny_g", "lny_b", "ln3_g", "ln3_b", "li2_w", "li3_w", "li3_b"):
            t[a1 + name] = c(a[a1 + name])
        t[a1 + "li2_bT"] = c(a[a1 + "li2_b"].reshape(4, 128).T)
    for name in ("b1", "quantum_phases", "quantum_weights_real", "quantum_weights_imag"):
        t[f"L1_ffn_{name}T"] = c(a[f"L1_ffn_{name}"].reshape(4, 128).T)
    for name in ("L1_ffn_W1", "L1_ffn_W2", "L1_ffn_b2", "L0_xattn_ln2_g", "L0_xattn_ln2_b"):
        t[name] = c(a[name])

    t["L0_ffn_gate_wT"] = c(a["L0_ffn_gate_w"].T)
    for name in ("w1", "w3"):
        t[f"L0_ffn_{name}T"] = c(a[f"L0_ffn_{name}"].reshape(-1, 128).T)
    t["L0_ffn_w2T"] = c(a["L0_ffn_w2"].transpose(0, 2, 1).reshape(-1, 128))

    def slots(w):
        out = np.zeros(w.shape[:-1] + (16, 32), w.dtype)
        out[..., :8] = w.reshape(w.shape[:-1] + (16, 8))
        return out.reshape(w.shape[:-1] + (512,))
    d = "L1_attn_"
    wq, wk, wv = (a[d + "in_proj_weight"][n * 128:(n + 1) * 128].T for n in range(3))
    bq, bk, bv = (a[d + "in_proj_bias"][n * 128:(n + 1) * 128] for n in range(3))

    def repeat(w):
        w = w.reshape(w.shape[:-1] + (4, 4, 1, 8))
        return np.concatenate([w] * 4, axis=-2).reshape(w.shape[:-4] + (512,))
    t[d + "wq"], t[d + "wv"], t[d + "wo"] = c(wq), c(wv), c(a[d + "out_w"].T)
    t[d + "bq"], t[d + "bv"] = c(bq.reshape(128, 1)), c(bv.reshape(128, 1))
    t[d + "wq_rep"], t[d + "wk_rep"] = c(repeat(wq)), c(repeat(wk))
    t[d + "bq_rep"], t[d + "bk_rep"] = c(repeat(bq).reshape(4, 128).T), c(repeat(bk).reshape(4, 128).T)
    t[d + "out_b"] = c(a[d + "out_b"])
    near = lambda dist: [min(max(n, -16), 16) + 16 for n in dist]
    keys = np.zeros((16, 8, 16, 63), np.float32)
    for h in range(16):
        keys[h, :, h, :] = a[d + "rel_k_table"][near(range(-31, 32))].T
    t[d + "keys"] = keys.reshape(128, 16 * 63)
    values = np.zeros((4, 32, 32, 4, 8), np.float32)
    for i in range(4):
        for place in range(32):
            values[i, :, place, i, :] = a[d + "rel_v_table"][near(range(-place, 32 - place))]
    t[d + "values"] = values.reshape(128, 32 * 32)
    row = np.arange(128)
    own = (row[:, None] // 8 % 4 == row[None, :] // 32).astype(np.float32)
    t[d + "own"] = own
    t[d + "own_scaled"] = own * np.float32(8 ** -0.5)
    t[d + "row_head"] = (row[:, None] // 32 == np.arange(4)).astype(np.float32)
    t[d + "row_position"] = t[d + "row_head"]
    for name in ("Wq", "Wk"):
        t[f"L1_xattn_{name}P"] = c(slots(a[f"L1_xattn_{name}"]))
    for name in ("bq", "bk"):
        t[f"L1_xattn_{name}P"] = c(slots(a[f"L1_xattn_{name}"]).reshape(4, 128).T)
    for name in ("Wv", "bv"):
        t[f"L1_xattn_{name}P"] = c(slots(a[f"L1_xattn_{name}"]))
    t["L1_xattn_WoP"] = c(slots(a["L1_xattn_Wo"].T).T)
    t["L1_xattn_bo"] = c(a["L1_xattn_bo"])
    return t


def kernel(**inputs):
    import numpy as np
    import concourse.bacc as bacc
    from concourse.bass_utils import run_bass_kernel_spmd

    nc = bacc.Bacc("TRN2", target_bir_lowering=False, num_devices=1)
    arrays = lay_out({name: np.asarray(a) for name, a in inputs.items()})
    t = {name: nc.dram_tensor(name, a.shape, mybir.dt.from_np(a.dtype), kind="ExternalInput").ap() for name, a in arrays.items()}
    out = nc.dram_tensor("out", (NB, S, DM), F32, kind="ExternalOutput").ap()
    program(nc, t, out)
    return run_bass_kernel_spmd(nc, [arrays], core_ids=[0]).results[0]["out"]
```

```python
from contextlib import ExitStack

import concourse.bass as bass
from concourse import mybir
from concourse.alu_op_type import AluOpType as ALU

ACT = mybir.ActivationFunctionType
X_AXIS = mybir.AxisListType.X
F32 = mybir.dt.float32
BF16 = mybir.dt.bfloat16

NB = 32
S = 128
DM = 128
DC = 64
EPS = 1e-5
BANK = 512
WEIGHTS = 7720
NEG = -1e30


def need(eng, sem, value):
    if isinstance(value, int) and value <= 0:
        return
    eng.wait_ge(sem, value)


def count(b, per, add):
    return b * per + add


def back(b, n, per):
    return (b, n) if n >= 0 else (b - 1, n + per)


def early(b):
    return isinstance(b, int) and b < 2


def late(b):
    return isinstance(b, int) and b + 2 >= NB


def over_pairs(eng, body, head=1, tail=1):
    for b in range(2 * head):
        body(b, b % 2, b == 0, False)
    with eng.Fori(head, NB // 2 - tail) as i:
        for par in (0, 1):
            body(i * 2 + par, par, False, False)
    for b in range(NB - 2 * tail, NB):
        body(b, b % 2, False, b == NB - 1)


def cols(tile, b, width):
    if isinstance(b, int):
        return tile[:, b * width:(b + 1) * width]
    return tile[:, bass.ds(b * width, width)]


def spread(row, parts=128):
    n = row.shape[0]
    return row.rearrange("(a n) -> a n", a=1).broadcast_to([parts, n])


class Norm:

    def __init__(self, g, name, per, ctx):
        nc = g.nc
        self.g, self.per = g, per
        self.stats = ctx.enter_context(nc.sbuf_tensor(name + "_stats", [128, per, 6], F32))
        self.mv = ctx.enter_context(nc.sbuf_tensor(name + "_mean_var", [128, per, 2], F32))
        self.var_eps = ctx.enter_context(nc.sbuf_tensor(name + "_var_eps", [128, per, 1], F32))
        self.rstd = ctx.enter_context(nc.sbuf_tensor(name + "_rstd", [128, per, 1], F32))
        self.stats_done = g.sem(name + "_stats_done")
        self.moments = g.sem(name + "_moments_ready")
        self.eps_added = g.sem(name + "_eps_added")
        self.rstd_ready = g.sem(name + "_rstd_ready")

    def dve_moments(self, dve, b, n, src):
        done = count(b, self.per, n + 1)
        dve.bn_stats(self.stats[:, n, :], src).then_inc(self.stats_done, 1)
        self.g.wait_apart(dve, self.stats_done, done)
        dve.bn_aggr(self.mv[:, n, :], self.stats[:, n, :]).then_inc(self.moments, 1)

    def pool_rstd(self, pool, b, n):
        done = count(b, self.per, n + 1)
        pool.wait_ge(self.moments, done)
        pool.tensor_tensor(self.var_eps[:, n, :], self.mv[:, n, 1:2], self.g.eps[:, :], ALU.add).then_inc(self.eps_added, 1)
        pool.wait_ge(self.eps_added, done)
        pool.tensor_tensor(self.rstd[:, n, :], self.var_eps[:, n, :], self.g.minus_half[:, :], ALU.pow).then_inc(self.rstd_ready, 1)

    def dve_scale(self, dve, b, n, out, src):
        dve.wait_ge(self.rstd_ready, count(b, self.per, n + 1))
        return dve.tensor_scalar(out, src, self.mv[:, n, 0:1], self.rstd[:, n, 0:1], ALU.subtract, ALU.mult)


class Globals:

    def __init__(self, nc, t, ctx):
        self.nc, self.t, self.ctx, self.phase = nc, t, ctx, None
        self.next_weights = []
        sb = self.sb
        self.ident = sb("ident", [128, 128], F32)
        self.ident_bf = sb("ident_bf", [128, 128], BF16)
        self.eps = sb("eps", [128, 1], F32)
        self.minus_half = sb("minus_half", [128, 1], F32)
        self.x1 = sb("x1", [128, NB * DM], F32)
        self.xc = sb("xc", [128, NB * DM], F32)
        self.xo = sb("xo", [128, NB * DM], F32)
        self.nx = sb("nx", [128, NB * DM], F32)
        self.context = sb("context", [128, NB * DC], F32)
        self.context_n = sb("context_n", [128, NB * DC], F32)
        self.weights_area = sb("weights", [128, WEIGHTS], F32)
        self.setup_done = self.sem("setup_done")
        self.waits_passed = {nc.vector.engine: self.sem("dve_waits_passed"), nc.gpsimd.engine: self.sem("pool_waits_passed")}

    def wait_apart(self, eng, sem, value):
        need(eng, sem, value)
        eng.sem_inc(self.waits_passed[eng.engine], 1)

    def issue_next(self, sp):
        for weights in self.next_weights:
            weights.issue(sp)
        self.next_weights = []

    def sb(self, name, shape, dt=F32, ctx=None):
        return (ctx or self.ctx).enter_context(self.nc.sbuf_tensor(name, shape, dt))

    def sem(self, name):
        sem = (self.phase or self.ctx).enter_context(self.nc.semaphore(name))
        if self.phase:
            self.phase_sems.append(sem)
        return sem

    def run_phase(self, phase):
        with ExitStack() as self.phase:
            self.phase_sems = []
            phase(self)
            numbers = sorted(sem.num for sem in self.phase_sems)
            with self.nc.Block() as block:
                @block.gpsimd
                def _(pool):
                    first = 0
                    for i, number in enumerate(numbers):
                        if i + 1 == len(numbers) or numbers[i + 1] != number + 1:
                            pool.sem_clear(range(numbers[first], number + 1))
                            first = i + 1
        self.phase = None

    def banks(self, names, ctx):
        return [ctx.enter_context(self.nc.psum_tensor(n, [128, BANK], F32)) for n in names]


class Area:

    def __init__(self, tile):
        self.whole, self.used = tile, 0

    def take(self, width):
        first, self.used = self.used, self.used + width
        assert self.used <= self.whole.shape[1]
        return self.whole[:, first:self.used]


class Weights:

    def __init__(self, g, name, area):
        self.g, self.name, self.loads, self.tiles, self.area = g, name, [], {}, area
        self.loaded = g.sem(name + "weights_loaded")

    def tile(self, key, shape, src, where=None):
        tile = self.area.take(shape[1])
        self.tiles[key] = tile
        self.loads.append((tile if where is None else where(tile), src))
        return tile

    def __getitem__(self, key):
        return self.tiles[key]

    @property
    def total(self):
        return 16 * len(self.loads)

    def issue(self, eng):
        for dst, src in self.loads:
            eng.dma_start(dst, src).then_inc(self.loaded, 16)


def declare_weights(g):
    t = g.t
    g.weights = {}
    area = Area(g.weights_area)
    col = lambda v: v.rearrange("(p a) -> p a", a=1)
    chunks = lambda tile: tile[:, :].rearrange("p (c n) -> p c n", n=DM)
    rows = lambda m: m.rearrange("(c p) n -> p c n", p=128)
    for name, src, dy in (("b_", "L0_xattn_a1_", DM), ("d_", "L0_xattn_a2_", DC)):
        w = g.weights[name] = Weights(g, name, area)
        w.tile("wq", [128, 512], t[src + "wq"], lambda x: x[:, :])
        w.tile("wk", [128, 512], t[src + "wk"], lambda x: x[0:dy, :])
        w.tile("wv", [128, 512], t[src + "wv"], lambda x: x[0:dy, :])
        w.tile("wo", [128, 4 * DM], rows(t[src + "li1_w"]), chunks)
        w.tile("bo", [128, DM], spread(t[src + "li1_b"]), lambda x: x[:, :])
        w.tile("gx", [128, 1], col(t[src + "lnx_g"]), lambda x: x[:, :])
        w.tile("bx", [128, 1], col(t[src + "lnx_b"]), lambda x: x[:, :])
        w.tile("gy", [128, 1], col(t[src + "lny_g"]), lambda x: x[0:dy, :])
        w.tile("by", [128, 1], col(t[src + "lny_b"]), lambda x: x[0:dy, :])
    for name, src in (("c_", "L0_xattn_a1_"), ("e_", "L0_xattn_a2_")):
        w = g.weights[name] = Weights(g, name, area)
        w.tile("w1", [128, 512], t[src + "li2_w"], lambda x: x[:, :])
        w.tile("w2", [128, 4 * DM], rows(t[src + "li3_w"]), chunks)
        w.tile("b1", [128, 4], t[src + "li2_bT"], lambda x: x[:, :])
        w.tile("b2", [128, DM], spread(t[src + "li3_b"]), lambda x: x[:, :])
        w.tile("gx", [128, 1], col(t[src + "ln3_g"]), lambda x: x[:, :])
        w.tile("bx", [128, 1], col(t[src + "ln3_b"]), lambda x: x[:, :])
        if name == "c_":
            w.tile("ln_g", [128, DM], spread(t["L0_xattn_ln2_g"]), lambda x: x[:, :])
            w.tile("ln_b", [128, DM], spread(t["L0_xattn_ln2_b"]), lambda x: x[:, :])


def declare_layer1_weights(g):
    t = g.t
    area = Area(g.weights_area)
    chunks = lambda tile: tile[:, :].rearrange("p (c n) -> p c n", n=DM)
    rows = lambda m: m.rearrange("(c p) n -> p c n", p=128)
    w = g.weights["i_"] = Weights(g, "i_", area)
    w.tile("w1", [128, 512], t["L1_ffn_W1"], lambda x: x[:, :])
    w.tile("w2", [128, 4 * DM], rows(t["L1_ffn_W2"]), chunks)
    w.tile("b1", [128, 4], t["L1_ffn_b1T"], lambda x: x[:, :])
    w.tile("b2", [128, DM], spread(t["L1_ffn_b2"]), lambda x: x[:, :])
    w.tile("theta", [128, 4], t["L1_ffn_quantum_phasesT"], lambda x: x[:, :])
    w.tile("wr", [128, 4], t["L1_ffn_quantum_weights_realT"], lambda x: x[:, :])
    w.tile("wi", [128, 4], t["L1_ffn_quantum_weights_imagT"], lambda x: x[:, :])
    w = g.weights["g_"] = Weights(g, "g_", area)
    for name, shape in (("wq", [128, 128]), ("wq_rep", [128, 512]), ("wk", [128, 128]), ("wv", [128, 128]), ("wo", [128, 128]), ("keys", [128, 16 * 63]),
                        ("values", [128, 32 * 32]), ("bq", [128, 1]), ("bv", [128, 1]), ("bq_rep", [128, 4]), ("bk_rep", [128, 4]),
                        ("row_head", [128, 4]), ("own_scaled", [128, 128])):
        w.tile(name, shape, t["L1_attn_" + name], lambda x: x[:, :])
    w.tile("bo", [128, DM], spread(t["L1_attn_out_b"]), lambda x: x[:, :])
    w = g.weights["h_"] = Weights(g, "h_", area)
    w.tile("wq", [128, 512], t["L1_xattn_WqP"], lambda x: x[:, :])
    w.tile("wk", [128, 512], t["L1_xattn_WkP"], lambda x: x[0:DC, :])
    w.tile("wv", [128, 512], t["L1_xattn_WvP"], lambda x: x[0:DC, :])
    w.tile("wo", [128, 4 * DM], rows(t["L1_xattn_WoP"]), chunks)
    w.tile("bo", [128, DM], spread(t["L1_xattn_bo"]), lambda x: x[:, :])
    w.tile("bv", [128, 512], spread(t["L1_xattn_bvP"]), lambda x: x[:, :])
    w.tile("bq", [128, 4], t["L1_xattn_bqP"], lambda x: x[:, :])
    w.tile("bk", [128, 4], t["L1_xattn_bkP"], lambda x: x[:, :])


def setup(g):
    nc = g.nc
    steps = g.sem("setup_steps")
    ctx_loaded = g.sem("context_loaded")
    with nc.Block() as block:
        @block.sync
        def _(sp):
            sp.dma_start(g.context[:, :].rearrange("s (b c) -> s b c", b=NB), g.t["ctx_512"].rearrange("b s c -> s b c")).then_inc(ctx_loaded, 16)
            sp.wait_ge(ctx_loaded, 16)

        @block.gpsimd
        def _(pool):
            pool.memset(g.eps[:, :], EPS).then_inc(steps, 1)
            pool.memset(g.minus_half[:, :], -0.5).then_inc(steps, 1)
            pool.memset(g.ident[:, :], 0.0).then_inc(steps, 1)
            pool.memset(g.ident_bf[:, :], 0.0).then_inc(steps, 1)
            pool.wait_ge(steps, 4)
            for m in (g.ident, g.ident_bf):
                pool.affine_select(out=m[:, :], in_=m[:, :], compare_op=ALU.not_equal, fill=1.0, base=0,
                                   pattern=[[-1, 128]], channel_multiplier=1).then_inc(steps, 1)
            pool.wait_ge(steps, 6)
            pool.sem_inc(g.setup_done, 1)


def self_attention(g):
    nc, t = g.nc, g.t
    H, HK, HD, G4 = 64, 8, 64, 4
    NG = H // G4
    NP = NG // 2
    X_FIRST = 2
    Q_FIRST = 1024
    NCH = H * HD // 128
    SCALE = HD ** -0.5
    with ExitStack() as ctx:
        sb = lambda name, shape, dt=F32: g.sb("a_" + name, shape, dt, ctx)
        wq = sb("wq", [128, H * HD])
        wk = sb("wk", [128, HK * HD])
        wv = sb("wv", [128, HK * HD])
        wo = sb("wo", [128, NCH * DM])
        bq = sb("bq", [128, NCH])
        bk = sb("bk", [128, HK // 2])
        bv = sb("bv", [128, HK * HD])
        bo = sb("bo", [128, DM])
        ln_g, ln_b = sb("ln_g", [128, DM]), sb("ln_b", [128, DM])
        sinks, neg_sinks = sb("sinks", [128, H]), sb("neg_sinks", [128, H])
        mask = sb("mask", [128, G4 * S], BF16)
        x_in = sb("x_in", [128, 2, DM])
        xT = sb("xT", [128, 2, S])
        kT = sb("kT", [128, 2, HK // 2 * S])
        v = sb("v", [128, 2, HK * HD])
        qT = sb("qT", [128, 2, 4 * S])
        ex, probs = sb("ex", [128, 2, G4 * S]), sb("probs", [128, 2, G4 * S])
        probsT = sb("probsT", [128, 4, G4 * S])
        oT = sb("oT", [128, 2, 4 * S])
        max_neg, shift = sb("max_neg", [128, 2, G4]), sb("shift", [128, 2, G4])
        sums, sink_arg, sink_exp = sb("sums", [128, 2, G4]), sb("sink_arg", [128, 2, G4]), sb("sink_exp", [128, 2, G4])
        denom, rden = sb("denom", [128, 2, G4]), sb("rden", [128, 2, G4])
        res, res2 = sb("res", [128, DM]), sb("res2", [128, DM])
        n1, n1g = sb("n1", [128, DM]), sb("n1g", [128, DM])
        s_even, s_odd, pt0, pt1, po0, po1, p_y, p_q = g.banks(
            ["a_s_even", "a_s_odd", "a_pt0", "a_pt1", "a_po0", "a_po1", "a_py", "a_pq"], ctx)
        p_s, p_t, p_o = [s_even, s_odd], [pt0, pt1], [po0, po1]
        norm = Norm(g, "a_ln", 4, ctx)

        sem = lambda n: g.sem("a_" + n)
        weights, w_wo = sem("weights_loaded"), sem("wo_loaded")
        wq_loaded, x_loaded = ([sem(f"{n}_loaded{k}") for k in (0, 1)] for n in ("wq", "x"))
        x_ready, mask_zero, mask_ready, neg_sinks_ready = sem("x_ready"), sem("mask_zero"), sem("mask_ready"), sem("neg_sinks_ready")
        xT_done, xT_ready = sem("xT_done"), sem("xT_ready")
        kv_done, kv_ready = sem("kv_done"), sem("kv_ready")
        q_done, q_ready = sem("q_done"), sem("q_ready")
        scores_done, max_ready, shift_ready, ex_ready = sem("scores_done"), sem("max_ready"), sem("shift_ready"), sem("ex_ready")
        arg_ready, sinkexp_ready, denom_ready, rden_ready = sem("arg_ready"), sem("sinkexp_ready"), sem("denom_ready"), sem("rden_ready")
        probsT_done, probsT_ready = sem("probsT_done"), sem("probsT_ready")
        probs_ready = sem("probs_ready")
        oT_done, oT_ready = sem("oT_done"), sem("oT_ready")
        y_done, res_ready, res2_ready = sem("y_done"), sem("res_ready"), sem("res2_ready")
        x1_ready, n1_ready, n1g_ready, xc_ready, nx_ready, context_ready = sem("x1_ready"), sem("n1_ready"), sem("n1g_ready"), sem("xc_ready"), sem("nx_ready"), sem("context_ready")
        E0 = 4

        def key_head(gr):
            return gr // 4 * 2 + gr % 2

        def heads(gr):
            first = key_head(gr) * 8 + gr // 2 % 2 * G4
            return slice(first, first + G4)

        with nc.Block() as block:
            @block.sync
            def _(sp):
                def load_x(k, first, end):
                    sp.dma_start(g.x1[:, first * DM:end * DM].rearrange("s (b n) -> s b n", b=end - first),
                                 t["x"][first:end].rearrange("b s n -> s b n")).then_inc(x_loaded[k], 16)

                def load_wq(k, first, end):
                    sp.dma_start(wq[:, first:end], t["L0_attn_WqT"][:, first:end]).then_inc(wq_loaded[k], 16)

                load_x(0, 0, X_FIRST)
                sp.dma_start(wk[:, :], t["L0_attn_WkT"]).then_inc(weights, 16)
                sp.dma_start(bk[:, :], t["L0_attn_bkT"]).then_inc(weights, 16)
                sp.dma_start(wv[:, :], t["L0_attn_WvT"]).then_inc(weights, 16)
                sp.dma_start(bv[:, :], spread(t["L0_attn_bv"])).then_inc(weights, 16)
                sp.dma_start(bq[:, :], t["L0_attn_bqT"]).then_inc(weights, 16)
                sp.dma_start(sinks[:, :], spread(t["L0_attn_sinks"])).then_inc(weights, 16)
                load_wq(0, 0, Q_FIRST)
                load_wq(1, Q_FIRST, H * HD)
                sp.dma_start(wo[:, :].rearrange("p (c n) -> p c n", n=DM), t["L0_attn_WoT"].rearrange("(c p) n -> p c n", p=128)).then_inc(w_wo, 16)
                sp.dma_start(bo[:, :], spread(t["L0_attn_bo"])).then_inc(w_wo, 16)
                sp.dma_start(ln_g[:, :], spread(t["L0_xattn_ln1_g"])).then_inc(w_wo, 16)
                sp.dma_start(ln_b[:, :], spread(t["L0_xattn_ln1_b"])).then_inc(w_wo, 16)
                load_x(1, X_FIRST, NB)
                for w in g.weights.values():
                    w.issue(sp)

            @block.gpsimd
            def _(pool):
                pool.memset(mask[:, :], 0.0).then_inc(mask_zero, 1)
                pool.wait_ge(mask_zero, 1)
                m = mask[:, :].rearrange("p (a k) -> p a k", a=G4)
                pool.affine_select(out=m, in_=m, compare_op=ALU.is_ge, fill=NEG, base=0,
                                   pattern=[[0, G4], [-1, S]], channel_multiplier=1).then_inc(mask_ready, 1)

                def copy_x(b, par):
                    pool.tensor_copy(x_in[:, par, :], cols(g.x1, b, DM)).then_inc(x_ready, 1)

                pool.wait_ge(x_loaded[0], 16)
                copy_x(0, 0)
                pool.wait_ge(weights, 6 * 16)

                def finish(b, gr):
                    if gr == E0:
                        pool.wait_ge(res_ready, b + 1)
                        need(pool, x1_ready, b)
                        pool.tensor_tensor(res2[:, :], res[:, :], bo[:, :], ALU.add).then_inc(res2_ready, 1)
                    if gr == E0 + 1:
                        norm.pool_rstd(pool, b, 0)
                    if gr == E0 + 2:
                        norm.pool_rstd(pool, b, 1)
                    if gr == E0 + 4:
                        norm.pool_rstd(pool, b, 2)
                    if gr == E0 + 6:
                        pool.wait_ge(n1_ready, b + 1)
                        need(pool, xc_ready, b)
                        pool.tensor_tensor(n1g[:, :], n1[:, :], ln_g[:, :], ALU.mult).then_inc(n1g_ready, 1)
                        g.wait_apart(pool, n1g_ready, b + 1)
                        pool.tensor_tensor(cols(g.xc, b, DM), n1g[:, :], ln_b[:, :], ALU.add).then_inc(xc_ready, 1)
                    if gr == E0 + 8:
                        norm.pool_rstd(pool, b, 3)

                def argue(b, gr):
                    n = count(b, NG, gr)
                    par = gr % 2
                    pool.wait_ge(shift_ready, n + 1)
                    need(pool, sinkexp_ready, n - 1)
                    pool.tensor_tensor(sink_arg[:, par, :], sinks[:, heads(gr)], shift[:, par, :], ALU.add).then_inc(arg_ready, 1)

                def total(b, gr):
                    n = count(b, NG, gr)
                    par = gr % 2
                    pool.wait_ge(sinkexp_ready, n + 1)
                    pool.wait_ge(ex_ready, n + 1)
                    need(pool, rden_ready, n - 1)
                    pool.tensor_tensor(denom[:, par, :], sums[:, par, :], sink_exp[:, par, :], ALU.add).then_inc(denom_ready, 1)

                def divide(b, gr):
                    n = count(b, NG, gr)
                    par = gr % 2
                    pool.wait_ge(rden_ready, n + 1)
                    need(pool, probsT_done, n - 1)
                    pool.tensor_tensor(probs[:, par, :].rearrange("p (h k) -> p h k", k=S), ex[:, par, :].rearrange("p (h k) -> p h k", k=S),
                                       rden[:, par, :].rearrange("p (h a) -> p h a", a=1).broadcast_to([128, G4, S]), ALU.mult).then_inc(probs_ready, 1)

                def body(b, par, first, last):
                    for gr in range(NG):
                        argue(b, gr)
                        total(b, gr)
                        divide(b, gr)
                        if not first:
                            finish(b - 1, gr)
                        if first and gr == E0:
                            pool.wait_ge(x_loaded[1], 16)
                            pool.wait_ge(w_wo, 4 * 16)
                        if gr == E0 and not last:
                            copy_x(b + 1, 1 - par)
                over_pairs(pool, body)
                for gr in range(E0, E0 + 9):
                    finish(NB - 1, gr)

            @block.scalar
            def _(act):
                act.wait_ge(weights, 6 * 16)

                def q_copy(b, k):
                    n = count(b, NP, k)
                    act.wait_ge(q_done, n + 1)
                    need(act, scores_done, count(b, NG, 2 * k - 2))
                    for c in range(4):
                        ch = 4 * k + c
                        ins = act.activation(qT[:, k % 2, c * S:(c + 1) * S], p_q[:, c * S:(c + 1) * S], ACT.Identity, bias=bq[:, ch:ch + 1])
                    ins.then_inc(q_ready, 1)

                def xT_copy(b, par):
                    act.wait_ge(xT_done, b + 1)
                    act.activation(xT[:, par, :], p_q[:, 0:S], ACT.Copy).then_inc(xT_ready, 1)

                def exps(b, gr):
                    n = count(b, NG, gr)
                    par = gr % 2
                    act.wait_ge(shift_ready, n + 1)
                    need(act, probs_ready, n - 1)
                    need(act, denom_ready, n - 1)
                    for j in range(G4):
                        ins = act.activation(ex[:, par, j * S:(j + 1) * S], p_s[par][:, j * S:(j + 1) * S], ACT.Exp,
                                             bias=shift[:, par, j:j + 1], scale=SCALE, accum_out=sums[:, par, j:j + 1])
                    ins.then_inc(ex_ready, 1)
                    act.wait_ge(arg_ready, n + 1)
                    act.activation(sink_exp[:, par, :], sink_arg[:, par, :], ACT.Exp).then_inc(sinkexp_ready, 1)

                xT_copy(0, 0)
                q_copy(0, 0)

                def body(b, par, first, last):
                    for gr in range(NG):
                        exps(b, gr)
                        if gr % 2 == 0:
                            if gr < NG - 2:
                                q_copy(b, gr // 2 + 1)
                            elif not last:
                                q_copy(b + 1, 0)
                        if gr == 7 and not last:
                            xT_copy(b + 1, 1 - par)
                over_pairs(act, body)

            @block.vector
            def _(dve):
                dve.wait_ge(weights, 6 * 16)
                dve.tensor_scalar(neg_sinks[:, :], sinks[:, :], -1.0, None, ALU.mult).then_inc(neg_sinks_ready, 1)
                dve.wait_ge(neg_sinks_ready, 1)

                def kv_copy(b, k, par):
                    dve.wait_ge(kv_done, count(b, 2, k + 1))
                    if k == 0:
                        dve.tensor_tensor(kT[:, par, :].rearrange("p (h s) -> p h s", s=S), p_q[:, :].rearrange("p (h s) -> p h s", s=S),
                                          bk[:, :].rearrange("p (h a) -> p h a", a=1).broadcast_to([128, 4, S]), ALU.add).then_inc(kv_ready, 1)
                    else:
                        dve.tensor_tensor(v[:, par, :], p_q[:, :], bv[:, :], ALU.add).then_inc(kv_ready, 1)

                def shifts(b, gr):
                    n = count(b, NG, gr)
                    par = gr % 2
                    dve.wait_ge(scores_done, n + 1)
                    dve.tensor_reduce(max_neg[:, par, :], p_s[par][:, :].rearrange("p (h k) -> p h k", k=S), X_AXIS, ALU.max, negate=True).then_inc(max_ready, 1)
                    dve.wait_ge(max_ready, n + 1)
                    need(dve, ex_ready, n - 1)
                    need(dve, arg_ready, n - 1)
                    dve.scalar_tensor_tensor(out=shift[:, par, :], in0=max_neg[:, par, :], scalar=SCALE,
                                             in1=neg_sinks[:, heads(gr)], op0=ALU.mult, op1=ALU.min).then_inc(shift_ready, 1)

                def invert(b, gr):
                    n = count(b, NG, gr)
                    par = gr % 2
                    dve.wait_ge(denom_ready, n + 1)
                    need(dve, probs_ready, n - 1)
                    dve.reciprocal(rden[:, par, :], denom[:, par, :]).then_inc(rden_ready, 1)

                def probsT_copy(b, gr):
                    n = count(b, NG, gr)
                    dve.wait_ge(probsT_done, n + 1)
                    need(dve, oT_done, count(b, NP, gr // 2 - 1))
                    dve.tensor_copy(probsT[:, gr % 4, :], p_t[gr % 2][:, :]).then_inc(probsT_ready, 1)

                def oT_copy(b, k):
                    n = count(b, NP, k)
                    dve.wait_ge(oT_done, n + 1)
                    need(dve, y_done, n - 1)
                    dve.tensor_copy(oT[:, k % 2, :], p_o[k % 2][:, :]).then_inc(oT_ready, 1)

                def finish(b, gr, par):
                    if gr == E0:
                        dve.wait_ge(y_done, count(b, NP, NP))
                        need(dve, res2_ready, b)
                        dve.tensor_tensor(res[:, :], p_y[:, 0:DM], x_in[:, par, :], ALU.add).then_inc(res_ready, 1)
                    if gr == E0 + 1:
                        dve.wait_ge(res2_ready, b + 1)
                        norm.dve_moments(dve, b, 0, res2[:, :])
                    if gr == E0 + 2:
                        norm.dve_moments(dve, b, 1, cols(g.context, b, DC))
                    if gr == E0 + 3:
                        norm.dve_scale(dve, b, 0, cols(g.x1, b, DM), res2[:, :]).then_inc(x1_ready, 1)
                    if gr == E0 + 4:
                        g.wait_apart(dve, x1_ready, b + 1)
                        norm.dve_moments(dve, b, 2, cols(g.x1, b, DM))
                    if gr == E0 + 5:
                        norm.dve_scale(dve, b, 1, cols(g.context_n, b, DC), cols(g.context, b, DC)).then_inc(context_ready, 1)
                    if gr == E0 + 6:
                        need(dve, n1g_ready, b)
                        norm.dve_scale(dve, b, 2, n1[:, :], cols(g.x1, b, DM)).then_inc(n1_ready, 1)
                    if gr == E0 + 8:
                        g.wait_apart(dve, xc_ready, b + 1)
                        norm.dve_moments(dve, b, 3, cols(g.xc, b, DM))
                    if gr == E0 + 10:
                        norm.dve_scale(dve, b, 3, cols(g.nx, b, DM), cols(g.xc, b, DM)).then_inc(nx_ready, 1)

                for k in (0, 1):
                    kv_copy(0, k, 0)

                def body(b, par, first, last):
                    for gr in range(NG):
                        if gr % 2 == 1 and (not first or gr >= 5):
                            oT_copy(*back(b, gr // 2 - 2, NP))
                        if not first or gr >= 1:
                            invert(*back(b, gr - 1, NG))
                        shifts(b, gr)
                        if not first or gr >= 2:
                            probsT_copy(*back(b, gr - 2, NG))
                        if not first:
                            finish(b - 1, gr, 1 - par)
                        if gr in (9, 11) and not last:
                            kv_copy(b + 1, (gr - 9) // 2, 1 - par)
                over_pairs(dve, body)
                invert(NB - 1, NG - 1)
                for gr in (NG - 2, NG - 1):
                    probsT_copy(NB - 1, gr)
                for k in (NP - 2, NP - 1):
                    oT_copy(NB - 1, k)
                for gr in range(E0, E0 + 11):
                    finish(NB - 1, gr, 1)
                dve.wait_ge(nx_ready, NB)
                dve.wait_ge(context_ready, NB)

            @block.tensor
            def _(pe):
                pe.wait_ge(weights, 6 * 16)
                pe.wait_ge(mask_ready, 1)
                pe.wait_ge(g.setup_done, 1)

                def transpose_x(b, par):
                    pe.wait_ge(x_ready, b + 1)
                    need(pe, q_ready, count(b - 1, NP, 5) if not (isinstance(b, int) and b == 0) else 0)
                    pe.transpose(p_q[:, 0:S], x_in[:, par, :], g.ident[:, :]).then_inc(xT_done, 1)

                def project_kv(b, k, par):
                    if k == 0:
                        pe.wait_ge(xT_ready, b + 1)
                    need(pe, kv_ready, count(b, 2, k))
                    if not (isinstance(b, int) and b == 0):
                        pe.wait_ge(q_ready, count(b - 1, NP, 6 + k))
                    if k == 0:
                        for c in range(4):
                            ins = pe.matmul(p_q[:, c * S:(c + 1) * S], wk[:, c * 128:(c + 1) * 128], xT[:, par, :], start=True, stop=True)
                    else:
                        ins = pe.matmul(p_q[:, :], xT[:, par, :], wv[:, :], start=True, stop=True)
                    ins.then_inc(kv_done, 1)

                def project_q(b, k, par):
                    n = count(b, NP, k)
                    need(pe, q_ready, n)
                    if k == 5:
                        if not (isinstance(b, int) and b == NB - 1):
                            pe.wait_ge(xT_ready, b + 2)
                    if k in (6, 7):
                        if not (isinstance(b, int) and b == NB - 1):
                            pe.wait_ge(kv_ready, count(b + 1, 2, k - 5))
                    if k == 0:
                        pe.wait_ge(kv_ready, count(b, 2, 2))
                    if isinstance(b, int) and b == 0 and k in (0, 2):
                        pe.wait_ge(wq_loaded[k // 2], 16)
                    for c in range(4):
                        ch = 4 * k + c
                        ins = pe.matmul(p_q[:, c * S:(c + 1) * S], wq[:, ch * 128:(ch + 1) * 128], xT[:, par, :], start=True, stop=True)
                    ins.then_inc(q_done, 1)

                def score(b, gr, par):
                    n = count(b, NG, gr)
                    r = gr % 2
                    if r == 0:
                        pe.wait_ge(q_ready, count(b, NP, gr // 2 + 1))
                    if gr == 0:
                        pe.wait_ge(kv_ready, count(b, 2, 2))
                    need(pe, ex_ready, n - 1)
                    pe.matmul(p_s[r][:, :], g.ident_bf[:, :], mask[:, :], start=True, stop=False, skip_group_check=True)
                    for j in range(G4):
                        ins = pe.matmul(p_s[r][:, j * S:(j + 1) * S], qT[64 * r:64 * r + 64, gr // 2 % 2, j * S:(j + 1) * S],
                                        kT[64 * r:64 * r + 64, par, gr // 4 * S:(gr // 4 + 1) * S], start=False, stop=True, skip_group_check=True)
                    ins.then_inc(scores_done, 1)

                def transpose_probs(b, gr):
                    n = count(b, NG, gr)
                    r = gr % 2
                    pe.wait_ge(probs_ready, n + 1)
                    need(pe, probsT_ready, n - 1)
                    for j in range(G4):
                        ins = pe.transpose(p_t[r][:, j * S:(j + 1) * S], probs[:, r, j * S:(j + 1) * S], g.ident[:, :])
                    ins.then_inc(probsT_done, 1)

                def weigh(b, k, par):
                    n = count(b, NP, k)
                    pe.wait_ge(probsT_ready, count(b, NG, 2 * k + 2))
                    need(pe, oT_ready, n - 1)
                    for r in (0, 1):
                        kv = key_head(2 * k + r)
                        ins = pe.matmul(p_o[k % 2][r * HD:(r + 1) * HD, :], v[:, par, kv * HD:(kv + 1) * HD], probsT[:, (2 * k + r) % 4, :], start=True, stop=True)
                    ins.then_inc(oT_done, 1)

                def project_o(b, k):
                    n = count(b, NP, k)
                    if isinstance(b, int) and b == 0 and k == 0:
                        pe.wait_ge(w_wo, 4 * 16)
                    if k == 0:
                        need(pe, res_ready, b)
                    pe.wait_ge(oT_ready, n + 1)
                    for c in range(4):
                        ch = 4 * k + c
                        ins = pe.matmul(p_y[:, 0:DM], oT[:, k % 2, c * S:(c + 1) * S], wo[:, ch * DM:(ch + 1) * DM], start=(ch == 0), stop=(ch == NCH - 1))
                    ins.then_inc(y_done, 1)

                transpose_x(0, 0)
                for k in (0, 1):
                    project_kv(0, k, 0)
                project_q(0, 0, 0)

                def body(b, par, first, last):
                    for gr in range(NG):
                        score(b, gr, par)
                        if not first or gr >= 2:
                            transpose_probs(*back(b, gr - 2, NG))
                        if gr % 2 == 0 and (not first or gr >= 4):
                            weigh(*back(b, gr // 2 - 2, NP), par if gr >= 4 else 1 - par)
                        if gr % 2 == 1 and (not first or gr >= 5):
                            project_o(*back(b, gr // 2 - 2, NP))
                        if gr % 2 == 0:
                            if gr < NG - 2:
                                project_q(b, gr // 2 + 1, par)
                            elif not last:
                                project_q(b + 1, 0, 1 - par)
                        if gr == 7 and not last:
                            transpose_x(b + 1, 1 - par)
                        if gr in (9, 11) and not last:
                            project_kv(b + 1, (gr - 9) // 2, 1 - par)
                over_pairs(pe, body)
                for gr in (NG - 2, NG - 1):
                    transpose_probs(NB - 1, gr)
                for k in (NP - 2, NP - 1):
                    weigh(NB - 1, k, 1)
                    project_o(NB - 1, k)


class Heads16:

    def __init__(self, name, scale, width, own_keys, affine, bias, later_mask):
        self.name, self.scale, self.width = name, scale, width
        self.own_keys, self.affine, self.bias, self.later_mask = own_keys, affine, bias, later_mask


def attention16(g, cfg):
    nc, t = g.nc, g.t
    NG, G4, HD, DY = 4, 4, 32, cfg.width
    OC = 16 * HD // 128
    with ExitStack() as ctx:
        sb = lambda name, shape, dt=F32: g.sb(cfg.name + name, shape, dt, ctx)
        W = g.weights[cfg.name]
        kvw = DY if not cfg.own_keys else DM
        x_in, y_in = sb("x_in", [128, DM]), sb("y_in", [128, DY])
        xT, yT = sb("xT", [128, S]), sb("yT", [128, S])
        qT, kT = sb("qT", [128, 2, 4 * S]), sb("kT", [128, 2, 4 * S])
        v = sb("v", [128, 2, 16 * HD])
        ex, probs = sb("ex", [128, 2, G4 * S]), sb("probs", [128, 2, G4 * S])
        probsT, oT = sb("probsT", [128, 2 * NG, G4 * S]), sb("oT", [128, OC * S])
        max_neg, shift = sb("max_neg", [128, 2, G4]), sb("shift", [128, 2, G4])
        sums, rden = sb("sums", [128, 2, G4]), sb("rden", [128, 2, G4])
        res, res2 = sb("res", [128, DM]), sb("res2", [128, DM])
        banks = g.banks([cfg.name + n for n in ("s0", "s1", "s2", "s3", "pt", "po", "pa", "pb")], ctx)
        p_s, (p_t, p_o, p_a, p_b) = banks[:4], banks[4:]
        norm = Norm(g, cfg.name + "ln", 1, ctx)
        if cfg.later_mask:
            keep = sb("keep", [128, S])

        sem = lambda n: g.sem(cfg.name + n)
        keep_one, keep_ready = sem("keep_one"), sem("keep_ready")
        x_ready, T_done, T_ready = sem("x_ready"), sem("T_done"), sem("T_ready")
        q_done, q_ready, k_done, k_ready, v_done, v_ready = (sem(n) for n in ("q_done", "q_ready", "k_done", "k_ready", "v_done", "v_ready"))
        scores_done, max_ready, shift_ready, ex_ready = sem("scores_done"), sem("max_ready"), sem("shift_ready"), sem("ex_ready")
        rden_ready, probs_ready, probsT_done, probsT_ready = sem("rden_ready"), sem("probs_ready"), sem("probsT_done"), sem("probsT_ready")
        oT_done, oT_ready, y_done, res_ready, res2_ready, out_ready = (sem(n) for n in ("oT_done", "oT_ready", "y_done", "res_ready", "res2_ready", "out_ready"))

        residual = g.x1 if cfg.name == "h_" else g.xc
        q_src = g.x1 if cfg.name == "h_" else g.nx
        k_src = g.context if cfg.name == "h_" else g.context_n

        with nc.Block() as block:
            @block.sync
            def _(sp):
                g.issue_next(sp)

            @block.gpsimd
            def _(pool):
                if cfg.later_mask:
                    pool.memset(keep[:, :], 1.0).then_inc(keep_one, 1)
                    pool.wait_ge(keep_one, 1)
                    pool.affine_select(out=keep[:, :], in_=keep[:, :], compare_op=ALU.is_gt, fill=0.0, base=0,
                                       pattern=[[-1, S]], channel_multiplier=1).then_inc(keep_ready, 1)
                pool.wait_ge(W.loaded, W.total)

                def copy_in(b):
                    g.wait_apart(pool, T_done, b)
                    ins = pool.tensor_copy(x_in[:, :], cols(q_src, b, DM))
                    if not cfg.own_keys:
                        ins.then_inc(x_ready, 1)
                        ins = pool.tensor_copy(y_in[:, :], cols(k_src, b, DC))
                    ins.then_inc(x_ready, 1)

                def divide(b, gr):
                    n = count(b, NG, gr)
                    pool.wait_ge(rden_ready, n + 1)
                    need(pool, probsT_done, n - 1)
                    pool.tensor_tensor(probs[:, gr % 2, :].rearrange("p (h k) -> p h k", k=S), ex[:, gr % 2, :].rearrange("p (h k) -> p h k", k=S),
                                       rden[:, gr % 2, :].rearrange("p (h a) -> p h a", a=1).broadcast_to([128, G4, S]), ALU.mult).then_inc(probs_ready, 1)

                def finish(b, gr):
                    if gr == 0:
                        g.wait_apart(pool, res_ready, b + 1)
                        if cfg.name == "h_":
                            need(pool, out_ready, b)
                            pool.tensor_tensor(res2[:, :], res[:, :], W["bo"][:, :], ALU.add).then_inc(res2_ready, 1)
                        else:
                            pool.tensor_tensor(cols(g.xo, b, DM), res[:, :], W["bo"][:, :], ALU.add).then_inc(res2_ready, 1)
                    if gr == 1:
                        norm.pool_rstd(pool, b, 0)

                copy_in(0)
                copy_in(1)

                def body(b, par, first, last):
                    for gr in range(NG):
                        divide(b, gr)
                        if gr in (0, 1) and not early(b):
                            finish(b - 2, gr)
                        if gr == 0 and not late(b):
                            copy_in(b + 2)
                over_pairs(pool, body, head=2)
                for b in (NB - 2, NB - 1):
                    for gr in (0, 1):
                        finish(b, gr)

            @block.scalar
            def _(act):
                act.wait_ge(W.loaded, W.total)

                def T_copy(b):
                    act.wait_ge(T_done, b + 1)
                    if cfg.affine:
                        act.activation(xT[:, :], p_a[:, 0:S], ACT.Identity, scale=W["gx"][:, 0:1], bias=W["bx"][:, 0:1])
                        src = p_a[0:kvw, 0:S] if cfg.own_keys else p_a[0:kvw, S:2 * S]
                        act.activation(yT[0:kvw, :], src, ACT.Identity, scale=W["gy"][0:kvw, 0:1], bias=W["by"][0:kvw, 0:1]).then_inc(T_ready, 1)
                    else:
                        act.activation(xT[:, :], p_a[:, 0:S], ACT.Copy)
                        act.activation(yT[0:kvw, :], p_a[0:kvw, S:2 * S], ACT.Copy).then_inc(T_ready, 1)

                def q_copy(b, par):
                    act.wait_ge(q_done, b + 1)
                    if cfg.bias:
                        for c in range(4):
                            ins = act.activation(qT[:, par, c * S:(c + 1) * S], p_b[:, c * S:(c + 1) * S], ACT.Identity, bias=W["bq"][:, c:c + 1])
                    else:
                        ins = act.activation(qT[:, par, :], p_b[:, :], ACT.Copy)
                    ins.then_inc(q_ready, 1)

                def exps(b, gr):
                    n = count(b, NG, gr)
                    act.wait_ge(shift_ready, n + 1)
                    need(act, probs_ready, n - 1)
                    for j in range(G4):
                        ins = act.activation(ex[:, gr % 2, j * S:(j + 1) * S], p_s[gr][:, j * S:(j + 1) * S], ACT.Exp,
                                             bias=shift[:, gr % 2, j:j + 1], scale=cfg.scale, accum_out=sums[:, gr % 2, j:j + 1])
                    ins.then_inc(ex_ready, 1)

                def k_copy(b, par):
                    act.wait_ge(k_done, b + 1)
                    if cfg.bias:
                        for c in range(4):
                            ins = act.activation(kT[:, par, c * S:(c + 1) * S], p_a[:, c * S:(c + 1) * S], ACT.Identity, bias=W["bk"][:, c:c + 1])
                    else:
                        ins = act.activation(kT[:, par, :], p_a[:, :], ACT.Copy)
                    ins.then_inc(k_ready, 1)

                def oT_copy(b):
                    act.wait_ge(oT_done, b + 1)
                    need(act, y_done, b)
                    act.activation(oT[:, :], p_o[:, :], ACT.Copy).then_inc(oT_ready, 1)

                T_copy(0)
                q_copy(0, 0)
                k_copy(0, 0)

                def body(b, par, first, last):
                    for gr in range(NG):
                        if gr == 0 and not early(b):
                            oT_copy(b - 2)
                        if gr == 0 and not last:
                            T_copy(b + 1)
                        exps(b, gr)
                        if gr == 1 and not last:
                            q_copy(b + 1, 1 - par)
                        if gr == 2 and not last:
                            k_copy(b + 1, 1 - par)
                over_pairs(act, body, head=2)
                oT_copy(NB - 2)
                oT_copy(NB - 1)

            @block.vector
            def _(dve):
                dve.wait_ge(W.loaded, W.total)
                if cfg.later_mask:
                    dve.wait_ge(keep_ready, 1)

                def v_copy(b, par):
                    dve.wait_ge(v_done, b + 1)
                    need(dve, oT_done, b - 1)
                    if cfg.bias:
                        dve.tensor_tensor(v[:, par, :], p_b[:, 0:16 * HD], W["bv"][:, :], ALU.add).then_inc(v_ready, 1)
                    else:
                        dve.tensor_copy(v[:, par, :], p_b[:, 0:16 * HD]).then_inc(v_ready, 1)

                def shifts(b, gr):
                    n = count(b, NG, gr)
                    par = gr % 2
                    dve.wait_ge(scores_done, n + 1)
                    dve.tensor_reduce(max_neg[:, par, :], p_s[gr][:, :].rearrange("p (h k) -> p h k", k=S), X_AXIS, ALU.max, negate=True).then_inc(max_ready, 1)
                    dve.wait_ge(max_ready, n + 1)
                    need(dve, ex_ready, n - 1)
                    dve.tensor_scalar(shift[:, par, :], max_neg[:, par, :], cfg.scale, None, ALU.mult).then_inc(shift_ready, 1)

                def invert(b, gr):
                    n = count(b, NG, gr)
                    dve.wait_ge(ex_ready, n + 1)
                    need(dve, probs_ready, n - 1)
                    dve.reciprocal(rden[:, gr % 2, :], sums[:, gr % 2, :]).then_inc(rden_ready, 1)

                def probsT_copy(b, gr, par):
                    dve.wait_ge(probsT_done, count(b, NG, gr + 1))
                    need(dve, oT_done, b - 1)
                    to = probsT[:, par * NG + gr, :]
                    if cfg.later_mask:
                        dve.tensor_tensor(to.rearrange("p (h q) -> p h q", q=S), p_t[:, :].rearrange("p (h q) -> p h q", q=S),
                                          keep[:, :].rearrange("p (a q) -> p a q", a=1).broadcast_to([128, G4, S]), ALU.mult).then_inc(probsT_ready, 1)
                    else:
                        dve.tensor_copy(to, p_t[:, :]).then_inc(probsT_ready, 1)

                def finish(b, gr):
                    if gr == 0:
                        dve.wait_ge(y_done, b + 1)
                        need(dve, res2_ready, b)
                        dve.tensor_tensor(res[:, :], p_b[:, 0:DM], cols(residual, b, DM), ALU.add).then_inc(res_ready, 1)
                    if gr == 1:
                        src = res2[:, :] if cfg.name == "h_" else cols(g.xo, b, DM)
                        g.wait_apart(dve, res2_ready, b + 1)
                        norm.dve_moments(dve, b, 0, src)
                    if gr == 3:
                        src, dst = (res2[:, :], g.x1) if cfg.name == "h_" else (cols(g.xo, b, DM), g.nx)
                        norm.dve_scale(dve, b, 0, cols(dst, b, DM), src).then_inc(out_ready, 1)

                v_copy(0, 0)

                def body(b, par, first, last):
                    for gr in range(NG):
                        if not first or gr >= 1:
                            invert(*back(b, gr - 1, NG))
                        shifts(b, gr)
                        if not first or gr >= 2:
                            probsT_copy(*back(b, gr - 2, NG), par if gr >= 2 else 1 - par)
                        if not early(b):
                            finish(b - 2, gr)
                        if gr == 3 and not last:
                            v_copy(b + 1, 1 - par)
                over_pairs(dve, body, head=2)
                invert(NB - 1, NG - 1)
                for gr in (NG - 2, NG - 1):
                    probsT_copy(NB - 1, gr, 1)
                for b in (NB - 2, NB - 1):
                    for gr in range(NG):
                        finish(b, gr)
                dve.wait_ge(out_ready, NB)

            @block.tensor
            def _(pe):
                pe.wait_ge(W.loaded, W.total)
                pe.wait_ge(g.setup_done, 1)

                def transpose_in(b):
                    need(pe, k_ready, b)
                    if cfg.own_keys:
                        pe.wait_ge(x_ready, b + 1)
                        pe.transpose(p_a[:, 0:S], x_in[:, :], g.ident[:, :]).then_inc(T_done, 1)
                    else:
                        pe.wait_ge(x_ready, count(b, 2, 2))
                        pe.transpose(p_a[:, 0:S], x_in[:, :], g.ident[:, :])
                        pe.transpose(p_a[0:DC, S:2 * S], y_in[:, :], g.ident[:, :]).then_inc(T_done, 1)

                def project_q(b):
                    pe.wait_ge(T_ready, b + 1)
                    if isinstance(b, int) and b < 3:
                        need(pe, v_ready, b)
                    need(pe, res_ready, b - 2)
                    for c in range(4):
                        ins = pe.matmul(p_b[:, c * S:(c + 1) * S], W["wq"][:, c * 128:(c + 1) * 128], xT[:, :], start=True, stop=True)
                    ins.then_inc(q_done, 1)

                def project_k(b):
                    pe.wait_ge(T_ready, b + 1)
                    for c in range(4):
                        ins = pe.matmul(p_a[:, c * S:(c + 1) * S], W["wk"][0:kvw, c * 128:(c + 1) * 128], yT[0:kvw, :], start=True, stop=True)
                    ins.then_inc(k_done, 1)

                def project_v(b):
                    pe.wait_ge(q_ready, b + 1)
                    pe.matmul(p_b[:, 0:16 * HD], yT[0:kvw, :], W["wv"][0:kvw, :], start=True, stop=True).then_inc(v_done, 1)

                def score(b, gr, par):
                    n = count(b, NG, gr)
                    if gr == 0:
                        pe.wait_ge(q_ready, b + 1)
                        pe.wait_ge(k_ready, b + 1)
                    need(pe, ex_ready, n - 3)
                    for c in range(4):
                        r = 32 * gr
                        ins = pe.matmul(p_s[gr][:, c * S:(c + 1) * S], qT[r:r + 32, par, c * S:(c + 1) * S], kT[r:r + 32, par, c * S:(c + 1) * S],
                                        start=True, stop=True, tile_position=(r, 0))
                    ins.then_inc(scores_done, 1)

                def transpose_probs(b, gr):
                    n = count(b, NG, gr)
                    pe.wait_ge(probs_ready, n + 1)
                    need(pe, probsT_ready, n)
                    for j in range(G4):
                        ins = pe.transpose(p_t[:, j * S:(j + 1) * S], probs[:, gr % 2, j * S:(j + 1) * S], g.ident[:, :])
                    ins.then_inc(probsT_done, 1)

                def weigh(b, half, par):
                    if half == 0:
                        pe.wait_ge(v_ready, b + 1)
                        pe.wait_ge(probsT_ready, count(b, NG, NG))
                        need(pe, oT_ready, b)
                    for c in (2 * half, 2 * half + 1):
                        for j in range(G4):
                            h = 4 * c + j
                            ins = pe.matmul(p_o[j * HD:(j + 1) * HD, c * S:(c + 1) * S], v[:, par, h * HD:(h + 1) * HD],
                                            probsT[:, par * NG + j, c * S:(c + 1) * S], start=True, stop=True)
                    if half == 1:
                        ins.then_inc(oT_done, 1)

                def project_o(b):
                    pe.wait_ge(oT_ready, b + 1)
                    if b_known_last(b):
                        pe.wait_ge(v_ready, NB)
                        need(pe, res_ready, b)
                    else:
                        pe.wait_ge(v_ready, b + 3)
                    for c in range(OC):
                        ins = pe.matmul(p_b[:, 0:DM], oT[:, c * S:(c + 1) * S], W["wo"][:, c * DM:(c + 1) * DM], start=(c == 0), stop=(c == OC - 1))
                    ins.then_inc(y_done, 1)

                def b_known_last(b):
                    return isinstance(b, int) and b + 3 > NB

                transpose_in(0)
                project_q(0)
                project_k(0)
                project_v(0)

                def body(b, par, first, last):
                    for gr in range(NG):
                        score(b, gr, par)
                        if gr == 0 and not last:
                            transpose_in(b + 1)
                        if not first or gr >= 2:
                            transpose_probs(*back(b, gr - 2, NG))
                        if gr == 0 and not early(b):
                            project_o(b - 2)
                        if gr == 1 and not last:
                            project_q(b + 1)
                        if gr == 2 and not last:
                            project_k(b + 1)
                        if gr >= 2 and not first:
                            weigh(b - 1, gr - 2, 1 - par)
                        if gr == 3 and not last:
                            project_v(b + 1)
                over_pairs(pe, body)
                project_o(NB - 2)
                for gr in (NG - 2, NG - 1):
                    transpose_probs(NB - 1, gr)
                for half in (0, 1):
                    weigh(NB - 1, half, 1)
                project_o(NB - 1)


BB = 4
NBK = NB // BB


class NormBlock:

    def __init__(self, g, name, per, ctx):
        nc = g.nc
        self.g, self.per = g, per
        sb = lambda n, w: ctx.enter_context(nc.sbuf_tensor(name + n, [128, per, BB, w], F32))
        self.stats, self.mv, self.var_eps, self.rstd = sb("_stats", 6), sb("_mean_var", 2), sb("_var_eps", 1), sb("_rstd", 1)
        self.stats_done, self.moments = g.sem(name + "_stats_done"), g.sem(name + "_moments_ready")
        self.eps_added, self.rstd_ready = g.sem(name + "_eps_added"), g.sem(name + "_rstd_ready")

    def dve_moments(self, dve, i, n, src):
        done = count(i, self.per, n + 1)
        for k in range(BB):
            ins = dve.bn_stats(self.stats[:, n, k, :], src[:, k * DM:(k + 1) * DM])
        ins.then_inc(self.stats_done, 1)
        self.g.wait_apart(dve, self.stats_done, done)
        for k in range(BB):
            ins = dve.bn_aggr(self.mv[:, n, k, :], self.stats[:, n, k, :])
        ins.then_inc(self.moments, 1)

    def pool_rstd(self, pool, i, n):
        done = count(i, self.per, n + 1)
        four = lambda tile: tile[:, :].rearrange("p (a k) -> p a k", a=1).broadcast_to([128, BB, 1])
        pool.wait_ge(self.moments, done)
        pool.tensor_tensor(self.var_eps[:, n], self.mv[:, n, :, 1:2], four(self.g.eps), ALU.add).then_inc(self.eps_added, 1)
        pool.wait_ge(self.eps_added, done)
        pool.tensor_tensor(self.rstd[:, n], self.var_eps[:, n], four(self.g.minus_half), ALU.pow).then_inc(self.rstd_ready, 1)

    def dve_scale(self, dve, i, n, out, src):
        dve.wait_ge(self.rstd_ready, count(i, self.per, n + 1))
        for k in range(BB):
            ins = dve.tensor_scalar(out[:, k * DM:(k + 1) * DM], src[:, k * DM:(k + 1) * DM], self.mv[:, n, k, 0:1], self.rstd[:, n, k, 0:1],
                                    ALU.subtract, ALU.mult)
        return ins


def over_blocks(eng, body, ahead=1):
    for i in range(ahead):
        body(i, i == 0, False)
    with eng.Fori(ahead, NBK - 1) as i:
        body(i, False, False)
    body(NBK - 1, False, True)


def block_cols(tile, i):
    return cols(tile, i, BB * DM)


def mlp(g, name):
    nc = g.nc
    FC = 4
    quantum, two_norms = name == "i_", name == "c_"
    LAG = 3 if quantum else 2
    W = g.weights[name]
    PI = 3.14159274101257324
    TURN_HI, TURN_LO = 6.28125, 0.0019353071795864769
    ROUND = 1.5 * 2.0 ** 23
    with ExitStack() as ctx:
        sb = lambda n, shape, dt=F32: g.sb(name + n, shape, dt, ctx)
        x_in, xT = sb("x_in", [128, BB * DM]), sb("xT", [128, BB * S])
        hidden = sb("hidden", [128, FC, BB * S])
        res, sum1, sum2, sum3 = (sb(n, [128, BB * DM]) for n in ("res", "sum1", "sum2", "sum3"))
        n1, n1g = sb("n1", [128, BB * DM]), sb("n1g", [128, BB * DM])
        p_t, h0, h1, p_y = g.banks([name + n for n in ("pt", "h0", "h1", "py")], ctx)
        p_h = [h0, h1]
        norm = NormBlock(g, name + "ln", 2 if two_norms else 1, ctx)
        sem = lambda n: g.sem(name + n)
        x_ready, T_done, T_ready, h_done, h_ready, y_done = (sem(n) for n in ("x_ready", "T_done", "T_ready", "h_done", "h_ready", "y_done"))
        res_ready, sum1_ready, sum2_ready, sum3_ready = (sem(n) for n in ("res_ready", "sum1_ready", "sum2_ready", "sum3_ready"))
        n1_ready, n1g_ready, xc_ready, out_ready = (sem(n) for n in ("n1_ready", "n1g_ready", "xc_ready", "out_ready"))
        total = sum1 if quantum else sum2 if two_norms else sum3
        total_ready = sum1_ready if quantum else sum2_ready if two_norms else sum3_ready
        if quantum:
            pre, arg, turns, turns_i, arg1, arg2, arg3, sine, mixed = (
                sb(n, [128, 2, BB * S]) for n in ("pre", "arg", "turns", "turns_i", "arg1", "arg2", "arg3", "sine", "mixed"))
            small = {n: sb("k_" + n, [128, FC]) for n in ("turns", "turns_i", "r1", "r2", "r3", "neg", "abs", "cos_arg", "sin", "cos", "sw", "cw", "phase", "phase_w", "coef", "b_tenth", "offset", "half_pi")}
            k_step, coef_ready, pre_done, arg_done, turns_done, turns_i_done, arg1_done, arg2_done, arg3_done, sine_done, mixed_done = (
                sem(n) for n in ("k_step", "coef_ready", "pre_done", "arg_done", "turns_done", "turns_i_done", "arg1_done", "arg2_done", "arg3_done", "sine_done", "mixed_done"))

        with nc.Block() as block:
            @block.gpsimd
            def _(pool):
                pool.wait_ge(W.loaded, W.total)
                wide = lambda tile: tile[:, :].rearrange("p (a n) -> p a n", a=1).broadcast_to([128, BB, DM])
                four = lambda tile: tile.rearrange("p (k n) -> p k n", n=DM)

                def copy_in(i):
                    g.wait_apart(pool, T_done, i)
                    pool.tensor_copy(x_in[:, :], block_cols(g.x1 if quantum else g.nx, i)).then_inc(x_ready, 1)

                def finish(i, between, second):
                    pool.wait_ge(res_ready, i + 1)
                    need(pool, out_ready if quantum else sum2_ready, i)
                    pool.tensor_tensor(four(sum1[:, :]), four(res[:, :]), wide(W["b2"]), ALU.add).then_inc(sum1_ready, 1)
                    if not quantum:
                        g.wait_apart(pool, sum1_ready, i + 1)
                        need(pool, n1_ready if two_norms else sum3_ready, i)
                        pool.tensor_tensor(sum2[:, :], sum1[:, :], block_cols(g.xc, i), ALU.add).then_inc(sum2_ready, 1)
                    if name == "e_":
                        g.wait_apart(pool, sum2_ready, i + 1)
                        need(pool, out_ready, i)
                        pool.tensor_tensor(sum3[:, :], sum2[:, :], block_cols(g.x1, i), ALU.add).then_inc(sum3_ready, 1)
                    between()
                    if second:
                        norm.pool_rstd(pool, i - 1, 1)
                    norm.pool_rstd(pool, i, 0)
                    if two_norms:
                        pool.wait_ge(n1_ready, i + 1)
                        need(pool, xc_ready, i)
                        pool.tensor_tensor(four(n1g[:, :]), four(n1[:, :]), wide(W["ln_g"]), ALU.mult).then_inc(n1g_ready, 1)
                        g.wait_apart(pool, n1g_ready, i + 1)
                        pool.tensor_tensor(four(block_cols(g.xc, i)), four(n1g[:, :]), wide(W["ln_b"]), ALU.add).then_inc(xc_ready, 1)

                copy_in(0)
                copy_in(1)

                def body(i, first, last):
                    def next_in():
                        if not (isinstance(i, int) and i + 2 >= NBK):
                            copy_in(i + 2)
                    if first:
                        next_in()
                    else:
                        finish(i - 1, next_in, two_norms and not (isinstance(i, int) and i < 2))
                body(0, True, False)
                body(1, False, False)
                with pool.Fori(2, NBK - 2) as i:
                    body(i, False, False)
                body(NBK - 2, False, False)
                body(NBK - 1, False, True)
                finish(NBK - 1, lambda: None, two_norms)
                if two_norms:
                    norm.pool_rstd(pool, NBK - 1, 1)

            @block.scalar
            def _(act):
                act.wait_ge(W.loaded, W.total)

                def T_copy(i):
                    act.wait_ge(T_done, i + 1)
                    need(act, h_done, count(i, FC, 0))
                    if quantum:
                        act.activation(xT[:, :], p_t[:, :], ACT.Copy).then_inc(T_ready, 1)
                    else:
                        act.activation(xT[:, :], p_t[:, :], ACT.Identity, scale=W["gx"][:, 0:1], bias=W["bx"][:, 0:1]).then_inc(T_ready, 1)

                def gelu(i, f):
                    n = count(i, FC, f)
                    act.wait_ge(h_done, n + 1)
                    need(act, y_done, n - 3)
                    act.activation(hidden[:, f, :], p_h[f % 2][:, :], ACT.Gelu, bias=W["b1"][:, f:f + 1]).then_inc(h_ready, 1)

                def pre_sine(i, f):
                    n = count(i, FC, f)
                    act.wait_ge(h_done, n + 1)
                    need(act, arg1_done, n - 1)
                    act.activation(arg[:, f % 2, :], p_h[f % 2][:, :], ACT.Identity, scale=0.1, bias=small["offset"][:, f:f + 1]).then_inc(arg_done, 1)

                def pre_mix(i, f):
                    n = count(i, FC, f)
                    need(act, mixed_done, n - 1)
                    act.activation(pre[:, f % 2, :], p_h[f % 2][:, :], ACT.Identity, bias=W["b1"][:, f:f + 1]).then_inc(pre_done, 1)

                def post_sine(i, f):
                    n = count(i, FC, f)
                    act.wait_ge(arg3_done, n + 1)
                    need(act, mixed_done, n - 1)
                    act.activation(sine[:, f % 2, :], arg3[:, f % 2, :], ACT.Sin).then_inc(sine_done, 1)

                def relu(i, f):
                    n = count(i, FC, f)
                    act.wait_ge(mixed_done, n + 1)
                    need(act, y_done, n - 3)
                    act.activation(hidden[:, f, :], mixed[:, f % 2, :], ACT.Relu).then_inc(h_ready, 1)

                if quantum:
                    act.wait_ge(k_step, 6)
                    act.activation(small["sin"][:, :], small["r3"][:, :], ACT.Sin).then_inc(k_step, 1)
                    act.wait_ge(k_step, 10)
                    act.activation(small["cos"][:, :], small["cos_arg"][:, :], ACT.Sin).then_inc(k_step, 1)
                    act.wait_ge(coef_ready, 1)
                T_copy(0)

                def body(i, first, last):
                    for f in range(FC):
                        if quantum:
                            pre_sine(i, f)
                            if not first or f >= 1:
                                post_sine(*back(i, f - 1, FC))
                            pre_mix(i, f)
                            if not first or f >= 2:
                                relu(*back(i, f - 2, FC))
                        else:
                            gelu(i, f)
                        if f == 3 and not last:
                            T_copy(i + 1)
                over_blocks(act, body, ahead=2)
                if quantum:
                    post_sine(NBK - 1, FC - 1)
                    relu(NBK - 1, FC - 2)
                    relu(NBK - 1, FC - 1)

            @block.vector
            def _(dve):
                dve.wait_ge(W.loaded, W.total)

                def reduce_arg(a, n, turns, turns_i, r1, r2, r3, sems):
                    dve.tensor_scalar(turns, a, 1.0 / (2.0 * PI), ROUND, ALU.mult, ALU.add).then_inc(sems[0], 1)
                    dve.wait_ge(sems[0], n[0])
                    dve.tensor_scalar(turns_i, turns, ROUND, None, ALU.subtract).then_inc(sems[1], 1)
                    dve.wait_ge(sems[1], n[1])
                    dve.scalar_tensor_tensor(out=r1, in0=turns_i, scalar=-TURN_HI, in1=a, op0=ALU.mult, op1=ALU.add).then_inc(sems[2], 1)
                    dve.wait_ge(sems[2], n[2])
                    dve.scalar_tensor_tensor(out=r2, in0=turns_i, scalar=-TURN_LO, in1=r1, op0=ALU.mult, op1=ALU.add).then_inc(sems[3], 1)
                    dve.wait_ge(sems[3], n[3])

                if quantum:
                    theta, wr, wi = W["theta"], W["wr"], W["wi"]
                    k = small
                    reduce_arg(theta[:, :], (1, 2, 3, 4), k["turns"][:, :], k["turns_i"][:, :], k["r1"][:, :], k["r2"][:, :], k["r3"][:, :], (k_step,) * 4)
                    dve.memset(k["half_pi"][:, :], PI / 2).then_inc(k_step, 1)
                    dve.tensor_scalar(k["r3"][:, :], k["r2"][:, :], -PI, PI, ALU.max, ALU.min).then_inc(k_step, 1)
                    dve.wait_ge(k_step, 7)
                    dve.tensor_scalar(k["neg"][:, :], k["r3"][:, :], -1.0, None, ALU.mult).then_inc(k_step, 1)
                    dve.wait_ge(k_step, 8)
                    dve.tensor_tensor(k["abs"][:, :], k["r3"][:, :], k["neg"][:, :], ALU.max).then_inc(k_step, 1)
                    dve.wait_ge(k_step, 9)
                    dve.tensor_tensor(k["cos_arg"][:, :], k["half_pi"][:, :], k["abs"][:, :], ALU.subtract).then_inc(k_step, 1)
                    dve.wait_ge(k_step, 11)
                    dve.tensor_tensor(k["cw"][:, :], k["cos"][:, :], wr[:, :], ALU.mult).then_inc(k_step, 1)
                    dve.tensor_tensor(k["sw"][:, :], k["sin"][:, :], wi[:, :], ALU.mult).then_inc(k_step, 1)
                    dve.tensor_scalar(k["b_tenth"][:, :], W["b1"][:, :], 0.1, None, ALU.mult).then_inc(k_step, 1)
                    dve.wait_ge(k_step, 14)
                    dve.tensor_tensor(k["phase"][:, :], k["cw"][:, :], k["sw"][:, :], ALU.add).then_inc(k_step, 1)
                    dve.tensor_tensor(k["offset"][:, :], k["b_tenth"][:, :], theta[:, :], ALU.add).then_inc(k_step, 1)
                    dve.wait_ge(k_step, 16)
                    dve.tensor_tensor(k["phase_w"][:, :], k["phase"][:, :], wi[:, :], ALU.mult).then_inc(k_step, 1)
                    dve.wait_ge(k_step, 17)
                    dve.tensor_scalar(k["coef"][:, :], k["phase_w"][:, :], 0.1, None, ALU.mult).then_inc(coef_ready, 1)
                    dve.wait_ge(coef_ready, 1)

                def reduce_range(i, f):
                    n = count(i, FC, f) + 1
                    r = f % 2
                    dve.wait_ge(arg_done, n)
                    reduce_arg(arg[:, r, :], (n, n, n, n), turns[:, r, :], turns_i[:, r, :], arg1[:, r, :], arg2[:, r, :], None,
                               (turns_done, turns_i_done, arg1_done, arg2_done))
                    need(dve, sine_done, n - 2)
                    dve.tensor_scalar(arg3[:, r, :], arg2[:, r, :], -PI, PI, ALU.max, ALU.min).then_inc(arg3_done, 1)

                def mix(i, f):
                    n = count(i, FC, f) + 1
                    r = f % 2
                    dve.wait_ge(sine_done, n)
                    need(dve, h_ready, n - 2)
                    dve.scalar_tensor_tensor(out=mixed[:, r, :], in0=sine[:, r, :], scalar=small["coef"][:, f:f + 1], in1=pre[:, r, :],
                                             op0=ALU.mult, op1=ALU.add).then_inc(mixed_done, 1)

                def project_read(i):
                    dve.wait_ge(y_done, count(i, FC, FC))
                    need(dve, sum1_ready, i)
                    dve.tensor_tensor(res[:, :], p_y[:, :], block_cols(g.x1 if quantum else g.xo, i), ALU.add).then_inc(res_ready, 1)

                def norm1(i):
                    g.wait_apart(dve, total_ready, i + 1)
                    norm.dve_moments(dve, i, 0, total[:, :])

                def norm2(i):
                    if two_norms:
                        need(dve, n1g_ready, i)
                        norm.dve_scale(dve, i, 0, n1[:, :], total[:, :]).then_inc(n1_ready, 1)
                    else:
                        norm.dve_scale(dve, i, 0, block_cols(g.x1, i), total[:, :]).then_inc(out_ready, 1)

                def second_moments(i):
                    g.wait_apart(dve, xc_ready, i + 1)
                    norm.dve_moments(dve, i, 1, block_cols(g.xc, i))

                def second_scale(i):
                    norm.dve_scale(dve, i, 1, block_cols(g.nx, i), block_cols(g.xc, i)).then_inc(out_ready, 1)

                def body(i, first, last):
                    for f in range(FC):
                        if not first and quantum and f == FC - 1:
                            norm1(i - 1)
                        if quantum:
                            reduce_range(i, f)
                            if not first or f >= 1:
                                mix(*back(i, f - 1, FC))
                        if not first:
                            if f == LAG - 1:
                                project_read(i - 1)
                            second = two_norms and not (isinstance(i, int) and i < 2)
                            if f == 2 and second:
                                second_moments(i - 2)
                            if f == 2 and not quantum:
                                norm1(i - 1)
                            if f == 3 and second:
                                second_scale(i - 2)
                            if f == 3:
                                norm2(i - 1)
                over_blocks(dve, body, ahead=2)
                if quantum:
                    mix(NBK - 1, FC - 1)
                project_read(NBK - 1)
                if two_norms:
                    second_moments(NBK - 2)
                norm1(NBK - 1)
                if two_norms:
                    second_scale(NBK - 2)
                norm2(NBK - 1)
                if two_norms:
                    second_moments(NBK - 1)
                    second_scale(NBK - 1)
                dve.wait_ge(out_ready, NBK)

            @block.tensor
            def _(pe):
                pe.wait_ge(W.loaded, W.total)
                pe.wait_ge(g.setup_done, 1)

                def transpose_in(i):
                    pe.wait_ge(x_ready, i + 1)
                    need(pe, T_ready, i)
                    for k in range(BB):
                        ins = pe.transpose(p_t[:, k * S:(k + 1) * S], x_in[:, k * DM:(k + 1) * DM], g.ident[:, :])
                    ins.then_inc(T_done, 1)

                def expand(i, f):
                    n = count(i, FC, f)
                    if f == 0:
                        pe.wait_ge(T_ready, i + 1)
                    if quantum:
                        need(pe, pre_done, n - 1)
                    else:
                        need(pe, h_ready, n - 1)
                    pe.matmul(p_h[f % 2][:, :], W["w1"][:, f * 128:(f + 1) * 128], xT[:, :], start=True, stop=True).then_inc(h_done, 1)

                def project(i, f):
                    n = count(i, FC, f)
                    if f == 0:
                        need(pe, res_ready, i)
                    pe.wait_ge(h_ready, n + 1)
                    for k in range(BB):
                        ins = pe.matmul(p_y[:, k * DM:(k + 1) * DM], hidden[:, f, k * S:(k + 1) * S], W["w2"][:, f * DM:(f + 1) * DM],
                                        start=(f == 0 and k == 0), stop=(f == FC - 1), skip_group_check=True)
                    ins.then_inc(y_done, 1)

                transpose_in(0)

                def body(i, first, last):
                    for f in range(FC):
                        expand(i, f)
                        if f == 2 and not last:
                            transpose_in(i + 1)
                        if not first or f >= LAG:
                            project(*back(i, f - LAG, FC))
                over_blocks(pe, body)
                for f in range(FC - LAG, FC):
                    project(NBK - 1, f)


def cross_mlp1(g):
    mlp(g, "c_")


def cross_mlp2(g):
    mlp(g, "e_")


def quantum_mlp(g):
    mlp(g, "i_")


NE = 8


def declare_experts(g, ctx):
    t = g.t
    w = g.weights["f_"] = Weights(g, "f_", Area(g.sb("f_weights", [128, NE * 3 * 512 + NE], F32, ctx)))
    w.tile("gate", [128, NE], t["L0_ffn_gate_wT"], lambda x: x[:, :])
    w.tile("w1", [128, NE * 512], t["L0_ffn_w1T"], lambda x: x[:, :])
    w.tile("w3", [128, NE * 512], t["L0_ffn_w3T"], lambda x: x[:, :])
    w.tile("w2", [128, NE * 512], t["L0_ffn_w2T"].rearrange("(c p) n -> p c n", p=128), lambda x: x[:, :].rearrange("p (c n) -> p c n", n=DM))


def gate(g, xT_all, weight):
    nc = g.nc
    JITTER = 0.01
    W = g.weights["f_"]
    with ExitStack() as ctx:
        sb = lambda n, shape, dt=F32: g.sb("fg_" + n, shape, dt, ctx)
        x_in, xT = sb("x_in", [128, BB * DM]), sb("xT", [128, BB * S])
        three = [128, NB, NE]
        scores, top = sb("scores", three), sb("top", three)
        place = sb("place", three, mybir.dt.uint32)
        place_f, neg, size, expert = sb("place_f", three), sb("neg", three), sb("size", three), sb("expert", three)
        dist, far, keep, chosen, up, ex, masked = (sb(n, [128, 2, NB, NE]) for n in ("dist", "far", "keep", "chosen", "up", "ex", "masked"))
        others = sb("others", three)
        total, mult = sb("total", [128, 2, NB]), sb("mult", [128, 2, NB])
        parts = sb("parts", [128, 2, NB, NE])
        p_t, p_g = g.banks(["fg_pt", "fg_pg"], ctx)
        sem = lambda n: g.sem("fg_" + n)
        x_ready, T_done, T_ready, gate_done, scores_ready, expert_ready, top_done, place_done, step, ex_ready, weight_ready = (
            sem(n) for n in ("x_ready", "T_done", "T_ready", "gate_done", "scores_ready", "expert_ready", "top_done", "place_done", "step", "ex_ready", "weight_ready"))
        all_copied = sem("all_copied")
        with nc.Block() as block:
            @block.sync
            def _(sp):
                g.issue_next(sp)

            @block.gpsimd
            def _(pool):
                pool.iota(expert[:, :, :], [[0, NB], [1, NE]], base=0, channel_multiplier=0, allow_small_or_imprecise_dtypes=True).then_inc(expert_ready, 1)
                def copy_in(i, first, last):
                    g.wait_apart(pool, T_done, i)
                    pool.tensor_copy(x_in[:, :], block_cols(g.x1, i)).then_inc(x_ready, 1)
                over_blocks(pool, copy_in)

            @block.scalar
            def _(act):
                def body(i, first, last):
                    act.wait_ge(T_done, i + 1)
                    need(act, gate_done, i)
                    need(act, all_copied, i)
                    act.activation(xT[:, :], p_t[:, :], ACT.Copy).then_inc(T_ready, 1)
                over_blocks(act, body)
                act.wait_ge(step, EXP_STEP)
                act.activation(ex[:, :, :, :], up[:, :, :, :], ACT.Exp, scale=-1.0).then_inc(ex_ready, 1)

            @block.tensor
            def _(pe):
                pe.wait_ge(W.loaded, W.total)
                pe.wait_ge(g.setup_done, 1)

                def transpose_in(i):
                    pe.wait_ge(x_ready, i + 1)
                    need(pe, T_ready, i)
                    for k in range(BB):
                        ins = pe.transpose(p_t[:, k * S:(k + 1) * S], x_in[:, k * DM:(k + 1) * DM], g.ident[:, :])
                    ins.then_inc(T_done, 1)

                def body(i, first, last):
                    if not last:
                        transpose_in(i + 1)
                    pe.wait_ge(T_ready, i + 1)
                    need(pe, scores_ready, i)
                    for k in range(BB):
                        ins = pe.matmul(p_g[:, k * NE:(k + 1) * NE], xT[:, k * S:(k + 1) * S], W["gate"][:, :], start=True, stop=True)
                    ins.then_inc(gate_done, 1)
                transpose_in(0)
                over_blocks(pe, body)

            @block.vector
            def _(dve):
                with dve.Fori(0, NBK) as i:
                    g.wait_apart(dve, T_ready, i + 1)
                    dve.tensor_copy(block_cols(xT_all, i), xT[:, :]).then_inc(all_copied, 1)
                    g.wait_apart(dve, gate_done, i + 1)
                    dve.tensor_copy(cols(scores[:, :, :].rearrange("p b e -> p (b e)"), i, BB * NE), p_g[:, 0:BB * NE]).then_inc(scores_ready, 1)
                dve.wait_ge(all_copied, NBK)
                dve.wait_ge(scores_ready, NBK)
                for b in range(NB):
                    dve.max(top[:, b, :], scores[:, b, :]).then_inc(top_done, 1)
                dve.wait_ge(top_done, NB)
                for b in range(NB):
                    dve.max_index(place[:, b, :], top[:, b, :], scores[:, b, :]).then_inc(place_done, 1)
                dve.wait_ge(place_done, NB)
                dve.wait_ge(expert_ready, 1)
                bc = lambda tile, n: tile[:, :, n:n + 1].broadcast_to(three)
                steps = [0]

                def then(ins):
                    steps[0] += 1
                    ins.then_inc(step, 1)
                    dve.wait_ge(step, steps[0])

                then(dve.tensor_copy(place_f[:, :, :], place[:, :, :]))
                then(dve.tensor_scalar(neg[:, :, :], scores[:, :, :], -1.0, None, ALU.mult))
                then(dve.tensor_tensor(size[:, :, :], scores[:, :, :], neg[:, :, :], ALU.max))
                for n in (0, 1):
                    then(dve.tensor_tensor(chosen[:, n], expert[:, :, :], bc(place_f, n), ALU.is_equal))
                    then(dve.tensor_tensor(dist[:, n], bc(top, n), scores[:, :, :], ALU.subtract))
                    then(dve.tensor_tensor(far[:, n], size[:, :, :], bc(top, n), ALU.max))
                then(dve.scalar_tensor_tensor(out=keep[:, :, :, :].rearrange("p n b e -> p (n b e)"), in0=far[:, :, :, :].rearrange("p n b e -> p (n b e)"),
                                              scalar=2 * JITTER, in1=dist[:, :, :, :].rearrange("p n b e -> p (n b e)"), op0=ALU.mult, op1=ALU.is_ge))
                then(dve.tensor_scalar(others[:, :, :], chosen[:, 0], -1.0, 1.0, ALU.mult, ALU.add))
                then(dve.tensor_tensor(masked[:, 1], keep[:, 1], others[:, :, :], ALU.mult))
                then(dve.tensor_copy(masked[:, 0], keep[:, 0]))
                then(dve.tensor_scalar(up[:, :, :, :], dist[:, :, :, :], 0.0, None, ALU.max))
                assert steps[0] == EXP_STEP
                dve.wait_ge(ex_ready, 1)
                then(dve.tensor_tensor(parts[:, :, :, :], masked[:, :, :, :], ex[:, :, :, :], ALU.mult))
                then(dve.tensor_reduce(total[:, :, :], parts[:, :, :, :], X_AXIS, ALU.add))
                then(dve.reciprocal(mult[:, :, :], total[:, :, :]))
                for n in (0, 1):
                    then(dve.tensor_tensor(dist[:, n], chosen[:, n], mult[:, n, :].rearrange("p (b a) -> p b a", a=1).broadcast_to(three), ALU.mult))
                dve.tensor_tensor(weight[:, :, :], dist[:, 0], dist[:, 1], ALU.add).then_inc(weight_ready, 1)
                dve.wait_ge(weight_ready, 1)


EXP_STEP = 14


def experts(g):
    nc = g.nc
    FC = 4
    NM = NE * FC
    W = g.weights["f_"]
    with ExitStack() as ctx:
        sb = lambda n, shape, dt=F32: g.sb("f_" + n, shape, dt, ctx)
        xT_all = g.xo
        weight = sb("weight", [128, NB, NE])
        gate(g, xT_all, weight)
        act_a, hidden = sb("act_a", [128, 2, BB * S]), sb("hidden", [128, FC, BB * S])
        w_now = sb("w_now", [128, BB * NE])
        weighed, acc = sb("weighed", [128, 2, BB * DM]), sb("acc", [128, 2, BB * DM])
        total = sb("total", [128, BB * DM])
        a0, a1, b0, b1, y0, y1 = g.banks(["f_" + n for n in ("a0", "a1", "b0", "b1", "y0", "y1")], ctx)
        p_a, p_b, p_y = [a0, a1], [b0, b1], [y0, y1]
        norm = NormBlock(g, "f_ln", 1, ctx)
        sem = lambda n: g.sem("f_" + n)
        a_done, b_done, silu_ready, h_ready, y_done, weighed_ready, acc_ready, total_ready, out_ready = (
            sem(n) for n in ("a_done", "b_done", "silu_ready", "h_ready", "y_done", "weighed_ready", "acc_ready", "total_ready", "out_ready"))
        w_ready = sem("w_ready")

        with nc.Block() as block:
            @block.gpsimd
            def _(pool):
                def weights_of(i):
                    g.wait_apart(pool, weighed_ready, count(i, NE, 0))
                    pool.tensor_copy(w_now[:, :], cols(weight[:, :, :].rearrange("p b e -> p (b e)"), i, BB * NE)).then_inc(w_ready, 1)

                def body(i, first, last):
                    weights_of(i)
                    for e in range(NE):
                        n = count(i, NE, e)
                        if e == 0:
                            if not first:
                                pool.wait_ge(total_ready, i)
                            g.wait_apart(pool, weighed_ready, n + 1)
                            pool.tensor_tensor(acc[:, 0, :], weighed[:, 0, :], block_cols(g.x1, i), ALU.add).then_inc(acc_ready, 1)
                            if not first:
                                norm.pool_rstd(pool, i - 1, 0)
                        else:
                            pool.wait_ge(weighed_ready, n + 1)
                            pool.wait_ge(acc_ready, n)
                            pool.tensor_tensor(acc[:, e % 2, :], weighed[:, e % 2, :], acc[:, 1 - e % 2, :], ALU.add).then_inc(acc_ready, 1)
                over_blocks(pool, body)
                norm.pool_rstd(pool, NBK - 1, 0)

            @block.scalar
            def _(act):
                def body(i, first, last):
                    for m in range(NM):
                        n = count(i, NM, m)
                        act.wait_ge(a_done, n + 1)
                        need(act, h_ready, n - 1)
                        act.activation(act_a[:, m % 2, :], p_a[m % 2][:, :], ACT.Silu).then_inc(silu_ready, 1)
                over_blocks(act, body)

            @block.vector
            def _(dve):
                def weigh(i, e):
                    n = count(i, NE, e)
                    if e == 0:
                        dve.wait_ge(w_ready, i + 1)
                    dve.wait_ge(y_done, count(i, NM, FC * (e + 1)))
                    need(dve, acc_ready, n - 1)
                    dve.tensor_tensor(weighed[:, e % 2, :].rearrange("p (k n) -> p k n", n=DM), p_y[e % 2][:, :].rearrange("p (k n) -> p k n", n=DM),
                                      w_now[:, e:BB * NE:NE].rearrange("p (k a) -> p k a", a=1).broadcast_to([128, BB, DM]), ALU.mult).then_inc(weighed_ready, 1)

                def finish(i, part):
                    if part == 0:
                        dve.wait_ge(acc_ready, count(i, NE, NE))
                        need(dve, out_ready, i)
                        dve.tensor_copy(total[:, :], acc[:, (NE - 1) % 2, :]).then_inc(total_ready, 1)
                        g.wait_apart(dve, total_ready, i + 1)
                        norm.dve_moments(dve, i, 0, total[:, :])
                    else:
                        norm.dve_scale(dve, i, 0, block_cols(g.x1, i), total[:, :]).then_inc(out_ready, 1)

                def body(i, first, last):
                    for m in range(NM):
                        n = count(i, NM, m)
                        dve.wait_ge(silu_ready, n + 1)
                        dve.wait_ge(b_done, n + 1)
                        need(dve, y_done, n - 3)
                        dve.tensor_tensor(hidden[:, m % FC, :], act_a[:, m % 2, :], p_b[m % 2][:, :], ALU.mult).then_inc(h_ready, 1)
                        if m % FC == 2 and (m >= FC or not first):
                            weigh(*back(i, m // FC - 1, NE))
                        if m == 6 and not first:
                            finish(i - 1, 0)
                        if m == 10 and not first:
                            finish(i - 1, 1)
                over_blocks(dve, body, ahead=2)
                weigh(NBK - 1, NE - 1)
                finish(NBK - 1, 0)
                finish(NBK - 1, 1)
                dve.wait_ge(out_ready, NBK)

            @block.tensor
            def _(pe):
                def expand(i, m):
                    n = count(i, NM, m)
                    xT = block_cols(xT_all, i)
                    for w, bank, free, done in (("w1", p_a, silu_ready, a_done), ("w3", p_b, h_ready, b_done)):
                        need(pe, free, n - 1)
                        pe.matmul(bank[m % 2][:, :], W[w][:, m * 128:(m + 1) * 128], xT, start=True, stop=True).then_inc(done, 1)

                def project(i, m):
                    n = count(i, NM, m)
                    e, f = m // FC, m % FC
                    if f == 0:
                        need(pe, weighed_ready, count(i, NE, e - 1))
                    pe.wait_ge(h_ready, n + 1)
                    for k in range(BB):
                        ins = pe.matmul(p_y[e % 2][:, k * DM:(k + 1) * DM], hidden[:, f, k * S:(k + 1) * S], W["w2"][:, m * DM:(m + 1) * DM],
                                        start=(f == 0 and k == 0), stop=(f == FC - 1), skip_group_check=True)
                    ins.then_inc(y_done, 1)

                def body(i, first, last):
                    for m in range(NM):
                        expand(i, m)
                        if not first or m >= 2:
                            project(*back(i, m - 2, NM))
                over_blocks(pe, body)
                project(NBK - 1, NM - 2)
                project(NBK - 1, NM - 1)


RH, RD, RT = 16, 8, NB
SG = 4
RMAX = 16


def relative_attention(g):
    nc = g.nc
    by_place = nc.dram_tensor("distance_scores", [S, RT, RH * RT], F32, kind="Internal").ap()
    probs_dram = nc.dram_tensor("distance_probs", [S, RT, RH * RT], F32, kind="Internal").ap()
    distance_scores(g, g.xo, by_place)
    group_attention(g, g.xo, g.xc, by_place, probs_dram)
    distance_values(g, g.xc, probs_dram)


def distance_scores(g, xT_all, scores_dram):
    nc = g.nc
    W = g.weights["g_"]
    SCALE = RD ** -0.5
    with ExitStack() as ctx:
        sb = lambda n, shape, dt=F32: g.sb("g1_" + n, shape, dt, ctx)
        x_in, xT, qT = sb("x_in", [128, BB * DM]), sb("xT", [128, BB * S]), sb("qT", [128, BB * S])
        out = sb("out", [128, BB, RH * RT])
        p_t, p_q, *p_d = g.banks(["g1_pt", "g1_pq", "g1_d0", "g1_d1", "g1_d2", "g1_d3"], ctx)
        sem = lambda n: g.sem("g1_" + n)
        x_ready, T_done, T_ready, copied, q_done, q_ready, d_done, d_ready = (
            sem(n) for n in ("x_ready", "T_done", "T_ready", "copied", "q_done", "q_ready", "d_done", "d_ready"))
        stored = [sem(f"stored{k}") for k in range(BB)]
        with nc.Block() as block:
            @block.sync
            def _(sp):
                with sp.Fori(0, NBK) as i:
                    for k in range(BB):
                        sp.wait_ge(d_ready, i * BB + k + 1)
                        sp.dma_start(scores_dram[:, bass.ds(i * BB + k, 1), :].rearrange("s a n -> s (a n)"), out[:, k, :]).then_inc(stored[k], 16)
                for k in range(BB):
                    sp.wait_ge(stored[k], 16 * NBK)

            @block.gpsimd
            def _(pool):
                def copy_in(i, first, last):
                    g.wait_apart(pool, T_done, i)
                    pool.tensor_copy(x_in[:, :], block_cols(g.x1, i)).then_inc(x_ready, 1)
                over_blocks(pool, copy_in)

            @block.scalar
            def _(act):
                def T_copy(i):
                    act.wait_ge(T_done, i + 1)
                    need(act, q_done, i)
                    need(act, copied, i)
                    act.activation(xT[:, :], p_t[:, :], ACT.Copy).then_inc(T_ready, 1)

                def body(i, first, last):
                    if not last:
                        T_copy(i + 1)
                    for k in range(BB):
                        act.wait_ge(d_done, i * BB + k + 1)
                        need(act, stored[k], i * 16)
                        act.activation(out[:, k, :], p_d[k][:, :], ACT.Copy).then_inc(d_ready, 1)
                T_copy(0)
                over_blocks(act, body)

            @block.vector
            def _(dve):
                dve.wait_ge(W.loaded, W.total)

                def body(i, first, last):
                    dve.wait_ge(q_done, i + 1)
                    need(dve, d_done, i * BB)
                    dve.tensor_scalar(qT[:, :], p_q[:, :], W["bq"][:, 0:1], SCALE, ALU.add, ALU.mult).then_inc(q_ready, 1)
                    g.wait_apart(dve, T_ready, i + 1)
                    dve.tensor_copy(block_cols(xT_all, i), xT[:, :]).then_inc(copied, 1)
                over_blocks(dve, body)
                dve.wait_ge(copied, NBK)

            @block.tensor
            def _(pe):
                pe.wait_ge(W.loaded, W.total)
                pe.wait_ge(g.setup_done, 1)
                keys = W["keys"][:, :].rearrange("p (h u) -> p h u", u=2 * RT - 1)

                def transpose_in(i):
                    pe.wait_ge(x_ready, i + 1)
                    need(pe, T_ready, i)
                    for k in range(BB):
                        ins = pe.transpose(p_t[:, k * S:(k + 1) * S], x_in[:, k * DM:(k + 1) * DM], g.ident[:, :])
                    ins.then_inc(T_done, 1)

                def body(i, first, last):
                    pe.wait_ge(T_ready, i + 1)
                    need(pe, q_ready, i)
                    pe.matmul(p_q[:, :], W["wq"][:, :], xT[:, :], start=True, stop=True).then_inc(q_done, 1)
                    if not last:
                        transpose_in(i + 1)
                    pe.wait_ge(q_ready, i + 1)
                    for k in range(BB):
                        need(pe, d_ready, (i - 1) * BB + k + 1)
                        first_column = i * (-BB) + (RT - 1 - k)
                        seen = slice(first_column, first_column + RT) if isinstance(i, int) else bass.ds(first_column, RT)
                        pe.matmul(p_d[k][:, :].rearrange("p (h u) -> p h u", u=RT), qT[:, k * S:(k + 1) * S],
                                  keys[:, :, seen], start=True, stop=True).then_inc(d_done, 1)
                transpose_in(0)
                over_blocks(pe, body)


def group_attention(g, xT_all, oT_all, scores_dram, probs_dram):
    nc = g.nc
    W = g.weights["g_"]
    with ExitStack() as ctx:
        sb = lambda n, shape, dt=F32: g.sb("g2_" + n, shape, dt, ctx)
        xT = sb("xT", [128, 2, S])
        k = sb("k", [128, 4 * RT])
        q_own, k_own, v_own = (sb(n, [128, 2, 4 * S]) for n in ("q_own", "k_own", "v_own"))
        near = sb("near", [128, 2, BANK])
        scores, moved, ex, probs = (sb(n, [128, 2, BANK]) for n in ("scores", "moved", "ex", "probs"))
        top, total, inv = (sb(n, [128, 2, RH]) for n in ("top", "total", "inv"))
        probsT, o = sb("probsT", [128, 4 * S]), sb("o", [128, 2, S])
        p_q, p_k, p_v, p_s, p_t, p_o, p_oT = g.banks(["g2_" + n for n in ("pq", "pk", "pv", "ps", "pt", "po", "poT")], ctx)
        sem = lambda n: g.sem("g2_" + n)
        xT_ready, q_done, q_placed, k_done, k_ready, k_placed, v_zero, v_done, v_ready = (
            sem(n) for n in ("xT_ready", "q_done", "q_placed", "k_done", "k_ready", "k_placed", "v_zero", "v_done", "v_ready"))
        s_done, s_ready, top_ready, moved_ready, ex_ready, total_ready, inv_ready, probs_ready = (
            sem(n) for n in ("s_done", "s_ready", "top_ready", "moved_ready", "ex_ready", "total_ready", "inv_ready", "probs_ready"))
        t_done, t_ready, o_done, o_ready, oT_done, oT_ready = (
            sem(n) for n in ("t_done", "t_ready", "o_done", "o_ready", "oT_done", "oT_ready"))
        near_loaded = [sem(f"near_loaded{k}") for k in (0, 1)]
        stored = [sem(f"stored{k}") for k in (0, 1)]
        tokens = lambda tile: tile[:, :].rearrange("p (t s) -> p s t", s=S)

        def of_group(tile, j):
            return tokens(tile)[:, j * SG:(j + 1) * SG, :] if isinstance(j, int) else tokens(tile)[:, bass.ds(j * SG, SG), :]

        def rows(dram, j):
            part = dram[j * SG:(j + 1) * SG] if isinstance(j, int) else dram[bass.ds(j * SG, SG)]
            return part.rearrange("s t n -> (s t) n")

        with nc.Block() as block:
            @block.sync
            def _(sp):
                def store(j, par):
                    sp.wait_ge(probs_ready, j + 1)
                    sp.dma_start(rows(probs_dram, j), probs[:, par, :]).then_inc(stored[par], 16)

                for j in (0, 1):
                    sp.dma_start(near[:, j, :], rows(scores_dram, j)).then_inc(near_loaded[j], 16)
                with sp.Fori(0, NB // 2 - 1) as i:
                    for par in (0, 1):
                        store(i * 2 + par, par)
                        sp.wait_ge(s_ready, i * 2 + par + 1)
                        sp.dma_start(near[:, par, :], rows(scores_dram, i * 2 + par + 2)).then_inc(near_loaded[par], 16)
                for j in (NB - 2, NB - 1):
                    store(j, j % 2)
                for par in (0, 1):
                    sp.wait_ge(stored[par], 16 * NB // 2)

            @block.gpsimd
            def _(pool):
                def copy_in(j, par):
                    g.wait_apart(pool, v_done, j - 1)
                    pool.tensor_copy(xT[:, par, :].rearrange("p (s t) -> p s t", s=SG), of_group(xT_all, j)).then_inc(xT_ready, 1)

                def move(j, par):
                    pool.wait_ge(top_ready, j + 1)
                    need(pool, ex_ready, j - 1)
                    pool.tensor_tensor(heads(moved[:, par, :]), heads(scores[:, par, :]), per_head(top[:, par, :]), ALU.subtract).then_inc(moved_ready, 1)

                def divide(j, par, k):
                    pool.wait_ge(inv_ready, j + 1)
                    need(pool, t_done, j - 1)
                    need(pool, stored[par], k)
                    pool.tensor_tensor(heads(probs[:, par, :]), heads(ex[:, par, :]), per_head(inv[:, par, :]), ALU.mult).then_inc(probs_ready, 1)

                pool.memset(v_own[:, :, :], 0.0).then_inc(v_zero, 1)
                for j in (0, 1, 2):
                    copy_in(j, j % 2)

                def body(j, par, first, last):
                    move(j, par)
                    if not (isinstance(j, int) and j + 3 >= NB):
                        copy_in(j + 3, 1 - par)
                    divide(j, par, stored_before(j, par))
                over_pairs(pool, body, tail=2)

            @block.scalar
            def _(act):
                act.wait_ge(W.loaded, W.total)

                act.wait_ge(v_zero, 1)

                def k_copy(j):
                    act.wait_ge(k_done, j + 1)
                    need(act, k_placed, j)
                    for c in range(4):
                        ins = act.activation(k[:, c * RT:(c + 1) * RT], p_k[:, c * RT:(c + 1) * RT], ACT.Identity, bias=W["bk_rep"][:, c:c + 1])
                    ins.then_inc(k_ready, 1)

                def v_copy(j, par):
                    act.wait_ge(v_done, j + 1)
                    need(act, o_done, j - 1)
                    for i in range(4):
                        of_head = lambda tile: tile[i * RT:(i + 1) * RT].rearrange("p (a i d) -> p i a d", i=4, d=RD)[:, i]
                        ins = act.activation(of_head(v_own[:, par, :]), of_head(p_v[:, :]), ACT.Copy)
                    ins.then_inc(v_ready, 1)

                def exp(j, par):
                    act.wait_ge(moved_ready, j + 1)
                    need(act, probs_ready, j - 1)
                    act.activation(ex[:, par, :], moved[:, par, :], ACT.Exp).then_inc(ex_ready, 1)

                def probsT_copy(j):
                    act.wait_ge(t_done, j + 1)
                    need(act, o_done, j)
                    act.activation(probsT[:, :], p_t[:, :], ACT.Copy).then_inc(t_ready, 1)

                def oT_copy(j):
                    act.wait_ge(oT_done, j + 1)
                    act.activation(of_group(oT_all, j), p_oT[:, 0:S].rearrange("p (s t) -> p s t", s=SG), ACT.Identity, bias=W["bv"][:, 0:1]).then_inc(oT_ready, 1)

                k_copy(0)
                k_copy(1)
                v_copy(0, 0)

                def body(j, par, first, last):
                    if not late(j):
                        k_copy(j + 2)
                    if not first:
                        probsT_copy(j - 1)
                    exp(j, par)
                    if not last:
                        v_copy(j + 1, 1 - par)
                    if not early(j):
                        oT_copy(j - 2)
                over_pairs(act, body)
                probsT_copy(NB - 1)
                oT_copy(NB - 2)
                oT_copy(NB - 1)
                act.wait_ge(oT_ready, NB)

            @block.vector
            def _(dve):
                dve.wait_ge(W.loaded, W.total)

                def place(j, par):
                    dve.wait_ge(q_done, j + 1)
                    need(dve, s_done, j - 1)
                    for c in range(4):
                        ins = dve.scalar_tensor_tensor(out=q_own[:, par, c * S:(c + 1) * S], in0=p_q[:, c * S:(c + 1) * S], scalar=W["bq_rep"][:, c:c + 1],
                                                       in1=W["own_scaled"][:, :], op0=ALU.add, op1=ALU.mult)
                    ins.then_inc(q_placed, 1)
                    dve.wait_ge(k_ready, j + 1)
                    dve.tensor_tensor(k_own[:, par, :].rearrange("p (c i t) -> p c i t", c=4, i=4), k[:, :].rearrange("p (c a t) -> p c a t", c=4, a=1).broadcast_to([128, 4, 4, RT]),
                                      W["row_head"][:, :].rearrange("p (b i a) -> p b i a", b=1, a=1).broadcast_to([128, 4, 4, RT]), ALU.mult).then_inc(k_placed, 1)

                def add_near(j, par, k):
                    dve.wait_ge(s_done, j + 1)
                    need(dve, moved_ready, j - 1)
                    dve.wait_ge(near_loaded[par], k + 16)
                    dve.tensor_tensor(scores[:, par, :], p_s[:, :], near[:, par, :], ALU.add).then_inc(s_ready, 1)
                    dve.wait_ge(s_ready, j + 1)
                    dve.tensor_reduce(top[:, par, :], heads(scores[:, par, :]), X_AXIS, ALU.max).then_inc(top_ready, 1)

                def sum_up(j, par):
                    dve.wait_ge(ex_ready, j + 1)
                    dve.tensor_reduce(total[:, par, :], heads(ex[:, par, :]), X_AXIS, ALU.add).then_inc(total_ready, 1)
                    dve.wait_ge(total_ready, j + 1)
                    need(dve, probs_ready, j - 1)
                    dve.reciprocal(inv[:, par, :], total[:, par, :]).then_inc(inv_ready, 1)

                def o_copy(j, par):
                    dve.wait_ge(o_done, j + 1)
                    need(dve, oT_done, j - 1)
                    dve.tensor_copy(o[:, par, :], p_o[:, 0:S]).then_inc(o_ready, 1)

                place(0, 0)
                place(1, 1)

                def body(j, par, first, last):
                    if not early(j):
                        o_copy(j - 2, par)
                    add_near(j, par, stored_before(j, par))
                    if not late(j):
                        place(j + 2, par)
                    sum_up(j, par)
                over_pairs(dve, body, head=2)
                o_copy(NB - 2, 0)
                o_copy(NB - 1, 1)

            @block.tensor
            def _(pe):
                pe.wait_ge(W.loaded, W.total)

                def project(j, par):
                    pe.wait_ge(xT_ready, j + 1)
                    need(pe, k_ready, j)
                    for c in range(4):
                        for s in range(SG):
                            at = slice(s * RT, (s + 1) * RT)
                            ins = pe.matmul(p_k[at, c * RT:(c + 1) * RT], W["wk"][:, c * 4 * RD:(c + 1) * 4 * RD], xT[:, par, at], start=True, stop=True)
                    ins.then_inc(k_done, 1)
                    need(pe, q_placed, j)
                    for c in range(4):
                        ins = pe.matmul(p_q[:, c * S:(c + 1) * S], W["wq_rep"][:, c * S:(c + 1) * S], xT[:, par, :], start=True, stop=True)
                    ins.then_inc(q_done, 1)

                def project_v(j, par):
                    need(pe, v_ready, j)
                    for s in range(SG):
                        for i in range(4):
                            of_head = lambda tile: tile.rearrange("p (c i d) -> p i c d", c=4, i=4)[:, i]
                            ins = pe.matmul(of_head(p_v[i * RT:(i + 1) * RT, s * S:(s + 1) * S]), xT[:, par, s * RT:(s + 1) * RT], of_head(W["wv"][:, :]),
                                            start=True, stop=True)
                    ins.then_inc(v_done, 1)

                def score(j, par):
                    pe.wait_ge(q_placed, j + 1)
                    pe.wait_ge(k_placed, j + 1)
                    need(pe, s_ready, j)
                    for c in range(4):
                        ins = pe.matmul(p_s[:, c * S:(c + 1) * S], q_own[:, par, c * S:(c + 1) * S], k_own[:, par, c * S:(c + 1) * S], start=True, stop=True)
                    ins.then_inc(s_done, 1)

                def transpose_probs(j, par):
                    pe.wait_ge(probs_ready, j + 1)
                    need(pe, t_ready, j)
                    for c in range(4):
                        ins = pe.transpose(p_t[:, c * S:(c + 1) * S], probs[:, par, c * S:(c + 1) * S], g.ident[:, :])
                    ins.then_inc(t_done, 1)

                def weigh(j, par):
                    pe.wait_ge(t_ready, j + 1)
                    pe.wait_ge(v_ready, j + 1)
                    need(pe, o_ready, j)
                    for c in range(4):
                        for s in range(SG):
                            at = slice(s * RT, (s + 1) * RT)
                            ins = pe.matmul(p_o[at, c * RT:(c + 1) * RT], probsT[:, c * S + s * RT:c * S + (s + 1) * RT],
                                            v_own[:, par, s * S + c * 4 * RD:s * S + (c + 1) * 4 * RD], start=True, stop=True)
                    ins.then_inc(o_done, 1)

                def transpose_o(j, par):
                    pe.wait_ge(o_ready, j + 1)
                    need(pe, oT_ready, j)
                    pe.transpose(p_oT[:, 0:S], o[:, par, :], g.ident[:, :]).then_inc(oT_done, 1)

                project(0, 0)
                project(1, 1)
                project_v(0, 0)

                def body(j, par, first, last):
                    score(j, par)
                    if not late(j):
                        project(j + 2, par)
                    if not first:
                        transpose_probs(j - 1, 1 - par)
                    if not last:
                        project_v(j + 1, 1 - par)
                    if not early(j):
                        transpose_o(j - 2, par)
                    if not first:
                        weigh(j - 1, 1 - par)
                over_pairs(pe, body, head=2)
                transpose_probs(NB - 1, 1)
                transpose_o(NB - 2, 0)
                weigh(NB - 1, 1)
                transpose_o(NB - 1, 1)


def heads(tile):
    return tile.rearrange("p (h t) -> p h t", t=RT)


def per_head(tile):
    return tile.rearrange("p (h a) -> p h a", a=1).broadcast_to([128, RH, RT])


def stored_before(j, par):
    return (j - par) // 2 * 16 if isinstance(j, int) else j * 8 - 8 * par


def distance_values(g, oT_all, probs_dram):
    nc = g.nc
    W = g.weights["g_"]
    with ExitStack() as ctx:
        sb = lambda n, shape, dt=F32: g.sb("g3_" + n, shape, dt, ctx)
        probs, probsT = sb("probs", [128, 2, BANK]), sb("probsT", [128, 2, BANK])
        values, oT = sb("values", [128, 2, 4 * RD]), sb("oT", [128, 2, S])
        res = sb("res", [128, DM])
        t0, t1, p_o, p_y = g.banks(["g3_" + n for n in ("t0", "t1", "po", "py")], ctx)
        p_t = [t0, t1]
        norm = Norm(g, "g3_ln", 1, ctx)
        sem = lambda n: g.sem("g3_" + n)
        loaded = [sem(f"loaded{k}") for k in (0, 1)]
        values_ready, t_done, t_ready, o_done, oT_ready, y_done, res_ready, sum_ready, out_ready = (
            sem(n) for n in ("values_ready", "t_done", "t_ready", "o_done", "oT_ready", "y_done", "res_ready", "sum_ready", "out_ready"))

        def known(t):
            return not isinstance(t, int) or t >= 0

        def place(dram, t):
            return dram[:, t, :] if isinstance(t, int) else dram[:, bass.ds(t, 1), :].rearrange("s a n -> s (a n)")

        with nc.Block() as block:
            @block.sync
            def _(sp):
                for t in (0, 1):
                    sp.dma_start(probs[:, t, :], place(probs_dram, t)).then_inc(loaded[t], 16)
                with sp.Fori(1, NB // 2) as i:
                    for par in (0, 1):
                        sp.wait_ge(t_done, i * 2 + par - 1)
                        sp.dma_start(probs[:, par, :], place(probs_dram, i * 2 + par)).then_inc(loaded[par], 16)

            @block.gpsimd
            def _(pool):
                def copy_values(t, par):
                    g.wait_apart(pool, o_done, t - 1)
                    pool.tensor_copy(values[:, par, :], cols(W["values"], t, 4 * RD)).then_inc(values_ready, 1)

                def add_bias(t):
                    g.wait_apart(pool, res_ready, t + 1)
                    pool.tensor_tensor(cols(g.x1, t, DM), res[:, :], W["bo"][:, :], ALU.add).then_inc(sum_ready, 1)

                copy_values(0, 0)
                copy_values(1, 1)

                def body(t, par, first, last):
                    if known(t - 2):
                        add_bias(t - 2)
                    if known(t - 3):
                        norm.pool_rstd(pool, t - 3, 0)
                    if not late(t):
                        copy_values(t + 2, par)
                over_pairs(pool, body, head=2)
                add_bias(NB - 2)
                norm.pool_rstd(pool, NB - 3, 0)
                add_bias(NB - 1)
                norm.pool_rstd(pool, NB - 2, 0)
                norm.pool_rstd(pool, NB - 1, 0)

            @block.scalar
            def _(act):
                def body(t, par, first, last):
                    act.wait_ge(t_done, t + 1)
                    need(act, o_done, t - 1)
                    act.activation(probsT[:, par, :], p_t[par][:, :], ACT.Copy).then_inc(t_ready, 1)
                over_pairs(act, body)

            @block.vector
            def _(dve):
                def add_o(t, par):
                    dve.wait_ge(o_done, t + 1)
                    need(dve, y_done, t - 1)
                    dve.tensor_tensor(oT[:, par, :], p_o[:, 0:S], cols(oT_all, t, S), ALU.add).then_inc(oT_ready, 1)

                def add_x(t):
                    dve.wait_ge(y_done, t + 1)
                    need(dve, sum_ready, t)
                    dve.tensor_tensor(res[:, :], p_y[:, 0:DM], cols(g.x1, t, DM), ALU.add).then_inc(res_ready, 1)

                def moments(t):
                    g.wait_apart(dve, sum_ready, t + 1)
                    norm.dve_moments(dve, t, 0, cols(g.x1, t, DM))

                def scale(t):
                    norm.dve_scale(dve, t, 0, cols(g.x1, t, DM), cols(g.x1, t, DM)).then_inc(out_ready, 1)

                def body(t, par, first, last):
                    if not first:
                        add_o(t - 1, 1 - par)
                    if known(t - 2):
                        add_x(t - 2)
                    if known(t - 4):
                        scale(t - 4)
                    if known(t - 3):
                        moments(t - 3)
                over_pairs(dve, body, head=2)
                add_o(NB - 1, 1)
                for t in range(NB, NB + 4):
                    if t - 2 < NB:
                        add_x(t - 2)
                    scale(t - 4)
                    if t - 3 < NB:
                        moments(t - 3)
                dve.wait_ge(out_ready, NB)

            @block.tensor
            def _(pe):
                def transpose(t, par, k):
                    pe.wait_ge(loaded[par], k + 16)
                    need(pe, t_ready, t - 1)
                    for c in range(4):
                        ins = pe.transpose(p_t[par][:, c * S:(c + 1) * S], probs[:, par, c * S:(c + 1) * S], g.ident[:, :])
                    ins.then_inc(t_done, 1)

                def weigh(t, par):
                    pe.wait_ge(t_ready, t + 1)
                    pe.wait_ge(values_ready, t + 1)
                    need(pe, oT_ready, t)
                    for c in range(4):
                        ins = pe.matmul(p_o[32 * c:32 * c + 32, 0:S], values[:, par, :], probsT[:, par, c * S:(c + 1) * S], start=True, stop=True)
                    ins.then_inc(o_done, 1)

                def project(t, par):
                    pe.wait_ge(oT_ready, t + 1)
                    need(pe, res_ready, t)
                    pe.matmul(p_y[:, 0:DM], oT[:, par, :], W["wo"][:, :], start=True, stop=True).then_inc(y_done, 1)

                def body(t, par, first, last):
                    transpose(t, par, stored_before(t, par))
                    if not first:
                        weigh(t - 1, 1 - par)
                    if not early(t):
                        project(t - 2, par)
                over_pairs(pe, body, head=2)
                weigh(NB - 1, 1)
                project(NB - 2, 0)
                project(NB - 1, 1)


def cross_self(g):
    attention16(g, Heads16("b_", 32 ** -0.5, DM, own_keys=True, affine=True, bias=False, later_mask=True))


def cross_context(g):
    attention16(g, Heads16("d_", 32 ** -0.5, DC, own_keys=False, affine=True, bias=False, later_mask=False))


def context_attention(g):
    attention16(g, Heads16("h_", 8 ** -0.5, DC, own_keys=False, affine=False, bias=True, later_mask=False))


def program(nc, t, out):
    with ExitStack() as ctx:
        g = Globals(nc, t, ctx)
        declare_weights(g)
        setup(g)
        g.run_phase(self_attention)
        with ExitStack() as experts_ctx:
            declare_experts(g, experts_ctx)
            g.next_weights = [g.weights["f_"]]
            for phase in (cross_self, cross_mlp1, cross_context, cross_mlp2):
                g.run_phase(phase)
            declare_layer1_weights(g)
            g.next_weights = [g.weights[name] for name in ("g_", "h_", "i_")]
            g.run_phase(experts)
        for phase in (relative_attention, context_attention, quantum_mlp):
            g.run_phase(phase)
        stored = g.sem("out_stored")
        with nc.Block() as block:
            @block.sync
            def _(sp):
                sp.dma_start(out.rearrange("b s n -> s b n"), g.x1[:, :].rearrange("s (b n) -> s b n", b=NB)).then_inc(stored, 16)
                sp.wait_ge(stored, 16)


PAIRED_HEADS = [(2 * (pair // 2) + r) * 8 + pair % 2 * 4 + j for pair in range(8) for j in range(4) for r in (0, 1)]


def lay_out(a):
    import numpy as np
    c = np.ascontiguousarray
    t = {}
    for name in ("x", "ctx_512"):
        t[name] = c(a[name])
    t["L0_attn_WkT"] = c(a["L0_attn_Wk"].T)
    t["L0_attn_bkT"] = c(a["L0_attn_bk"].reshape(4, 128).T)
    t["L0_attn_WqT"] = c(a["L0_attn_Wq"].reshape(64, 64, 128)[PAIRED_HEADS].reshape(4096, 128).T)
    t["L0_attn_bqT"] = c(a["L0_attn_bq"].reshape(64, 64)[PAIRED_HEADS].reshape(32, 128).T)
    t["L0_attn_WoT"] = c(a["L0_attn_Wo"].T.reshape(64, 64, 128)[PAIRED_HEADS].reshape(4096, 128))
    t["L0_attn_WvT"] = c(a["L0_attn_Wv"].T)
    for name in ("L0_attn_bv", "L0_attn_bo", "L0_attn_sinks", "L0_xattn_ln1_g", "L0_xattn_ln1_b"):
        t[name] = c(a[name])
    for a1 in ("L0_xattn_a1_", "L0_xattn_a2_"):
        for name in ("wq", "wk", "wv"):
            w = a[a1 + name]
            t[a1 + name] = c(w.transpose(1, 0, 2).reshape(w.shape[1], -1))
        for name in ("li1_w", "li1_b", "lnx_g", "lnx_b", "lny_g", "lny_b", "ln3_g", "ln3_b", "li2_w", "li3_w", "li3_b"):
            t[a1 + name] = c(a[a1 + name])
        t[a1 + "li2_bT"] = c(a[a1 + "li2_b"].reshape(4, 128).T)
    for name in ("b1", "quantum_phases", "quantum_weights_real", "quantum_weights_imag"):
        t[f"L1_ffn_{name}T"] = c(a[f"L1_ffn_{name}"].reshape(4, 128).T)
    for name in ("L1_ffn_W1", "L1_ffn_W2", "L1_ffn_b2", "L0_xattn_ln2_g", "L0_xattn_ln2_b"):
        t[name] = c(a[name])

    t["L0_ffn_gate_wT"] = c(a["L0_ffn_gate_w"].T)
    for name in ("w1", "w3"):
        t[f"L0_ffn_{name}T"] = c(a[f"L0_ffn_{name}"].reshape(-1, 128).T)
    t["L0_ffn_w2T"] = c(a["L0_ffn_w2"].transpose(0, 2, 1).reshape(-1, 128))

    def slots(w):
        out = np.zeros(w.shape[:-1] + (16, 32), w.dtype)
        out[..., :8] = w.reshape(w.shape[:-1] + (16, 8))
        return out.reshape(w.shape[:-1] + (512,))
    d = "L1_attn_"
    wq, wk, wv = (a[d + "in_proj_weight"][n * 128:(n + 1) * 128].T for n in range(3))
    bq, bk, bv = (a[d + "in_proj_bias"][n * 128:(n + 1) * 128] for n in range(3))

    t[d + "wq"], t[d + "wk"], t[d + "wv"], t[d + "wo"] = c(wq), c(wk), c(wv), c(a[d + "out_w"].T)
    t[d + "bq"], t[d + "bv"] = c(bq.reshape(128, 1)), c(bv.reshape(128, 1))
    t[d + "wq_rep"] = c(np.concatenate([wq.reshape(128, 4, 1, 32)] * 4, axis=2).reshape(128, 512))
    for name, bias in (("bq_rep", bq), ("bk_rep", bk)):
        t[d + name] = c(np.concatenate([bias.reshape(4, 32).T] * 4, axis=0))
    t[d + "out_b"] = c(a[d + "out_b"])
    near = lambda dist: [min(max(n, -16), 16) + 16 for n in dist]
    keys = np.zeros((16, 8, 16, 63), np.float32)
    for h in range(16):
        keys[h, :, h, :] = a[d + "rel_k_table"][near(range(-31, 32))].T
    t[d + "keys"] = keys.reshape(128, 16 * 63)
    values = np.zeros((4, 32, 32, 4, 8), np.float32)
    for i in range(4):
        for place in range(32):
            values[i, :, place, i, :] = a[d + "rel_v_table"][near(range(-place, 32 - place))]
    t[d + "values"] = values.reshape(128, 32 * 32)
    row = np.arange(128)
    t[d + "row_head"] = (row[:, None] // 8 % 4 == np.arange(4)).astype(np.float32)
    t[d + "own_scaled"] = (row[:, None] // 32 == row[None, :] // 32) * np.float32(8 ** -0.5)
    for name in ("Wq", "Wk"):
        t[f"L1_xattn_{name}P"] = c(slots(a[f"L1_xattn_{name}"]))
    for name in ("bq", "bk"):
        t[f"L1_xattn_{name}P"] = c(slots(a[f"L1_xattn_{name}"]).reshape(4, 128).T)
    for name in ("Wv", "bv"):
        t[f"L1_xattn_{name}P"] = c(slots(a[f"L1_xattn_{name}"]))
    t["L1_xattn_WoP"] = c(slots(a["L1_xattn_Wo"].T).T)
    t["L1_xattn_bo"] = c(a["L1_xattn_bo"])
    return t


def kernel(**inputs):
    import numpy as np
    import concourse.bacc as bacc
    from concourse.bass_utils import run_bass_kernel_spmd

    nc = bacc.Bacc("TRN2", target_bir_lowering=False, num_devices=1)
    arrays = lay_out({name: np.asarray(a) for name, a in inputs.items()})
    t = {name: nc.dram_tensor(name, a.shape, mybir.dt.from_np(a.dtype), kind="ExternalInput").ap() for name, a in arrays.items()}
    out = nc.dram_tensor("out", (NB, S, DM), F32, kind="ExternalOutput").ap()
    program(nc, t, out)
    return run_bass_kernel_spmd(nc, [arrays], core_ids=[0]).results[0]["out"]
```
